# Optimizing a Trainium2 kernel written in Bass

```python
import numpy as np
import jax
import jax.numpy as jnp

def _softmax(x, axis=-1):
    return jax.nn.softmax(x, axis=axis)

def _gelu(x):
    return jax.nn.gelu(x, approximate=True)

def _silu(x):
    return jax.nn.silu(x)

def _sigmoid(x):
    return jax.nn.sigmoid(x)

def _layernorm(x, axis=-1, eps=1e-05):
    m = jnp.mean(x, axis=axis, keepdims=True)
    v = jnp.var(x, axis=axis, keepdims=True)
    return (x - m) / jnp.sqrt(v + eps)

def _scatter_add(tgt, idx, src, axis=0):
    return tgt.at[idx].add(src)

def _segment_sum(src, seg, n):
    return jax.ops.segment_sum(src, seg, n)
kernel_name = 'mk_flamingo_gated_d2_seqx_r8_e56025'

def setup_inputs(seed: int=0):
    np.random.seed(seed)
    _w = jnp.asarray

    def _rec_inputs():
        import jax
        import jax.numpy as jnp
        _rk = jax.random.key(seed)
        x = -0.000125 + 0.9999 * jax.random.normal(jax.random.fold_in(_rk, 1), (64, 64, 128), jnp.float32)
        _lenS = 64 - jax.random.randint(jax.random.fold_in(_rk, 7), (64,), 0, max(1, 64 // 4) + 1, jnp.int32)
        _lenS2 = 64 - jax.random.randint(jax.random.fold_in(_rk, 8), (64,), 0, max(1, 64 // 4) + 1, jnp.int32)
        _ctx_1024P = jax.random.normal(jax.random.fold_in(_rk, 11), (64, 16, 128), jnp.float32)
        _ctx_1024c = jax.random.dirichlet(jax.random.fold_in(_rk, 511), 0.3 * jnp.ones((16,), jnp.float32), (64, 64))
        _ctx_1024t = jnp.einsum('bsk,bkd->bsd', _ctx_1024c, _ctx_1024P)
        _ctx_1024t = _ctx_1024t * jax.lax.rsqrt(jnp.mean(jnp.square(_ctx_1024t)) + 1e-12) * 0.953939
        ctx_1024 = -1.52775e-05 + 0.999936 * (_ctx_1024t + 0.3 * jax.random.normal(jax.random.fold_in(_rk, 611), (64, 64, 128), jnp.float32))
        _validS = jnp.arange(64)[None, :] < _lenS[:, None]
        _validS2 = jnp.arange(64)[None, :] < _lenS2[:, None]
        _causal = jnp.tril(jnp.ones((64, 64), dtype=bool))
        mask_Bx1x1xS2_bf1 = jnp.ones((64, 1, 1, 64), dtype=bool)
        _g = jax.random.normal(jax.random.fold_in(_rk, 9001), (2, 2), jnp.float32)
        _g = jnp.sign(_g) * jnp.maximum(jnp.abs(_g), 1.0) + (_g == 0) * 1.0
        g_xattn = _g[0]
        g_ffn = _g[1]
        return (x, ctx_1024, mask_Bx1x1xS2_bf1, g_xattn, g_ffn)
    x, ctx_1024, mask_Bx1x1xS2_bf1, g_xattn, g_ffn = _rec_inputs()

    def _L0_xattn_setup():
        import jax, jax.numpy as jnp
        import numpy as np
        C = 128
        H = 16
        DH = C // H

        def _sep(x):
            N, L, _ = x.shape
            return x.reshape(N, L, H, DH).transpose(0, 2, 1, 3)

        def _grp(x):
            N, _, L, _ = x.shape
            return x.transpose(0, 2, 1, 3).reshape(N, L, C)
        key = jax.random.key(seed)
        ks = jax.random.split(key, 16)
        s = 1.0 / np.sqrt(C)
        inp = {'x_q': jax.random.normal(ks[0], (8, 512, C), dtype=jnp.float32), 'x_kv': jax.random.normal(ks[1], (8, 512, C), dtype=jnp.float32), 'Wq': jax.random.normal(ks[2], (C, C), dtype=jnp.float32) * s, 'bq': jnp.zeros((C,), jnp.float32), 'Wqa': jax.random.normal(ks[3], (C, H), dtype=jnp.float32) * s, 'bqa': jnp.zeros((H,), jnp.float32), 'Wk': jax.random.normal(ks[4], (C, C), dtype=jnp.float32) * s, 'bk': jnp.zeros((C,), jnp.float32), 'Wka': jax.random.normal(ks[5], (C, H), dtype=jnp.float32) * s, 'bka': jnp.zeros((H,), jnp.float32), 'Wv': jax.random.normal(ks[6], (C, C), dtype=jnp.float32) * s, 'bv': jnp.zeros((C,), jnp.float32), 'Wt': jax.random.normal(ks[7], (C, C), dtype=jnp.float32) * s, 'bt': jnp.zeros((C,), jnp.float32), 'Wp': jax.random.normal(ks[8], (C, C), dtype=jnp.float32) * s, 'bp': jnp.zeros((C,), jnp.float32)}
        return inp
    _L0_xattn_all = _L0_xattn_setup()
    _L0_xattn_in = {k: v for k, v in _L0_xattn_all.items() if k in ('Wq', 'bq', 'Wqa', 'bqa', 'Wk', 'bk', 'Wka', 'bka', 'Wv', 'bv', 'Wt', 'bt', 'Wp', 'bp')}
    del _L0_xattn_all

    def _L0_ffn_setup():
        import jax, jax.numpy as jnp
        import numpy as np
        N_EMBD = 128
        NUM_EXPERTS = 8
        TOP_K = 2
        D_FF = 4 * N_EMBD
        B, S = (4, 256)
        key = jax.random.key(seed)
        ks = jax.random.split(key, 7)
        scale = lambda fan_in: 1.0 / np.sqrt(fan_in)
        x = jax.random.normal(ks[0], (B, S, N_EMBD), dtype=jnp.float32)
        W_router = jax.random.normal(ks[1], (N_EMBD, NUM_EXPERTS), dtype=jnp.float32) * scale(N_EMBD)
        b_router = jnp.zeros((NUM_EXPERTS,), dtype=jnp.float32)
        W1 = jax.random.normal(ks[2], (NUM_EXPERTS, N_EMBD, D_FF), dtype=jnp.float32) * scale(N_EMBD)
        b1 = jnp.zeros((NUM_EXPERTS, D_FF), dtype=jnp.float32)
        W2 = jax.random.normal(ks[3], (NUM_EXPERTS, D_FF, N_EMBD), dtype=jnp.float32) * scale(D_FF)
        b2 = jnpp = jnp.zeros((NUM_EXPERTS, N_EMBD), dtype=jnp.float32)
        return {'x': x, 'W_router': W_router, 'b_router': b_router, 'W1': W1, 'b1': b1, 'W2': W2, 'b2': b2}
    _L0_ffn_all = _L0_ffn_setup()
    _L0_ffn_in = {k: v for k, v in _L0_ffn_all.items() if k in ('W_router', 'b_router', 'W1', 'b1', 'W2', 'b2')}
    del _L0_ffn_all

    def _L1_xattn_setup():
        import jax, jax.numpy as jnp
        import numpy as np
        D_MODEL = 128
        N_HEADS = 16
        D_HEAD = D_MODEL // N_HEADS

        def _split_heads(x):
            B, L, D = x.shape
            return x.reshape(B, L, N_HEADS, D_HEAD).transpose(0, 2, 1, 3)
        key = jax.random.key(seed)
        ks = jax.random.split(key, 6)
        B, LQ, LK = (4, 64, 512)
        scale = 1.0 / np.sqrt(D_MODEL)
        return {'q_in': jax.random.normal(ks[0], (B, LQ, D_MODEL), dtype=jnp.float32), 'mem': jax.random.normal(ks[1], (B, LK, D_MODEL), dtype=jnp.float32), 'mem_mask': jnp.ones((B, 1, 1, LK), dtype=bool), 'Wq': jax.random.normal(ks[2], (D_MODEL, D_MODEL), dtype=jnp.float32) * scale, 'Wk': jax.random.normal(ks[3], (D_MODEL, D_MODEL), dtype=jnp.float32) * scale, 'Wv': jax.random.normal(ks[4], (D_MODEL, D_MODEL), dtype=jnp.float32) * scale, 'Wo': jax.random.normal(ks[5], (D_MODEL, D_MODEL), dtype=jnp.float32) * scale}
    _L1_xattn_all = _L1_xattn_setup()
    _L1_xattn_in = {k: v for k, v in _L1_xattn_all.items() if k in ('Wq', 'Wk', 'Wv', 'Wo')}
    del _L1_xattn_all

    def _L1_ffn_setup():
        import jax, jax.numpy as jnp
        import numpy as np
        B, T, D, FF, E, TOP_K = (4, 256, 128, 512, 8, 2)
        key = jax.random.key(seed)
        k0, k1, k2, k3 = jax.random.split(key, 4)
        x = jax.random.normal(k0, (B, T, D), dtype=jnp.float32)
        router_w = jax.random.normal(k1, (E, D), dtype=jnp.float32) * D ** (-0.5)
        w1 = jax.random.normal(k2, (E, D, FF), dtype=jnp.float32) * D ** (-0.5)
        w2 = jax.random.normal(k3, (E, FF, D), dtype=jnp.float32) * FF ** (-0.5)
        return {'x': x, 'router_w': router_w, 'w1': w1, 'w2': w2}
    _L1_ffn_all = _L1_ffn_setup()
    _L1_ffn_in = {k: v for k, v in _L1_ffn_all.items() if k in ('router_w', 'w1', 'w2')}
    del _L1_ffn_all
    return {'x': x, 'ctx_1024': ctx_1024, 'mask_Bx1x1xS2_bf1': mask_Bx1x1xS2_bf1, 'g_xattn': g_xattn, 'g_ffn': g_ffn, 'L0_xattn_Wq': _L0_xattn_in['Wq'], 'L0_xattn_bq': _L0_xattn_in['bq'], 'L0_xattn_Wqa': _L0_xattn_in['Wqa'], 'L0_xattn_bqa': _L0_xattn_in['bqa'], 'L0_xattn_Wk': _L0_xattn_in['Wk'], 'L0_xattn_bk': _L0_xattn_in['bk'], 'L0_xattn_Wka': _L0_xattn_in['Wka'], 'L0_xattn_bka': _L0_xattn_in['bka'], 'L0_xattn_Wv': _L0_xattn_in['Wv'], 'L0_xattn_bv': _L0_xattn_in['bv'], 'L0_xattn_Wt': _L0_xattn_in['Wt'], 'L0_xattn_bt': _L0_xattn_in['bt'], 'L0_xattn_Wp': _L0_xattn_in['Wp'], 'L0_xattn_bp': _L0_xattn_in['bp'], 'L0_ffn_W_router': _L0_ffn_in['W_router'], 'L0_ffn_b_router': _L0_ffn_in['b_router'], 'L0_ffn_W1': _L0_ffn_in['W1'], 'L0_ffn_b1': _L0_ffn_in['b1'], 'L0_ffn_W2': _L0_ffn_in['W2'], 'L0_ffn_b2': _L0_ffn_in['b2'], 'L1_xattn_Wq': _L1_xattn_in['Wq'], 'L1_xattn_Wk': _L1_xattn_in['Wk'], 'L1_xattn_Wv': _L1_xattn_in['Wv'], 'L1_xattn_Wo': _L1_xattn_in['Wo'], 'L1_ffn_router_w': _L1_ffn_in['router_w'], 'L1_ffn_w1': _L1_ffn_in['w1'], 'L1_ffn_w2': _L1_ffn_in['w2']}

def reference(x, ctx_1024, mask_Bx1x1xS2_bf1, g_xattn, g_ffn, L0_xattn_Wq, L0_xattn_bq, L0_xattn_Wqa, L0_xattn_bqa, L0_xattn_Wk, L0_xattn_bk, L0_xattn_Wka, L0_xattn_bka, L0_xattn_Wv, L0_xattn_bv, L0_xattn_Wt, L0_xattn_bt, L0_xattn_Wp, L0_xattn_bp, L0_ffn_W_router, L0_ffn_b_router, L0_ffn_W1, L0_ffn_b1, L0_ffn_W2, L0_ffn_b2, L1_xattn_Wq, L1_xattn_Wk, L1_xattn_Wv, L1_xattn_Wo, L1_ffn_router_w, L1_ffn_w1, L1_ffn_w2):
    import jax
    import jax.numpy as jnp

    def _L0_xattn_ref(x_q, x_kv, Wq, bq, Wqa, bqa, Wk, bk, Wka, bka, Wv, bv, Wt, bt, Wp, bp):
        import jax, jax.numpy as jnp
        import numpy as np
        C = 128
        H = 16
        DH = C // H

        def _sep(x):
            N, L, _ = x.shape
            return x.reshape(N, L, H, DH).transpose(0, 2, 1, 3)

        def _grp(x):
            N, _, L, _ = x.shape
            return x.transpose(0, 2, 1, 3).reshape(N, L, C)
        scale = 1.0 / np.sqrt(DH)
        queries = x_q @ Wq + bq
        q_w = jax.nn.softmax((queries @ Wqa + bqa) * scale, axis=-2).transpose(0, 2, 1)
        q_heads = _sep(queries)
        pooled_q = jnp.einsum('nhl,nhld->nhd', q_w, q_heads)
        pooled_q_grp = pooled_q.reshape(x_q.shape[0], 1, C)
        keys = x_kv @ Wk + bk
        keys_queries = keys * pooled_q_grp
        k_w = jax.nn.softmax((keys_queries @ Wka + bka) * scale, axis=-2).transpose(0, 2, 1)
        k_heads = _sep(keys)
        pooled_k = jnp.einsum('nhl,nhld->nhd', k_w, k_heads)
        values = _sep(x_kv @ Wv + bv)
        keys_values = values * pooled_k[:, :, None, :]
        keys_values = _grp(keys_values) @ Wt + bt
        out = _sep(keys_values) + q_heads
        out = _grp(out) @ Wp + bp
        return out

    def _L0_ffn_ref(x, W_router, b_router, W1, b1, W2, b2):
        import jax, jax.numpy as jnp
        import numpy as np
        N_EMBD = 128
        NUM_EXPERTS = 8
        TOP_K = 2
        D_FF = 4 * N_EMBD
        B, S = (4, 256)
        Bv, Sv, D = x.shape
        flat_x = x.reshape(-1, D)
        T = flat_x.shape[0]
        logits = flat_x @ W_router + b_router
        top_vals, top_idx = jax.lax.top_k(logits, TOP_K)
        neg_inf = jnp.full_like(logits, -jnp.inf)
        sparse_logits = neg_inf.at[jnp.arange(T)[:, None], top_idx].set(top_vals)
        router_weights = jax.nn.softmax(sparse_logits, axis=-1)
        final_output = jnp.zeros_like(flat_x)
        for e in range(NUM_EXPERTS):
            expert_mask = jnp.any(top_idx == e, axis=-1)
            h = jax.nn.relu(flat_x @ W1[e] + b1[e])
            y = h @ W2[e] + b2[e]
            w = router_weights[:, e] * expert_mask.astype(x.dtype)
            final_output = final_output + y * w[:, None]
        return final_output.reshape(Bv, Sv, D)

    def _L1_xattn_ref(q_in, mem, mem_mask, Wq, Wk, Wv, Wo):
        import jax, jax.numpy as jnp
        import numpy as np
        D_MODEL = 128
        N_HEADS = 16
        D_HEAD = D_MODEL // N_HEADS

        def _split_heads(x):
            B, L, D = x.shape
            return x.reshape(B, L, N_HEADS, D_HEAD).transpose(0, 2, 1, 3)
        q = _split_heads(q_in @ Wq.T)
        k = _split_heads(mem @ Wk.T)
        v = _split_heads(mem @ Wv.T)
        scores = jnp.einsum('bhqd,bhkd->bhqk', q, k) / jnp.sqrt(jnp.float32(D_HEAD))
        scores = jnp.where(mem_mask, scores, -jnp.inf)
        attn = jax.nn.softmax(scores, axis=-1)
        out = jnp.einsum('bhqk,bhkd->bhqd', attn, v)
        B, H, LQ, Dh = out.shape
        out = out.transpose(0, 2, 1, 3).reshape(B, LQ, H * Dh)
        return out @ Wo.T

    def _L1_ffn_ref(x, router_w, w1, w2):
        import jax, jax.numpy as jnp
        import numpy as np
        B, T, D, FF, E, TOP_K = (4, 256, 128, 512, 8, 2)
        b, t, d = x.shape
        e, k = (router_w.shape[0], TOP_K)
        xf = x.reshape(-1, d)
        n = xf.shape[0]
        logits = xf @ router_w.T
        topv, topi = jax.lax.top_k(logits, k)
        topw = jax.nn.softmax(topv.astype(jnp.float32), axis=-1).astype(x.dtype)
        idx_flat = topi.reshape(-1)
        w_flat = topw.reshape(-1)
        sort_idx = jnp.argsort(idx_flat)
        src = jnp.repeat(jnp.arange(n), k)
        rev = src[sort_idx]
        sw = w_flat[sort_idx]
        perm = xf[rev]
        chunks = perm.reshape(e, n * k // e, d)
        h = jax.nn.gelu(jnp.einsum('ecd,edf->ecf', chunks, w1), approximate=False)
        y = jnp.einsum('ecf,efd->ecd', h, w2).reshape(n * k, d)
        y = y * sw[:, None]
        out = jnp.zeros((n, d), dtype=x.dtype).at[rev].add(y)
        return out.reshape(b, t, d)
    x = x + jnp.tanh(g_xattn[0]) * _L0_xattn_ref(_layernorm(x, axis=-1), ctx_1024, L0_xattn_Wq, L0_xattn_bq, L0_xattn_Wqa, L0_xattn_bqa, L0_xattn_Wk, L0_xattn_bk, L0_xattn_Wka, L0_xattn_bka, L0_xattn_Wv, L0_xattn_bv, L0_xattn_Wt, L0_xattn_bt, L0_xattn_Wp, L0_xattn_bp)
    x = x + jnp.tanh(g_ffn[0]) * _L0_ffn_ref(_layernorm(x, axis=-1), L0_ffn_W_router, L0_ffn_b_router, L0_ffn_W1, L0_ffn_b1, L0_ffn_W2, L0_ffn_b2)
    x = x + jnp.tanh(g_xattn[1]) * _L1_xattn_ref(_layernorm(x, axis=-1), ctx_1024, mask_Bx1x1xS2_bf1, L1_xattn_Wq, L1_xattn_Wk, L1_xattn_Wv, L1_xattn_Wo)
    x = x + jnp.tanh(g_ffn[1]) * _L1_ffn_ref(_layernorm(x, axis=-1), L1_ffn_router_w, L1_ffn_w1, L1_ffn_w2)
    return x

_drawn_inputs = setup_inputs


def setup_inputs(seed=0):
    import zlib

    import numpy as np

    out = dict(_drawn_inputs(seed))
    spreads = {'g_ffn': (-1.0, 0.6),
     'L0_xattn_bq': (0.0, 0.1),
     'L0_xattn_bqa': (0.0, 0.8),
     'L0_xattn_bk': (0.0, 0.1),
     'L0_xattn_bka': (0.0, 0.8),
     'L0_xattn_bv': (0.0, 0.1),
     'L0_xattn_bt': (0.0, 0.1),
     'L0_xattn_bp': (0.0, 0.1),
     'L0_ffn_b_router': (0.0, 0.1),
     'L0_ffn_b1': (0.0, 0.1),
     'L0_ffn_b2': (0.0, 0.1)}
    factors = {'L0_xattn_Wqa': 3.454}
    for name, (base, spread) in spreads.items():
        noise = np.random.default_rng([zlib.crc32(name.encode()), seed]).standard_normal(out[name].shape)
        drawn = base * np.exp(spread * noise) if base else spread * noise
        out[name] = jnp.asarray(drawn.astype(out[name].dtype))
    for name, factor in factors.items():
        out[name] = (out[name] * factor).astype(out[name].dtype)
    return out
```

```python
from contextlib import ExitStack

import concourse.bass as bass
from concourse import mybir

ALU = mybir.AluOpType
ACT = mybir.ActivationFunctionType
F32 = mybir.dt.float32
F16 = mybir.dt.float16
U32 = mybir.dt.uint32
I32 = mybir.dt.int32
U8 = mybir.dt.uint8
AX = mybir.AxisListType.X
ds = bass.ds

P = 128
D = 128
SEQ = 64
NB = 64
NTOK = NB * SEQ
NT = NTOK // P
CT_TILES = 4
CHUNK = CT_TILES * P
NC = NTOK // CHUNK
CB = CHUNK // SEQ
H, DH = 16, 8
HP = H // 2
HG = 4
E, FF, TOPK = 8, 512, 2
FC = FF // P
SLOTS = NTOK * TOPK
TILE = 256
CAP = NTOK + TILE
ROW16 = 2 * D + 2
TILES = (SLOTS // TILE + E, SLOTS // TILE)
FIX0 = E * CAP
XS_ROWS = E * CAP + E * TILE
DUMMY = SLOTS
Y_ROWS = SLOTS + 2 * E * TILE
WSCALE = 256.0
EPS = 1e-5
BIG = 3.0e38
QK_SCALE = (float(DH) ** -0.5, 1.0)
MASKED = -60000.0
STORED = 32
XS_LEAD = 8


def bc(ap, axis, n):
    shape = list(ap.shape)
    shape.insert(axis, n)
    return ap.unsqueeze(axis).broadcast_to(shape)


def build(nc, A, out):
    ctx = ExitStack()
    with ctx:
        def sb(name, shape, dt=F32):
            return ctx.enter_context(nc.sbuf_tensor(name, shape, dt))

        def sem(name):
            return ctx.enter_context(nc.semaphore(name))

        xs = [nc.dram_tensor(f"xs{l}", [XS_ROWS, ROW16], F16).ap() for l in range(2)]
        ys = [nc.dram_tensor(f"ys{l}", [Y_ROWS, D], F32).ap() for l in range(2)]
        qk_dram = [nc.dram_tensor(n, [2, D, NTOK], F16).ap() for n in ("q_parts", "k_parts")]
        mask_dram = nc.dram_tensor("mask_row", [NT, P], F16).ap()

        X = sb("X", [P, NT, D])
        XN = sb("XN", [P, NT, D])
        W = sb("W", [P, 11, D])
        wq, wqT, wk, wkT, wv, wtT, wp, wq1T, wk1T, wv1T, wo1T = (W[:, i, :] for i in range(11))
        wa = sb("wa", [P, 2, H])
        wr = sb("wr", [P, 2, E])
        bcol = sb("bcol", [P, 4])
        bacol = sb("bacol", [P, 2])
        bprow = sb("bprow", [1, D])
        brb = sb("brb", [P, E])
        b1 = sb("b1", [P, E * FC])
        g4 = sb("g4", [P, 4])
        gt = sb("gt", [P, 4])
        ident = sb("ident", [P, P])
        ident16 = sb("ident16", [P, P], F16)
        tri16 = sb("tri16", [P, P], F16)
        ones16 = sb("ones16", [P, P], F16)
        onesrow = sb("onesrow", [1, P])
        hmask = sb("hmask", [P, H])
        expert_i = sb("expert_i", [P, E], I32)
        expert_row = sb("expert_row", [P, E])
        rev_i = sb("rev_i", [P, E], I32)
        rev = sb("rev", [P, E])
        id_tok = sb("id_tok", [P, NT, TOPK], U32)
        id_pad = sb("id_pad", [P, 2 * E, 2], U32)
        pos_i = sb("pos_i", [P, 80], I32)
        pos128 = sb("pos128", [P, 80])
        lane_i = sb("lane_i", [P, 1], I32)
        lane = sb("lane", [P, 1])
        eidx_i = sb("eidx_i", [P, 2, TILES[0]], I32)
        stats = sb("stats", [P, NT, 6])
        mv = sb("mv", [P, NT, 2])
        rstd = sb("rstd", [P, NT])
        nwt = sb("nwt", [P, 2, CT_TILES])
        lg = sb("lg", [P, NT, E])
        rtmp = sb("rtmp", [P, 2, CT_TILES, E])
        rmax = sb("rmax", [P, 4, NT])
        oh = [sb(f"oh{k}", [P, NT, E]) for k in range(TOPK)]
        sel16 = sb("sel16", [P, NT, E], F16)
        cum16 = sb("cum16", [P, E], F16)
        csum = sb("csum", [P, E])
        wdif = sb("wdif", [P, NT])
        wexp = sb("wexp", [P, NT])
        wden = sb("wden", [P, NT])
        wgt = sb("wgt", [P, NT, TOPK])
        adr = sb("adr", [P, NT, TOPK])
        adr_i = sb("adr_i", [P, NT, TOPK], U32)
        pack = sb("pack", [P, 2, CT_TILES, TOPK, ROW16], F16)
        turn = sb("turn", [1, XS_LEAD])
        zrow = sb("zrow", [P, ROW16], F16)
        rxt = sb("rxt", [P, CHUNK])
        cnt = sb("cnt", [P, E])
        cnt_i = sb("cnt_i", [P, E], I32)
        cnt_s = sb("cnt_s", [P, E])
        incl = sb("incl", [P, E])
        jump = sb("jump", [P, E])
        onesE = sb("onesE", [P, E])
        big1 = sb("big1", [P, 80, E])
        row_f = sb("row_f", [P, 80])
        er_f = sb("er_f", [P, 80])
        fx_f = sb("fx_f", [P, 3, 80])
        rows_i = sb("rows_i", [P, 80], I32)
        tail_f = sb("tail_f", [P, E])
        tail_i = sb("tail_i", [P, E], I32)
        fixp = sb("fixp", [P, 4, E])
        fixp_i = sb("fixp_i", [P, E], I32)
        fixadr_i = sb("fixadr_i", [P, E], U32)

        mask_u8 = sb("mask_u8", [NT, P], U8)
        mask_f = sb("mask_f", [NT, P])
        mask16 = sb("mask16", [NT, P], F16)
        mask_bias = sb("mask_bias", [P, NT])

        w1h = sb("w1h", [P, E * FF], F16)
        w1l = sb("w1l", [P, E * FF], F16)
        w2 = sb("w2", [P, E * FF])

        WORK = int(109.5 * 1024)
        work = sb("work", [P, WORK // 4])

        def at(kb, shape, dt=F32):
            size = {F32: 4, U32: 4, F16: 2}[dt]
            n = 1
            for s in shape:
                n *= s
            a = int(kb * 256)
            assert a + n * size // 4 <= WORK // 4, (kb, shape)
            v = work[:, a:a + n * size // 4]
            if dt is not F32:
                v = v.bitcast(dt)
            names = "abcdef"[:len(shape)]
            if len(shape) > 1:
                v = v.rearrange(f"p ({' '.join(names)}) -> p {' '.join(names)}",
                                **{k: s for k, s in zip(names[1:], shape[1:])})
            return v

        ctT = at(52, [NTOK])
        xnT = at(36, [NTOK])
        ctx_tok = at(0, [NT, D])
        sl = at(16, [1024])
        se = at(20, [1024])
        w2blk = at(24, [NT, 2, H])
        xp = at(28, [1024])
        prod = at(32, [1024])
        g32 = at(68, [NB, 32])
        gp = at(76, [NB, H])
        wa32 = at(80, [2, 4, 32])
        wka_bk = at(81, [32])
        wqqa = at(81.25, [32])
        wtp = at(82, [D])
        wqp = at(82.5, [D])
        crow = at(83, [D])
        btq = at(83.5, [2])
        qb = at(83.75, [2])
        kb16 = at(84, [H])
        pq = at(84.25, [NB])
        pkv = at(84.5, [NB])
        smx = at(84.75, [H])
        ssum = at(84.85, [16])
        srec = at(84.95, [16])
        uT = at(85.5, [2, CHUNK])
        w1raw = at(90, [2, FF])
        padt = at(94, [E, 2, ROW16], F16)
        b2b = at(104, [E * D])
        xin = at(0, [XS_LEAD, 2, ROW16], F16)
        xgT = at(8.25, [2, 2, TILE], F16)
        hid = at(10.25, [2, FC, TILE])
        yrow = at(18.5, [XS_LEAD, 2, D])
        yc = at(26.5, [2, CT_TILES, TOPK, D])
        fixs = at(104, [7, ROW16], F16)
        qmask = at(0, [2, HG, HG, CHUNK], F16)
        kmask = at(77.5, [2, HG, HG, CHUNK], F16)
        q3 = at(32, [2, HG, CHUNK], F16)
        k3 = at(40, [2, HG, CHUNK], F16)
        rmaxq = at(48, [2, CT_TILES, H])
        nmax = at(48.5, [CT_TILES * H])
        nmax16 = at(48.75, [2, CT_TILES * H], F16)
        nmaxT = at(49, [P], F16)
        orec = at(49.25, [32])
        onorm = at(49.5, [2, HP * 2 * DH])
        oT = at(50.5, [2, P])
        v9 = at(68, [2, CT_TILES, H, 2, DH + 1])
        qk16 = at(105.5, [2, 2, CHUNK], F16)
        w1raw1 = XN[:, 8:16, :].rearrange("p (u t) d -> p u (t d)", u=2)
        pexp = XN[:, NT // 2:NT, :].rearrange("p (u t) d -> p u (t d)", u=2)

        PS = ctx.enter_context(nc.psum_tensor("PS", [P, 8, 512], F32))
        PF = PS[:, :, :].rearrange("p b n -> p (b n)")

        def banks(b, n):
            return PF[:, b * 512:b * 512 + n]

        w_in = sem("w_in")
        x_in = [sem(f"x_in{c}") for c in range(NC)]
        pool_step = sem("pool_step")
        consts = sem("consts")
        dve_step = sem("dve_step")
        fold_ps, fold_sb = sem("fold_ps"), sem("fold_sb")
        xn_done = sem("xn_done")
        xt_ps, xt_done = sem("xt_ps"), sem("xt_done")
        c_ps, c_done = sem("c_ps"), sem("c_done")
        soft = {k: sem(f"soft_{k}") for k in ("logits", "shifted", "exp", "weights", "wT", "blocks", "pooled",
                                              "pooled_sb", "projected", "head_prod")}
        gsem = {k: sem(f"g_{k}") for k in ("moving", "ps", "sb")}
        v_ps, u_done = sem("v_ps"), sem("u_done")
        att_ps, x1_done = sem("att_ps"), sem("x1_done")
        gates = sem("gates")
        fold_in = sem("fold_in")
        rt = [{k: sem(f"r{l}_{k}") for k in ("xn", "xT", "xT_sb", "logits", "lg", "gap", "exp", "mask", "rank",
                                             "ranked", "count", "packed", "total", "table")} for l in range(2)]
        scat = [[sem(f"scat{l}_{u}") for u in range(2)] for l in range(2)]
        tails = sem("tails")
        zero, filled = sem("zero"), sem("filled")
        spare = sem("spare")
        fix_read, fix_kept = sem("fix_read"), sem("fix_kept")
        w1_in = [[sem(f"w1_in{l}_{u}") for u in range(2)] for l in range(2)]
        w2_in = [sem(f"w2_in{l}") for l in range(2)]
        w1_hi, w1_lo = [sem(f"w1_hi{l}") for l in range(2)], [sem(f"w1_lo{l}") for l in range(2)]
        ff = {k: [sem(f"f_{k}{u}") for u in range(n)] for k, n in
              (("xin", XS_LEAD), ("xT", 2), ("xT_sb", 2), ("up", 2), ("hid", 2), ("y", 2), ("yrow", 2), ("turn", 1),
               ("stored", XS_LEAD))}
        rounds = [TILES[l] // XS_LEAD for l in range(2)]
        before = [0, rounds[0]]
        y_in = [[sem(f"y_in{l}_{u}") for u in range(2)] for l in range(2)]
        x_ff = [sem(f"x_ff{l}") for l in range(2)]
        x_ffa = [sem(f"x_ffa{l}") for l in range(2)]
        xn3, x3t_ps, x3t_sb = sem("xn3"), sem("x3t_ps"), sem("x3t_sb")
        qk_ps, qk_hi, qk_lo = sem("qk_ps"), sem("qk_hi"), sem("qk_lo")
        qk_out = [sem(f"qk_out{u}") for u in range(2)]
        mask_rows, mask_T, mask_sb, mask_out = (sem(f"mask_{k}") for k in ("rows", "T", "sb", "out"))
        blank = sem("blank")
        s_in = [sem(f"s_in{u}") for u in range(2)]
        st_in = [sem(f"st_in{u}") for u in range(2)]
        v9_ps, v9_sb = sem("v9_ps"), sem("v9_sb")
        s_ps, s_max = sem("s_ps"), sem("s_max")
        n_ready, nT_ps, nT_sb = sem("n_ready"), sem("nT_ps"), sem("nT_sb")
        st_ps, p_done = sem("st_ps"), sem("p_done")
        av_ps, o_rec, o_norm = sem("av_ps"), sem("o_rec"), sem("o_norm")
        oT_ps, oT_sb, o_ps, x3_done = sem("oT_ps"), sem("oT_sb"), sem("o_ps"), sem("x3_done")
        stored = sem("stored")

        block = ctx.enter_context(nc.Block())

        def wait(engine, s, value):
            if not (isinstance(value, int) and value == 0):
                engine.wait_ge(s, value)

        def expert_tiles(engine, l, step):
            for q in range(XS_LEAD):
                step(0, q)
            with engine.Fori(1, TILES[l] // XS_LEAD) as i:
                for q in range(XS_LEAD):
                    step(i, q)

        def tiles(c):
            return slice(c * CT_TILES, (c + 1) * CT_TILES)

        def cols(c):
            return slice(c * CHUNK, (c + 1) * CHUNK)

        def slots(l, c):
            return tiles(c if l == 0 else c % 2)

        NW = 12
        S_LOADS, ST_LOADS = 3 + 3 * HG + 1, 3 + 3 * HG + 2 * HG
        LEAD = 6
        G0, G1 = -LEAD, 4 * (NC - 1) + 10
        BANK_XT, BANK_LG, BANK_RANK = (2, 7), (3, 7), (6, 7)

        def chunk_at(g, lead):
            k, rest = divmod(g - lead, CT_TILES)
            return k if rest == 0 and 0 <= k < NC else None

        @block.gpsimd
        def _(pool):
            n = [0]

            def then(ins):
                n[0] += 1
                ins.then_inc(pool_step, 1)
                pool.wait_ge(pool_step, n[0])

            g = nc.gpsimd
            g.memset(ident[:], 0.0)
            g.memset(ident16[:], 0.0)
            g.memset(tri16[:], 1.0)
            g.memset(ones16[:], 1.0)
            g.memset(onesrow[:], 1.0)
            g.memset(onesE[:], 1.0)
            g.memset(cum16[:], 0.0)
            g.memset(w2blk, 0.0)
            g.memset(g32, 0.0)
            g.memset(wa32, 0.0)
            g.memset(wqqa, 0.0)
            g.memset(padt, 0.0)
            g.memset(zrow[:], 0.0).then_inc(zero, 1)
            then(g.memset(hmask[:], 1.0))
            for t in (ident, ident16):
                g.affine_select(out=t[:], in_=t[:], compare_op=ALU.not_equal, fill=1.0, base=0,
                                pattern=[[-1, P]], channel_multiplier=1)
            g.affine_select(out=tri16[:], in_=tri16[:], compare_op=ALU.is_gt, fill=0.0, base=0,
                            pattern=[[1, P]], channel_multiplier=-1)
            then(g.affine_select(out=hmask[:], in_=hmask[:], compare_op=ALU.is_ge, fill=0.0, base=0,
                                 pattern=[[-DH, H]], channel_multiplier=1))
            g.affine_select(out=hmask[:], in_=hmask[:], compare_op=ALU.is_ge, fill=0.0, base=DH - 1,
                            pattern=[[DH, H]], channel_multiplier=-1)
            g.iota(expert_i[:], [[CAP, E]], base=0, channel_multiplier=0)
            g.iota(rev_i[:], [[-1, E]], base=E, channel_multiplier=0)
            g.iota(id_tok[:], [[TOPK * P, NT], [1, TOPK]], base=0, channel_multiplier=TOPK)
            g.iota(id_pad[:], [[TILE, 2 * E], [P, 2]], base=DUMMY, channel_multiplier=1)
            g.iota(pos_i[:], [[P, 80]], base=0, channel_multiplier=0)
            g.iota(lane_i[:], [[1, 1]], base=0, channel_multiplier=1)
            then(g.iota(eidx_i[:, 1, 0:TILES[1]], [[1, E], [0, TILES[1] // E]], base=0, channel_multiplier=0))
            g.tensor_copy(expert_row[:], expert_i[:])
            g.tensor_copy(rev[:], rev_i[:])
            g.tensor_copy(pos128[:], pos_i[:])
            g.tensor_copy(lane[:], lane_i[:]).then_inc(consts, 1)
            pid = padt.bitcast(U32)
            g.tensor_copy(pid[:, :, :, D:D + 1], id_pad[:, E:2 * E, :].unsqueeze(3)).then_inc(consts, 1)
            pool.wait_ge(consts, 2)
            g.dma_start(xs[0][FIX0:FIX0 + E * TILE, :].rearrange("(s u p) n -> p s u n", u=2, p=P),
                        padt).then_inc(spare, 16)
            pool.wait_ge(spare, 16)
            g.tensor_copy(pid[:, :, :, D:D + 1], id_pad[:, 0:E, :].unsqueeze(3)).then_inc(consts, 1)

            def scatter(l, c):
                pool.wait_ge(rt[l]["packed"], c + 1)
                pool.wait_ge(rt[l]["ranked"], c + 1)
                for s in range(CT_TILES):
                    for k in range(TOPK):
                        T = c * CT_TILES + s
                        g.indirect_dma_start(xs[l], bass.IndirectOffsetOnAxis(adr_i[:, T, k:k + 1], 0),
                                             pack[:, c % 2, s, k, :], None).then_inc(scat[l][c % 2], 16)

            def experts(l):
                def step(i, q):
                    pool.wait_ge(ff["yrow"][q % 2], (i + before[l]) * (XS_LEAD // 2) + q // 2 + 1)
                    g.tensor_tensor(turn[:, q:q + 1], lane[0:1, :], lane[0:1, :], ALU.mult).then_inc(ff["turn"][0], 1)
                    for u in range(2):
                        g.indirect_dma_start(
                            ys[l], bass.IndirectOffsetOnAxis(xin[:, q, u, :].bitcast(U32)[:, D:D + 1], 0),
                            yrow[:, q, u, :], None).then_inc(ff["stored"][q], 16)

                expert_tiles(pool, l, step)

            for c in range(NC):
                scatter(0, c)
            experts(0)
            pool.wait_ge(filled, 16 * E)
            for c in range(NC):
                scatter(1, c)
            pool.wait_ge(rt[1]["table"], 1)
            for u in range(2):
                pool.wait_ge(scat[1][u], 16 * CT_TILES * TOPK * (NC // 2))
            for q in range(E - 1):
                g.indirect_dma_start(fixs[:, q, :], None, xs[1][0:FIX0, :],
                                     bass.IndirectOffsetOnAxis(fixadr_i[:, q:q + 1], 0)).then_inc(fix_read, 16)
            experts(1)

        def load(sp, l, i_tile, q):
            for u in range(2):
                r = sp.value_load(rows_i[0:1, ds(i_tile * 2 + u, 1)], min_val=0, max_val=XS_ROWS - P)
                sp.dma_start(xin[:, q, u, :], xs[l][ds(r, P), :]).then_inc(ff["xin"][q], 16)

        def y_rows(l, c):
            return ys[l][c * CHUNK * TOPK:(c + 1) * CHUNK * TOPK, :].rearrange("(s p k) d -> p s (k d)", p=P, k=TOPK)

        x_rows = A["x"].rearrange("(t p) d -> p t d", p=P)
        c_rows = A["ctx"].rearrange("(t p) d -> p t d", p=P)
        out_rows = out.rearrange("(t p) d -> p t d", p=P)

        @block.sync
        def _(sp):
            for c in range(NC):
                t = slice(c * CT_TILES, (c + 1) * CT_TILES)
                sp.dma_start(X[:, t, :], x_rows[:, t, :]).then_inc(x_in[c], 16)
                if c == 0:
                    sp.dma_start(W[:], A["W"].rearrange("w i o -> i w o")).then_inc(w_in, 16)
                    sp.dma_start(wa[:], A["wa"].rearrange("w i o -> i w o")).then_inc(w_in, 16)
                    sp.dma_start(wr[:], A["wr"].rearrange("w i o -> i w o")).then_inc(w_in, 16)
                    sp.dma_start(bcol[:], A["bcol"]).then_inc(w_in, 16)
                    sp.dma_start(bacol[:], A["bacol"]).then_inc(w_in, 16)
                    sp.dma_start(bprow[:], A["bp"]).then_inc(w_in, 16)
                    sp.dma_start(brb[:], A["br"].partition_broadcast(P)).then_inc(w_in, 16)
                    sp.dma_start(b1[:], A["b1"]).then_inc(w_in, 16)
                    sp.dma_start(b2b, A["b2"].partition_broadcast(P)).then_inc(w_in, 16)
                    sp.dma_start(g4[:], A["g"].partition_broadcast(P)).then_inc(w_in, 16)
                    sp.dma_start(mask_u8[:], A["mask"]).then_inc(w_in, 16)
                    sp.dma_start(w2[:].rearrange("p (e c d) -> p e c d", e=E, c=FC),
                                 A["w2_0"].rearrange("e (c p) d -> p e c d", p=P)).then_inc(w_in, 16)
                sp.dma_start(ctx_tok[:, t, :], c_rows[:, t, :]).then_inc(x_in[c], 16)

            def w1_loads(l, raw):
                for e in range(E):
                    if e >= 2:
                        sp.wait_ge(w1_lo[l], e - 1)
                    sp.dma_start(raw[:, e % 2, :], A[f"w1_{l}"][e]).then_inc(w1_in[l][e % 2], 16)

            sp.wait_ge(zero, 1)
            for e in range(E):
                sp.dma_start(xs[1][e * CAP:(e + 1) * CAP, :].rearrange("(p m) n -> p m n", p=P),
                             bc(zrow[:], 1, CAP // P)).then_inc(filled, 16)
            w1_loads(0, w1raw)

            sp.wait_ge(rt[0]["table"], 1)
            sp.wait_ge(consts, 3)
            for e in range(E):
                r = sp.value_load(tail_i[0:1, e:e + 1], min_val=0, max_val=XS_ROWS - TILE)
                sp.dma_start(xs[0][ds(r, TILE), :].rearrange("(u p) n -> p u n", p=P), padt[:, e, :, :]).then_inc(tails, 16)
            sp.wait_ge(tails, 16 * E)
            sp.wait_ge(spare, 16)
            for u in range(2):
                sp.wait_ge(scat[0][u], 16 * CT_TILES * TOPK * (NC // 2))

            def experts(l):
                def step(i, q):
                    wait(sp, ff["stored"][q], (i + before[l]) * STORED)
                    load(sp, l, i * XS_LEAD + q, q)

                expert_tiles(sp, l, step)
                for q in range(XS_LEAD):
                    sp.wait_ge(ff["stored"][q], STORED * (before[l] + rounds[l]))
                for c in range(NC):
                    if c >= 2:
                        sp.wait_ge(x_ff[l], c - 1)
                    sp.dma_start(yc[:, c % 2, :, :, :].rearrange("p s k d -> p s (k d)"), y_rows(l, c)).then_inc(y_in[l][c % 2], 16)
                    if l == 1 and c >= 1:
                        store(c - 1)
                if l == 1:
                    store(NC - 1)

            def store(c):
                sp.wait_ge(x_ff[1], c + 1)
                t = slice(c * CT_TILES, (c + 1) * CT_TILES)
                sp.dma_start(out_rows[:, t, :], X[:, t, :]).then_inc(stored, 16)

            experts(0)

            sp.wait_ge(mask_rows, 1)
            sp.dma_start(mask_dram, mask16[:]).then_inc(mask_out, 16)
            for m in range(2 * NC):
                c, which = m // 2, m % 2
                sp.wait_ge(qk_lo, m + 1)
                sp.dma_start(qk_dram[which][:, :, cols(c)].rearrange("h p n -> p h n"), qk16[:, which, :, :])\
                    .then_inc(qk_out[which], 16)
            sp.wait_ge(x_ff[0], NC)
            sp.dma_start(w2[:].rearrange("p (e c d) -> p e c d", e=E, c=FC),
                         A["w2_1"].rearrange("e (c p) d -> p e c d", p=P)).then_inc(w2_in[1], 16)
            sp.wait_ge(blank, 1)
            sp.wait_ge(mask_out, 16)
            for which in range(2):
                sp.wait_ge(qk_out[which], 16 * NC)

            def grouped(which, part, c):
                return qk_dram[which][part, :, cols(c)].rearrange("(r i) t -> i r t", r=HG)

            def blocks(dst, which, part, term, c):
                for hj in range(HG):
                    p0 = term * 32 + hj * DH
                    yield (dst[p0:p0 + DH, c % 2, hj, :, :],
                           qk_dram[which][part, :, cols(c)].rearrange("(r j d) t -> j d r t", r=HG, j=HG)[hj])

            def load_s(c):
                u = c % 2
                if c >= 2:
                    sp.wait_ge(s_ps, CT_TILES * (c - 1))
                for term, (qp, kp) in enumerate(((0, 0), (1, 0), (0, 1))):
                    sp.dma_start(q3[term * 32:term * 32 + 32, u, :, :], grouped(0, qp, c)).then_inc(s_in[u], 16)
                    for d, s_ in blocks(kmask, 1, kp, term, c):
                        sp.dma_start(d, s_).then_inc(s_in[u], 16)
                row = mask_dram[tiles(c), :].rearrange("s p -> (s p)").unsqueeze(0).unsqueeze(1)
                sp.dma_start(kmask[96:97, u, :, :, :].rearrange("o j r n -> o (j r) n"), row.broadcast_to([1, H, CHUNK])).then_inc(s_in[u], 16)

            def load_st(c):
                u = c % 2
                if c >= 2:
                    sp.wait_ge(st_ps, CT_TILES * (c - 1))
                for term, (qp, kp) in enumerate(((0, 0), (1, 0), (0, 1))):
                    sp.dma_start(k3[term * 32:term * 32 + 32, u, :, :], grouped(1, kp, c)).then_inc(st_in[u], 16)
                    for d, s_ in blocks(qmask, 0, qp, term, c):
                        sp.dma_start(d, s_).then_inc(st_in[u], 16)

            def load_max(c):
                sp.wait_ge(nT_sb, c + 1)
                for j in range(2 * HG):
                    d = qmask[96 + j:97 + j, c % 2, j % HG, :, :].rearrange("o r n -> o (r n)")
                    sp.dma_start(d, nmaxT[16 * j:16 * j + 16, :]).then_inc(st_in[c % 2], 16)

            def w1_load(e):
                if e >= 2:
                    sp.wait_ge(w1_lo[1], e - 1)
                sp.dma_start(w1raw1[:, e % 2, :], A["w1_1"][e]).then_inc(w1_in[1][e % 2], 16)

            load_s(0)
            load_st(0)
            sp.wait_ge(blank, 2)
            load_s(1)
            for c in range(NC):
                load_max(c)
                if c + 2 < NC:
                    load_s(c + 2)
                if c + 1 < NC:
                    load_st(c + 1)
                w1_load(c)
            sp.wait_ge(rt[1]["table"], 1)
            sp.wait_ge(fix_read, 16 * (E - 1))
            sp.dma_start(xs[1][FIX0:FIX0 + (E - 1) * P, :].rearrange("(q p) n -> p q n", p=P), fixs).then_inc(fix_kept, 16)
            sp.wait_ge(fix_kept, 16)
            for u in range(2):
                sp.wait_ge(scat[1][u], 16 * CT_TILES * TOPK * (NC // 2))
            experts(1)
            sp.wait_ge(stored, 16 * NC)

        @block.tensor
        def _(pe):
            t = nc.tensor

            def mm(o, lhsT, rhs, start=True, stop=True):
                return t.matmul(o, lhsT, rhs, start=start, stop=stop, skip_group_check=True)

            pe.wait_ge(w_in, 16 * NW)
            pe.wait_ge(consts, 1)
            pe.wait_ge(fold_in, 2)
            mm(PS[:, 4, 0:H], wqT, wa[:, 0, :])
            mm(PS[:, 4, D:2 * D], wtT, wp)
            mm(PS[:, 4, 2 * D:3 * D], wqT, wp)
            mm(PS[0:1, 5, 0:D], btq[:, 0:1], wp)
            mm(PS[:, 5, D:D + 1], wa32[:, 0, :, :].rearrange("p j h -> p (j h)"), bcol[:, 0:1]).then_inc(fold_ps, 1)

            def q_logits(c):
                pe.wait_ge(xt_done, c + 1)
                pe.wait_ge(fold_sb, 1)
                j = 32 * (c % 4)
                mm(PS[j:j + 32, 6 + c // 4, :], wqqa, xnT[:, cols(c)]).then_inc(soft["logits"], 1)

            for c in range(NC):
                pe.wait_ge(xn_done, c + 1)
                if c >= 2:
                    pe.wait_ge(xt_done, c - 1)
                for s in range(CT_TILES):
                    ins = t.transpose(PS[:, c % 2, s * P:(s + 1) * P], XN[:, c * CT_TILES + s, :], ident[:])
                ins.then_inc(xt_ps, 1)
                pe.wait_ge(x_in[c], 32)
                if c >= 2:
                    pe.wait_ge(c_done, c - 1)
                for s in range(CT_TILES):
                    ins = t.transpose(PS[:, 2 + c % 2, s * P:(s + 1) * P], ctx_tok[:, c * CT_TILES + s, :], ident[:])
                ins.then_inc(c_ps, 1)
                if c >= 1:
                    q_logits(c - 1)
            q_logits(NC - 1)

            def pooled(r, src, w):
                pe.wait_ge(soft["weights"], r + 1)
                for i in range(8):
                    ins = t.transpose(PS[:, i // 4, (i % 4) * P:(i % 4 + 1) * P], se[:, i * P:(i + 1) * P], ident[:])
                ins.then_inc(soft["wT"], 1)
                pe.wait_ge(soft["blocks"], r + 1)
                for T in range(NT):
                    ins = mm(PF[:, 1024 + T * 32:1024 + (T + 1) * 32], src[:, T, :],
                             w2blk[:, T, :, :].rearrange("p b h -> p (b h)"))
                ins.then_inc(soft["pooled"], 1)
                pe.wait_ge(soft["pooled_sb"], r + 1)
                for i in range(2):
                    ins = mm(PS[:, 4 + i, :], w, xp[:, i * 512:(i + 1) * 512])
                ins.then_inc(soft["projected"], 1)

            pe.wait_ge(c_done, NC)
            pooled(0, XN, wq)
            pe.wait_ge(gsem["moving"], 1)
            for i in range(2):
                mm(PS[:, 2 + i, :], wkT, gp.rearrange("p b h -> p (b h)")[:, i * 512:(i + 1) * 512])
            pqv = pq.rearrange("p (a j b) -> p a j b", a=2, j=4)
            for j in range(4):
                ins = mm(PS[32 * j:32 * j + 32, 0, 0:16], wka_bk, pqv[:, :, j, :])
            ins.then_inc(gsem["ps"], 1)
            pe.wait_ge(gsem["sb"], 1)
            for b in range(NB):
                c, bb = b // CB, b % CB
                j = 32 * (c % 4)
                ins = mm(PS[j:j + 32, 6 + c // 4, bb * SEQ:(bb + 1) * SEQ], g32[:, b, :], ctT[:, b * SEQ:(b + 1) * SEQ])
            ins.then_inc(soft["logits"], 1)
            pooled(1, ctx_tok, wk)

            def values(c):
                pe.wait_ge(*((u_done, c - 1) if c >= 2 else (soft["head_prod"], 2)))
                mm(PS[:, 4 + c % 2, :], wv, ctT[:, cols(c)]).then_inc(v_ps, 1)

            def attended(c):
                pe.wait_ge(u_done, c + 1)
                if c >= 2:
                    pe.wait_ge(x1_done, c - 1)
                for s in range(CT_TILES):
                    o = PS[:, c % 2, s * D:(s + 1) * D]
                    T = c * CT_TILES + s
                    mm(o, uT[:, c % 2, s * P:(s + 1) * P], wtp, stop=False)
                    mm(o, xnT[:, T * P:(T + 1) * P], wqp, start=False, stop=False)
                    ins = mm(o, onesrow[:], crow[0:1, :], start=False)
                ins.then_inc(att_ps, 1)

            def route_transposed(l, c):
                pe.wait_ge(rt[l]["xn"], c + 1)
                if c >= 1:
                    pe.wait_ge(rt[l]["xT_sb"], c)
                for s in range(CT_TILES):
                    ins = t.transpose(PS[:, BANK_XT[l], s * P:(s + 1) * P], XN[:, slots(l, c).start + s, :], ident[:])
                ins.then_inc(rt[l]["xT"], 1)

            def route_logits(l, c):
                pe.wait_ge(rt[l]["xT_sb"], c + 1)
                if c >= 1:
                    pe.wait_ge(rt[l]["lg"], c)
                for s in range(CT_TILES):
                    ins = mm(PS[:, BANK_LG[l], s * E:(s + 1) * E], rxt[:, s * P:(s + 1) * P], wr[:, l, :])
                ins.then_inc(rt[l]["logits"], 1)

            def route_rank(l, c):
                pe.wait_ge(rt[l]["mask"], c + 1)
                if c >= 1:
                    pe.wait_ge(rt[l]["ranked"], c)
                    pe.wait_ge(rt[l]["count"], c)
                for s in range(CT_TILES):
                    o = PS[:, BANK_RANK[l], s * E:(s + 1) * E]
                    mm(o, ones16[:], cum16[:], stop=False)
                    for b in range(s):
                        mm(o, ones16[:], sel16[:, c * CT_TILES + b, :], start=False, stop=False)
                    ins = mm(o, tri16[:], sel16[:, c * CT_TILES + s, :], start=False)
                ins.then_inc(rt[l]["rank"], 1)

            def route_total(l):
                pe.wait_ge(rt[l]["count"], NC)
                mm(PS[:, BANK_RANK[l], 64:64 + E], ones16[:], cum16[:]).then_inc(rt[l]["total"], 1)

            for k in range(NC + 3):
                if k < NC:
                    values(k)
                if 1 <= k <= NC:
                    attended(k - 1)
                if 2 <= k <= NC + 1:
                    route_transposed(0, k - 2)
                    route_logits(0, k - 2)
                if k >= 3:
                    route_rank(0, k - 3)
            route_total(0)

            def experts(l):
                f, i0 = ff, before[l]
                pe.wait_ge(w1_lo[l], E)
                if l == 1:
                    pe.wait_ge(w2_in[1], 16)
                pe.wait_ge(rt[l]["table"], 1)

                def gather(i, q):
                    v, m = q % 2, (i + i0) * (XS_LEAD // 2) + q // 2
                    pe.wait_ge(f["xin"][q], (i + i0) * 32 + 32)
                    wait(pe, f["xT_sb"][v], m)
                    o = PS[:, v, 0:TILE].bitcast(F16).rearrange("p (h u n) -> p h u n", h=2, u=2)
                    for u in range(2):
                        for h in range(2):
                            ins = t.transpose(o[:, h, u, :], xin[:, q, u, h * D:(h + 1) * D], ident16[:])
                    ins.then_inc(f["xT"][v], 1)

                def up(i, q, e):
                    v, m = q % 2, (i + i0) * (XS_LEAD // 2) + q // 2
                    pe.wait_ge(f["xT_sb"][v], m + 1)
                    wait(pe, f["hid"][v], m)
                    for c in range(FC):
                        o = PF[:, (2 + 2 * v) * 512 + c * TILE:(2 + 2 * v) * 512 + (c + 1) * TILE]
                        for k, (w, h) in enumerate(((w1h, 0), (w1h, 1), (w1l, 0))):
                            ins = mm(o, w[:, ds(e * FF + c * P, P)], xgT[:, v, h, :], start=k == 0, stop=k == 2)
                    ins.then_inc(f["up"][v], 1)

                def down(i, q, e):
                    v, m = q % 2, (i + i0) * (XS_LEAD // 2) + q // 2
                    pe.wait_ge(f["hid"][v], m + 1)
                    wait(pe, f["yrow"][v], m)
                    for u in range(2):
                        for c in range(FC):
                            ins = mm(PS[:, 6 + v, u * D:(u + 1) * D], hid[:, v, c, u * P:(u + 1) * P],
                                     w2[:, ds(e * FF + c * D, D)], start=c == 0, stop=c == FC - 1)
                    ins.then_inc(f["y"][v], 1)

                def expert(tile):
                    return pe.value_load(eidx_i[0:1, l, ds(tile, 1)], min_val=0, max_val=E - 1)

                def round_(i, first, last):
                    for q in range(XS_LEAD):
                        if q < XS_LEAD - 1:
                            gather(i, q + 1)
                        elif not last:
                            gather(i + 1, 0)
                        up(i, q, expert(i * XS_LEAD + q))
                        if q >= 1:
                            down(i, q - 1, expert(i * XS_LEAD + q - 1))
                        elif not first:
                            down(i - 1, XS_LEAD - 1, expert(i * XS_LEAD - 1))

                n = TILES[l] // XS_LEAD
                gather(0, 0)
                round_(0, True, False)
                with pe.Fori(1, n - 1) as i:
                    round_(i, False, False)
                round_(n - 1, False, True)
                down(n - 1, XS_LEAD - 1, expert(TILES[l] - 1))

            experts(0)

            pe.wait_ge(mask_rows, 1)
            t.transpose(PS[:, 4, 0:NT], mask_f[:], ident[0:NT, 0:NT]).then_inc(mask_T, 1)
            for c in range(NC):
                pe.wait_ge(xn3, c + 1)
                if c >= 2:
                    pe.wait_ge(x3t_sb, c - 1)
                for s in range(CT_TILES):
                    ins = t.transpose(PS[:, c % 2, s * P:(s + 1) * P], XN[:, c * CT_TILES + s, :], ident[:])
                ins.then_inc(x3t_ps, 1)
                if c >= 1:
                    pe.wait_ge(qk_lo, 2 * c)
                pe.wait_ge(x3t_sb, c + 1)
                mm(PS[:, 2, :], wq1T, xnT[:, cols(c)]).then_inc(qk_ps, 1)
                mm(PS[:, 3, :], wk1T, ctT[:, cols(c)]).then_inc(qk_ps, 1)

            def scores(T):
                c, s = T // CT_TILES, T % CT_TILES
                if s == 0:
                    pe.wait_ge(s_in[c % 2], 16 * S_LOADS * (c // 2 + 1))
                if T >= 1:
                    pe.wait_ge(s_max, T)
                for b in range(2):
                    q_ = slice(s * P + b * SEQ, s * P + (b + 1) * SEQ)
                    for r in range(HG):
                        ins = mm(PF[b * SEQ:(b + 1) * SEQ, r * 256:(r + 1) * 256], q3[0:97, c % 2, r, q_],
                                 kmask[0:97, c % 2, :, r, q_])
                ins.then_inc(s_ps, 1)

            def scores_by_key(T):
                c, s = T // CT_TILES, T % CT_TILES
                if s == 0:
                    pe.wait_ge(st_in[c % 2], 16 * ST_LOADS * (c // 2 + 1))
                if T >= 1:
                    pe.wait_ge(p_done, T)
                for b in range(2):
                    q_ = slice(s * P + b * SEQ, s * P + (b + 1) * SEQ)
                    for r in range(HG):
                        ins = mm(PF[b * SEQ:(b + 1) * SEQ, 1024 + r * 256:1024 + (r + 1) * 256],
                                 k3[0:104, c % 2, r, q_], qmask[0:104, c % 2, :, r, q_])
                ins.then_inc(st_ps, 1)

            def weigh(T):
                c, s = T // CT_TILES, T % CT_TILES
                pe.wait_ge(p_done, T + 1)
                if s == 0:
                    pe.wait_ge(v9_sb, c + 1)
                if T >= 1:
                    pe.wait_ge(o_norm, T)
                for hp in range(HP):
                    ins = mm(PS[:, 4, hp * 36:(hp + 1) * 36], pexp[:, T % 2, hp * P:(hp + 1) * P],
                             v9[:, c % 2, s, 2 * hp:2 * hp + 2, :, :].rearrange("p h b n -> p (h b n)"))
                ins.then_inc(av_ps, 1)

            def heads_transposed(T):
                pe.wait_ge(o_norm, T + 1)
                if T >= 1:
                    pe.wait_ge(oT_sb, T)
                for b in range(2):
                    ins = t.transpose(PS[:, 5, b * P:(b + 1) * P], onorm[:, b, :], ident[:])
                ins.then_inc(oT_ps, 1)

            def project_heads(T):
                pe.wait_ge(oT_sb, T + 1)
                if T >= 1:
                    pe.wait_ge(x3_done, T)
                mm(PS[:, 6, 0:D], oT[:, T % 2, :], wo1T).then_inc(o_ps, 1)

            pe.wait_ge(mask_sb, 1)
            for g in range(G0, G1):
                if 0 <= g < NT:
                    scores_by_key(g)
                if 0 <= g + LEAD < NT:
                    scores(g + LEAD)
                if 0 <= g - 1 < NT:
                    weigh(g - 1)
                if 0 <= g - 2 < NT:
                    heads_transposed(g - 2)
                if 0 <= g - 3 < NT:
                    project_heads(g - 3)
                k = chunk_at(g, 9)
                if k is not None:
                    route_rank(1, k)
                k = chunk_at(g, 3 - LEAD)
                if k is not None:
                    pe.wait_ge(n_ready, k + 1)
                    if k >= 3:
                        pe.wait_ge(rt[1]["ranked"], k - 2)
                    t.transpose(PS[:, 7, 0:P // 2].bitcast(F16), nmax16.rearrange("p k n -> p (k n)"), ident16[:])\
                        .then_inc(nT_ps, 1)
                k = chunk_at(g, -2)
                if k is not None:
                    pe.wait_ge(nT_sb, k + 1)
                    for s in range(CT_TILES):
                        T = k * CT_TILES + s
                        ins = mm(PS[:, 7, s * D:(s + 1) * D], ctT[:, T * P:(T + 1) * P], wv1T)
                    ins.then_inc(v9_ps, 1)
                k = chunk_at(g, 7)
                if k is not None:
                    pe.wait_ge(v9_sb, min(k + 3, NC))
                    route_transposed(1, k)
                k = chunk_at(g, 8)
                if k is not None:
                    route_logits(1, k)
            route_total(1)
            experts(1)

        @block.scalar
        def _(act):
            a = nc.scalar
            act.wait_ge(w_in, 16 * NW)
            a.activation(gt[:], g4[:], ACT.Tanh).then_inc(gates, 1)
            for c in range(NC):
                act.wait_ge(xt_ps, c + 1)
                a.activation(xnT[:, cols(c)], PS[:, c % 2, :], ACT.Copy).then_inc(xt_done, 1)
                act.wait_ge(c_ps, c + 1)
                a.activation(ctT[:, cols(c)], PS[:, 2 + c % 2, :], ACT.Copy).then_inc(c_done, 1)

            def soft_steps(r):
                act.wait_ge(soft["shifted"], r + 1)
                a.activation(se, sl, ACT.Exp, scale=float(DH) ** -0.5).then_inc(soft["exp"], 1)
                act.wait_ge(soft["pooled"], r + 1)
                a.activation(xp, banks(2, 1024), ACT.Copy).then_inc(soft["pooled_sb"], 1)

            soft_steps(0)
            act.wait_ge(gsem["ps"], 1)
            act.wait_ge(consts, 1)
            a.activation(g32[:, :, 0:H], banks(2, 1024).rearrange("p (b h) -> p b h", h=H), ACT.Copy).then_inc(gsem["sb"], 1)
            soft_steps(1)

            def route_xT(l, c):
                act.wait_ge(rt[l]["xT"], c + 1)
                if c >= 1:
                    act.wait_ge(rt[l]["logits"], c)
                a.activation(rxt[:], PS[:, BANK_XT[l], :], ACT.Copy).then_inc(rt[l]["xT_sb"], 1)

            def route_exp(l, c):
                act.wait_ge(rt[l]["gap"], c + 1)
                a.activation(wexp[:, tiles(c)], wdif[:, tiles(c)], ACT.Exp).then_inc(rt[l]["exp"], 1)

            for c in range(NC):
                route_xT(0, c)
                route_exp(0, c)

            def experts(l):
                f, i0 = ff, before[l]
                act.wait_ge(rt[l]["table"], 1)
                def step(i, q):
                    v, m = q % 2, (i + i0) * (XS_LEAD // 2) + q // 2
                    act.wait_ge(f["up"][v], m + 1)
                    wait(act, f["y"][v], m)
                    b = 2 + 2 * v
                    if l == 0:
                        e = act.value_load(eidx_i[0:1, l, ds(i * XS_LEAD + q, 1)], min_val=0, max_val=E - 1)
                        for c in range(FC):
                            ins = a.activation(hid[:, v, c, :], PF[:, b * 512 + c * TILE:b * 512 + (c + 1) * TILE],
                                               ACT.Relu, bias=b1[:, ds(e * FC + c, 1)], scale=1 / WSCALE)
                    else:
                        ins = a.activation(hid[:, v, :, :].rearrange("p c n -> p (c n)"), banks(b, 1024),
                                           ACT.Gelu, scale=1 / WSCALE)
                    ins.then_inc(f["hid"][v], 1)

                expert_tiles(act, l, step)

            experts(0)

            act.wait_ge(mask_T, 1)
            a.activation(mask_bias[:], PS[:, 4, 0:NT], ACT.Copy).then_inc(mask_sb, 1)
            for c in range(NC):
                act.wait_ge(x3t_ps, c + 1)
                a.activation(xnT[:, cols(c)], PS[:, c % 2, :], ACT.Copy).then_inc(x3t_sb, 1)
                for which in range(2):
                    act.wait_ge(qk_ps, 2 * c + which + 1)
                    if c >= 1:
                        act.wait_ge(qk_out[which], 16 * c)
                    a.activation(qk16[:, which, 0, :], PS[:, 2 + which, :], ACT.Copy, scale=QK_SCALE[which]).then_inc(qk_hi, 1)

            act.wait_ge(mask_sb, 1)
            for g in range(G0, G1):
                T = g
                if 0 <= T < NT:
                    act.wait_ge(st_ps, T + 1)
                    if T >= 2:
                        act.wait_ge(av_ps, T - 1)
                    a.activation(pexp[:, T % 2, :], banks(2, 1024), ACT.Exp, bias=mask_bias[:, T:T + 1]).then_inc(p_done, 1)
                T = g - 2
                if 0 <= T < NT:
                    act.wait_ge(oT_ps, T + 1)
                    if T >= 2:
                        act.wait_ge(o_ps, T - 1)
                    for h2 in range(2):
                        ph = slice(h2 * 64, h2 * 64 + 64)
                        ins = a.activation(oT[ph, T % 2, :].rearrange("p (b q) -> p b q", b=2),
                                           PS[ph, 5, 0:2 * P].rearrange("p (b h q) -> p b h q", b=2, h=2)[:, :, h2, :],
                                           ACT.Copy)
                    ins.then_inc(oT_sb, 1)
                k = chunk_at(g, 3 - LEAD)
                if k is not None:
                    act.wait_ge(nT_ps, k + 1)
                    if k >= 1:
                        act.wait_ge(st_in[(k - 1) % 2], 16 * ST_LOADS * ((k - 1) // 2 + 1))
                    a.activation(nmaxT, PS[:, 7, 0:P // 2].bitcast(F16), ACT.Copy).then_inc(nT_sb, 1)
                k = chunk_at(g, -2)
                if k is not None:
                    act.wait_ge(v9_ps, k + 1)
                    act.wait_ge(blank, 1)
                    if k >= 2:
                        act.wait_ge(av_ps, CT_TILES * (k - 1))
                    for hb in range(2):
                        ph = slice(hb * 64, hb * 64 + 64)
                        ins = a.activation(v9[ph, k % 2, :, :, hb, 0:DH].rearrange("p s h d -> p (s h) d"),
                                           PS[ph, 7, :].rearrange("p (n d) -> p n d", d=DH), ACT.Copy)
                    ins.then_inc(v9_sb, 1)
                k = chunk_at(g, 7)
                if k is not None:
                    route_xT(1, k)
                k = chunk_at(g, 8)
                if k is not None:
                    route_exp(1, k)
            experts(1)

        @block.vector
        def _(dve):
            n = [0]
            v_ = nc.vector

            def link(ins):
                n[0] += 1
                ins.then_inc(dve_step, 1)
                dve.wait_ge(dve_step, n[0])

            def tt(o, x, y, op):
                return v_.tensor_tensor(o, x, y, op)

            def norm(c, slot, done):
                t = tiles(c)
                for T in range(t.start, t.stop):
                    ins = v_.bn_stats(stats[:, T, :], X[:, T, :])
                link(ins)
                for T in range(t.start, t.stop):
                    ins = v_.bn_aggr(mv[:, T, :], stats[:, T, :])
                link(ins)
                x, y, z = nwt[:, 0, :], rstd[:, t], nwt[:, 1, :]
                link(v_.tensor_scalar(x, mv[:, t, 1], EPS, None, ALU.add))
                link(v_.tensor_scalar(z.bitcast(I32), x.bitcast(I32), 1, None, ALU.arith_shift_right))
                link(v_.tensor_scalar(y.bitcast(I32), z.bitcast(I32), -1.0, float(0x5F3759DF), ALU.mult, ALU.add))
                for _ in range(3):
                    link(v_.scalar_tensor_tensor(out=z, in0=y, scalar=-0.5, in1=y, op0=ALU.mult, op1=ALU.mult))
                    link(tt(z, z, x, ALU.mult))
                    link(v_.scalar_tensor_tensor(out=y, in0=z, scalar=1.5, in1=y, op0=ALU.add, op1=ALU.mult))
                for s in range(CT_TILES):
                    T = t.start + s
                    ins = v_.tensor_scalar(XN[:, slot.start + s, :], X[:, T, :], mv[:, T, 0:1], rstd[:, T:T + 1],
                                           ALU.subtract, ALU.mult)
                ins.then_inc(done, 1)

            def split_w1(l, raw, e):
                dve.wait_ge(w1_in[l][e % 2], 16 * (e // 2 + 1))
                o = slice(e * FF, (e + 1) * FF)
                v_.tensor_scalar(w1h[:, o], raw[:, e % 2, :], WSCALE, None, ALU.mult).then_inc(w1_hi[l], 1)
                dve.wait_ge(w1_hi[l], e + 1)
                v_.scalar_tensor_tensor(out=w1l[:, o], in0=raw[:, e % 2, :], scalar=WSCALE, in1=w1h[:, o],
                                        op0=ALU.mult, op1=ALU.subtract).then_inc(w1_lo[l], 1)

            dve.wait_ge(w_in, 16 * NW)
            dve.wait_ge(consts, 1)
            v_.tensor_copy(wa32[:, :, :, 0:H], bc(wa[:], 2, 4)).then_inc(fold_in, 1)
            tt(btq[:, 0:1], bcol[:, 0:1], bcol[:, 3:4], ALU.add).then_inc(fold_in, 1)
            for c in range(NC):
                dve.wait_ge(x_in[c], 32)
                norm(c, tiles(c), xn_done)
                if c == 0:
                    dve.wait_ge(fold_ps, 1)
                    dve.wait_ge(gates, 1)
                    v_.tensor_copy(wqqa[:, 0:H], PS[:, 4, 0:H])
                    v_.tensor_scalar(wtp, PS[:, 4, D:2 * D], gt[:, 0:1], None, ALU.mult)
                    v_.tensor_scalar(wqp, PS[:, 4, 2 * D:3 * D], gt[:, 0:1], None, ALU.mult)
                    link(tt(crow[0:1, :], PS[0:1, 5, 0:D], bprow[:], ALU.add))
                    v_.tensor_scalar(crow[0:1, :], crow[0:1, :], gt[0:1, 0:1], None, ALU.mult)
                    tt(qb[:, 0:1], PS[:, 5, D:D + 1], bacol[:, 0:1], ALU.add).then_inc(fold_sb, 1)

            def softmax(r, groups=16):
                lp = banks(6, 1024)
                g3 = sl.rearrange("p (g l) -> p g l", l=SEQ)
                e3 = se.rearrange("p (g l) -> p g l", l=SEQ)
                dve.wait_ge(soft["logits"], NC + r)
                if r == 0:
                    dve.wait_ge(fold_sb, 1)
                    link(v_.tensor_scalar(sl, lp, qb[:, 0:1], None, ALU.add))
                else:
                    link(tt(g3, lp.rearrange("p (g l) -> p g l", l=SEQ), bc(kb16, 2, SEQ), ALU.add))
                link(v_.tensor_reduce(smx, g3, AX, ALU.max))
                tt(g3, g3, bc(smx, 2, SEQ), ALU.subtract).then_inc(soft["shifted"], 1)
                dve.wait_ge(soft["exp"], r + 1)
                link(v_.tensor_reduce(ssum, e3, AX, ALU.add))
                link(v_.reciprocal(srec, ssum))
                tt(e3, e3, bc(srec, 2, SEQ), ALU.mult).then_inc(soft["weights"], 1)
                dve.wait_ge(soft["wT"], r + 1)
                for hb in range(2):
                    ph = slice(hb * 64, hb * 64 + 64)
                    for a in range(2):
                        o = w2blk.rearrange("p (a j s) b h -> p a s j b h", a=2, j=4)[ph, a, :, :, hb, :]
                        i_ = PS[ph, a, :].rearrange("p (s j h) -> p s j h", s=4, j=4)[:, :, :, 0:H]
                        ins = v_.tensor_copy(o, i_)
                ins.then_inc(soft["blocks"], 1)

            def head_sum(r, dst, bias):
                dve.wait_ge(soft["projected"], r + 1)
                p3 = prod.rearrange("p (b h) -> p b h", h=H)
                link(tt(p3, banks(4, 1024).rearrange("p (b h) -> p b h", h=H), bc(hmask[:], 1, NB), ALU.mult))
                link(v_.tensor_reduce(dst, p3, AX, ALU.add))
                v_.tensor_scalar(dst, dst, bias, None, ALU.add).then_inc(soft["head_prod"], 1)
                dve.wait_ge(soft["head_prod"], r + 1)

            softmax(0)
            head_sum(0, pq, bcol[:, 0:1])
            v_.tensor_scalar(wka_bk, wa32[:, 1, 0, :], bcol[:, 1:2], None, ALU.mult)
            tt(gp, bc(wa[:, 1, :], 1, NB), bc(pq, 2, H), ALU.mult).then_inc(gsem["moving"], 1)
            dve.wait_ge(gsem["ps"], 1)
            link(v_.tensor_scalar(kb16, PS[:, 0, 0:16], bacol[:, 1:2], None, ALU.add))
            softmax(1)
            head_sum(1, pkv, bcol[:, 1:2])

            def scaled_values(c):
                dve.wait_ge(v_ps, c + 1)
                if c >= 2:
                    dve.wait_ge(att_ps, c - 1)
                v_.scalar_tensor_tensor(out=uT[:, c % 2, :].rearrange("p (b l) -> p b l", l=SEQ),
                                        in0=PS[:, 4 + c % 2, :].rearrange("p (b l) -> p b l", l=SEQ),
                                        scalar=bcol[:, 2:3], in1=bc(pkv[:, c * CB:(c + 1) * CB], 2, SEQ),
                                        op0=ALU.add, op1=ALU.mult).then_inc(u_done, 1)

            def residual(c):
                dve.wait_ge(att_ps, c + 1)
                x = X[:, tiles(c), :].rearrange("p s d -> p (s d)")
                tt(x, x, PS[:, c % 2, :], ALU.add).then_inc(x1_done, 1)
                dve.wait_ge(x1_done, c + 1)

            def route_norm(l, c):
                if l == 1 and c >= 2:
                    dve.wait_ge(rt[l]["xT"], c - 1)
                norm(c, slots(l, c), rt[l]["xn"])

            def route_choose(l, c):
                t = tiles(c)
                L = lg[:, t, :]
                a_, b_ = rtmp[:, 0, :, :], rtmp[:, 1, :, :]
                rv = bc(rev[:], 1, CT_TILES)
                lp = PS[:, BANK_LG[l], 0:CT_TILES * E].rearrange("p (s e) -> p s e", e=E)
                dve.wait_ge(rt[l]["logits"], c + 1)
                if l == 0:
                    tt(L, lp, bc(brb[:], 1, CT_TILES), ALU.add).then_inc(rt[l]["lg"], 1)
                else:
                    v_.tensor_copy(L, lp).then_inc(rt[l]["lg"], 1)
                dve.wait_ge(rt[l]["lg"], c + 1)
                link(v_.tensor_reduce(rmax[:, 0, t], L, AX, ALU.max))
                link(tt(a_, L, bc(rmax[:, 0, t], 2, E), ALU.is_equal))
                link(tt(a_, a_, rv, ALU.mult))
                link(v_.tensor_reduce(rmax[:, 1, t], a_, AX, ALU.max))
                link(tt(oh[0][:, t, :], a_, bc(rmax[:, 1, t], 2, E), ALU.is_equal))
                link(v_.scalar_tensor_tensor(out=b_, in0=oh[0][:, t, :], scalar=-BIG, in1=L, op0=ALU.mult, op1=ALU.add))
                link(v_.tensor_reduce(rmax[:, 2, t], b_, AX, ALU.max))
                tt(wdif[:, t], rmax[:, 2, t], rmax[:, 0, t], ALU.subtract).then_inc(rt[l]["gap"], 1)
                link(tt(a_, b_, bc(rmax[:, 2, t], 2, E), ALU.is_equal))
                link(tt(a_, a_, rv, ALU.mult))
                link(v_.tensor_reduce(rmax[:, 3, t], a_, AX, ALU.max))
                link(tt(oh[1][:, t, :], a_, bc(rmax[:, 3, t], 2, E), ALU.is_equal))
                tt(sel16[:, t, :], oh[0][:, t, :], oh[1][:, t, :], ALU.add).then_inc(rt[l]["mask"], 1)

            def route_rows(l, c):
                t, u = tiles(c), c % 2
                a_, b_ = rtmp[:, 0, :, :], rtmp[:, 1, :, :]
                dve.wait_ge(rt[l]["exp"], c + 1)
                link(v_.tensor_scalar(wden[:, t], wexp[:, t], 1.0, None, ALU.add))
                link(v_.reciprocal(wden[:, t], wden[:, t]))
                g_ = gt[:, 2 + l:3 + l]
                v_.tensor_scalar(wgt[:, t, 0], wden[:, t], g_, None, ALU.mult)
                v_.scalar_tensor_tensor(out=wgt[:, t, 1], in0=wden[:, t], scalar=g_, in1=wexp[:, t], op0=ALU.mult, op1=ALU.mult)
                dve.wait_ge(rt[l]["rank"], c + 1)
                link(tt(a_, PS[:, BANK_RANK[l], 0:CT_TILES * E].rearrange("p (s e) -> p s e", e=E), bc(expert_row[:], 1, CT_TILES), ALU.add))
                for k in range(TOPK):
                    link(tt(b_, oh[k][:, t, :], a_, ALU.mult))
                    link(v_.tensor_reduce(adr[:, t, k], b_, AX, ALU.add))
                v_.tensor_copy(adr_i[:, t, :], adr[:, t, :]).then_inc(rt[l]["ranked"], 1)
                link(v_.tensor_reduce(csum[:], sel16[:, t, :].rearrange("p s e -> p e s"), AX, ALU.add))
                tt(cum16[:], cum16[:], csum[:], ALU.add).then_inc(rt[l]["count"], 1)
                if c >= 2:
                    dve.wait_ge(scat[l][u], 16 * CT_TILES * TOPK * (c // 2))
                xn = XN[:, slots(l, c), :]
                for k in range(TOPK):
                    v_.tensor_copy(pack.bitcast(U32)[:, u, :, k, D:D + 1], id_tok[:, t, k:k + 1])
                link(v_.tensor_copy(pack[:, u, :, 0, 0:D], xn))
                link(tt(pack[:, u, :, 0, D:2 * D], xn, pack[:, u, :, 0, 0:D], ALU.subtract))
                v_.tensor_copy(pack[:, u, :, 1, 0:2 * D], pack[:, u, :, 0, 0:2 * D]).then_inc(rt[l]["packed"], 1)

            def route_table(l):
                nl = SLOTS // P if l == 1 else 2 * TILES[0]
                dve.wait_ge(rt[l]["total"], 1)
                link(v_.tensor_copy(cnt[:], PS[:, BANK_RANK[l], 64:64 + E]))
                if l == 0:
                    link(v_.tensor_scalar(cnt_s[:], cnt[:], float(TILE - 1), None, ALU.add))
                    link(v_.tensor_copy(cnt_i[:], cnt_s[:]))
                    link(v_.tensor_scalar(cnt_i[:], cnt_i[:], 8, 8, ALU.arith_shift_right, ALU.logical_shift_left))
                    link(v_.tensor_copy(cnt_s[:], cnt_i[:]))
                    link(tt(tail_f[:], cnt[:], expert_row[:], ALU.add))
                    v_.tensor_copy(tail_i[:], tail_f[:])
                else:
                    link(v_.tensor_copy(cnt_s[:], cnt[:]))
                link(v_.tensor_tensor_scan(incl[:], onesE[:], cnt_s[:], 0.0, ALU.mult, ALU.add))
                link(v_.tensor_scalar(jump[:], cnt_s[:], -1.0, float(CAP), ALU.mult, ALU.add))
                pos, row, er, B = pos128[:, 0:nl], row_f[:, 0:nl], er_f[:, 0:nl], big1[:, 0:nl, :]

                def count(B, at_, o_er, o_row, m):
                    link(tt(B, bc(incl[:], 1, m), bc(at_, 2, E), ALU.is_le))
                    if o_er is not None:
                        link(v_.tensor_reduce(o_er, B, AX, ALU.add))
                    if o_row is not None:
                        link(tt(B, B, bc(jump[:], 1, m), ALU.mult))
                        link(v_.tensor_reduce(o_row, B, AX, ALU.add))
                        link(tt(o_row, o_row, at_, ALU.add))

                count(B, pos, er, row, nl)
                if l == 0:
                    link(v_.tensor_scalar(fx_f[:, 0, 0:nl], er, float(E - 1), None, ALU.min))
                    v_.tensor_copy(eidx_i[:, 0, :], fx_f[:, 0, 0:nl].rearrange("p (j u) -> p j u", u=2)[:, :, 0])
                else:
                    last, er2, alt = fx_f[:, 0, 0:nl], fx_f[:, 1, 0:nl], fx_f[:, 2, 0:nl]
                    link(v_.tensor_scalar(last, pos, float(P - 1), None, ALU.add))
                    count(B, last, er2, None, nl)
                    link(tt(er2, er2, er, ALU.is_gt))
                    link(v_.tensor_scalar(alt, er, float(P), float(FIX0), ALU.mult, ALU.add))
                    link(tt(alt, alt, row, ALU.subtract))
                    link(tt(alt, alt, er2, ALU.mult))
                    link(tt(row, row, alt, ALU.add))
                    link(v_.tensor_copy(fixp_i[:], incl[:]))
                    link(v_.tensor_scalar(fixp_i[:], fixp_i[:], 7, 7, ALU.arith_shift_right, ALU.logical_shift_left))
                    link(v_.tensor_copy(fixp[:, 0, :], fixp_i[:]))
                    link(v_.tensor_scalar(fixp[:, 1, :], fixp[:, 0, :], float(SLOTS - P), lane[:, 0:1], ALU.min, ALU.add))
                    count(B[:, 0:E, :], fixp[:, 1, :], None, fixp[:, 2, :], E)
                    v_.tensor_copy(fixadr_i[:], fixp[:, 2, :])
                v_.tensor_copy(rows_i[:, 0:nl], row).then_inc(rt[l]["table"], 1)

            for k in range(NC + 3):
                if k < NC:
                    scaled_values(k)
                if 1 <= k <= NC:
                    residual(k - 1)
                    route_norm(0, k - 1)
                if 2 <= k <= NC + 1:
                    route_choose(0, k - 2)
                if 3 <= k <= NC + 2:
                    route_rows(0, k - 3)
                if k < E:
                    split_w1(0, w1raw, k)
            route_table(0)

            def parts_of_projection(c):
                for which in range(2):
                    dve.wait_ge(qk_hi, 2 * c + which + 1)
                    v_.scalar_tensor_tensor(out=qk16[:, which, 1, :], in0=PS[:, 2 + which, :], scalar=QK_SCALE[which],
                                            in1=qk16[:, which, 0, :], op0=ALU.mult, op1=ALU.subtract).then_inc(qk_lo, 1)

            def experts(l):
                f, i0 = ff, before[l]

                def parts(i, q):
                    v, m = q % 2, (i + i0) * (XS_LEAD // 2) + q // 2
                    dve.wait_ge(f["xT"][v], m + 1)
                    wait(dve, f["up"][v], m)
                    v_.tensor_copy(xgT[:, v, :, :].rearrange("p h n -> p (h n)"), PS[:, v, 0:TILE].bitcast(F16))\
                        .then_inc(f["xT_sb"][v], 1)

                def result(i, q):
                    v, m = q % 2, (i + i0) * (XS_LEAD // 2) + q // 2
                    dve.wait_ge(f["y"][v], m + 1)
                    if not (isinstance(i, int) and i + i0 == 0):
                        dve.wait_ge(f["turn"][0], (i + i0 - 1) * XS_LEAD + q + 1)
                        dve.wait_ge(f["stored"][q], (i + i0) * STORED)
                    y = PS[:, 6 + v, 0:2 * D].rearrange("p (u d) -> p u d", u=2)
                    if l == 0:
                        e = dve.value_load(eidx_i[0:1, l, ds(i * XS_LEAD + q, 1)], min_val=0, max_val=E - 1)
                        ins = tt(yrow[:, q, :, :], y, bc(b2b[:, ds(e * D, D)], 1, 2), ALU.add)
                    else:
                        ins = v_.tensor_copy(yrow[:, q, :, :], y)
                    ins.then_inc(f["yrow"][v], 1)

                def round_(i, first, last):
                    for q in range(XS_LEAD):
                        if q < XS_LEAD - 1:
                            parts(i, q + 1)
                        elif not last:
                            parts(i + 1, 0)
                        if q >= 1:
                            result(i, q - 1)
                        elif not first:
                            result(i - 1, XS_LEAD - 1)

                rounds_ = TILES[l] // XS_LEAD
                parts(0, 0)
                round_(0, True, False)
                with dve.Fori(1, rounds_ - 1) as i:
                    round_(i, False, False)
                round_(rounds_ - 1, False, True)
                result(rounds_ - 1, XS_LEAD - 1)
                for c in range(NC):
                    dve.wait_ge(y_in[l][c % 2], 16 * (c // 2 + 1))
                    for k in range(TOPK):
                        for s in range(CT_TILES):
                            T = c * CT_TILES + s
                            ins = v_.scalar_tensor_tensor(out=X[:, T, :], in0=yc[:, c % 2, s, k, :],
                                                          scalar=wgt[:, T, k:k + 1], in1=X[:, T, :],
                                                          op0=ALU.mult, op1=ALU.add)
                        if k == 0:
                            ins.then_inc(x_ffa[l], 1)
                            dve.wait_ge(x_ffa[l], c + 1)
                    ins.then_inc(x_ff[l], 1)

            experts(0)

            dve.wait_ge(w_in, 16 * NW)
            link(v_.tensor_copy(mask_f[:], mask_u8[:]))
            v_.tensor_scalar(mask16[:], mask_f[:], -1.0, -MASKED, ALU.add, ALU.mult)
            link(v_.tensor_scalar(mask_f[:], mask_f[:], -1.0, None, ALU.add))
            v_.tensor_scalar(mask_f[:], mask_f[:], BIG, None, ALU.mult).then_inc(mask_rows, 1)
            v_.tensor_scalar(wo1T, wo1T, gt[:, 1:2], None, ALU.mult)
            link(v_.memset(cum16[:], 0.0))
            link(v_.memset(v9, 0.0))
            for hb in range(2):
                v_.memset(v9[hb * 64:hb * 64 + 64, :, :, :, hb, DH:DH + 1].rearrange("p u s h n -> p (u s h) n"), 1.0)
            for c in range(NC):
                norm(c, tiles(c), xn3)
                if c == 1:
                    v_.memset(qmask, 0.0)
                    v_.memset(kmask[:, 0, :, :, :], 0.0)
                if c >= 1:
                    parts_of_projection(c - 1)
            parts_of_projection(NC - 1)
            v_.memset(q3[96:97, :, :, :], 1.0)
            v_.memset(k3[96:104, :, :, :], 1.0).then_inc(blank, 1)
            for which in range(2):
                dve.wait_ge(qk_out[which], 16 * NC)
            v_.memset(kmask[:, 1, :, :, :], 0.0).then_inc(blank, 1)

            for g in range(G0, G1):
                T = g + LEAD
                if 0 <= T < NT:
                    c, s = T // CT_TILES, T % CT_TILES
                    dve.wait_ge(s_ps, T + 1)
                    v_.tensor_reduce(rmaxq[:, c % 2, s, :], banks(0, 1024).rearrange("p (h k) -> p h k", h=H),
                                     AX, ALU.max).then_inc(s_max, 1)
                    if s == CT_TILES - 1:
                        dve.wait_ge(s_max, T + 1)
                        if c >= 1:
                            dve.wait_ge(nT_ps, c)
                        link(v_.tensor_scalar(nmax.rearrange("p (j r s) -> p s r j", j=HG, r=HG),
                                              rmaxq[:, c % 2, :, :].rearrange("p s (r j) -> p s r j", r=HG),
                                              -1.0, None, ALU.mult))
                        link(v_.tensor_copy(nmax16[:, 0, :], nmax))
                        tt(nmax16[:, 1, :], nmax, nmax16[:, 0, :], ALU.subtract).then_inc(n_ready, 1)
                T = g - 1
                if 0 <= T < NT:
                    o = PS[:, 4, 0:HP * 36].rearrange("p (m h b n) -> p m h b n", m=HP, h=2, b=2)
                    rec = orec.rearrange("p (b m h) -> p b m h", b=2, m=HP)
                    dve.wait_ge(av_ps, T + 1)
                    for b in range(2):
                        ins = v_.reciprocal(rec[:, b, :, :], o[:, :, :, b, DH])
                    ins.then_inc(o_rec, 1)
                    dve.wait_ge(o_rec, T + 1)
                    if T >= 1:
                        dve.wait_ge(oT_ps, T)
                    for b in range(2):
                        ins = tt(onorm[:, b, :].rearrange("p (h m d) -> p m h d", h=2, m=HP), o[:, :, :, b, 0:DH],
                                 bc(rec[:, b, :, :], 3, DH), ALU.mult)
                    ins.then_inc(o_norm, 1)
                T = g - 3
                if 0 <= T < NT:
                    dve.wait_ge(o_ps, T + 1)
                    tt(X[:, T, :], X[:, T, :], PS[:, 6, 0:D], ALU.add).then_inc(x3_done, 1)
                k = chunk_at(g, 6)
                if k is not None:
                    dve.wait_ge(x3_done, CT_TILES * (k + 1))
                    route_norm(1, k)
                k = chunk_at(g, 8)
                if k is not None:
                    route_choose(1, k)
                k = chunk_at(g, 9)
                if k is not None:
                    route_rows(1, k)
                k = chunk_at(g, 3)
                if k is not None:
                    split_w1(1, w1raw1, k)
            route_table(1)
            experts(1)


_OUT = ((NB, SEQ, D), "float32")


def kernel(**inputs):
    import numpy as np
    import concourse.bacc as bacc
    from concourse.bass_utils import run_bass_kernel_spmd

    v = {k: np.ascontiguousarray(a) for k, a in inputs.items()}
    col = lambda a: a.reshape(D, 1)

    def by_group(a):
        z = np.zeros((4, 32), a.dtype)
        z[:, :H] = a
        return z.reshape(P, 1)

    wo = v["L1_xattn_Wo"].T.reshape(HP, 2, DH, D).transpose(1, 0, 2, 3).reshape(D, D)
    arrays = {
        "x": v["x"].reshape(NTOK, D), "ctx": v["ctx_1024"].reshape(NTOK, D),
        "mask": v["mask_Bx1x1xS2_bf1"].reshape(NT, P).view(np.uint8),
        "g": np.concatenate([v["g_xattn"], v["g_ffn"]]).reshape(1, 4),
        "W": np.stack([v["L0_xattn_Wq"], v["L0_xattn_Wq"].T, v["L0_xattn_Wk"], v["L0_xattn_Wk"].T, v["L0_xattn_Wv"],
                       v["L0_xattn_Wt"].T, v["L0_xattn_Wp"], v["L1_xattn_Wq"].T, v["L1_xattn_Wk"].T,
                       v["L1_xattn_Wv"].T, wo]),
        "wa": np.stack([v["L0_xattn_Wqa"], v["L0_xattn_Wka"]]),
        "wr": np.stack([v["L0_ffn_W_router"], v["L1_ffn_router_w"].T]),
        "bcol": np.concatenate([col(v["L0_xattn_" + b]) for b in ("bq", "bk", "bv", "bt")], axis=1),
        "bacol": np.concatenate([by_group(v["L0_xattn_bqa"]), by_group(v["L0_xattn_bka"])], axis=1),
        "bp": v["L0_xattn_bp"].reshape(1, D), "br": v["L0_ffn_b_router"].reshape(1, E),
        "b1": v["L0_ffn_b1"].reshape(E, FC, P).transpose(2, 0, 1).reshape(P, E * FC),
        "b2": v["L0_ffn_b2"].reshape(1, E * D),
        "w1_0": v["L0_ffn_W1"], "w2_0": v["L0_ffn_W2"], "w1_1": v["L1_ffn_w1"], "w2_1": v["L1_ffn_w2"],
    }
    nc = bacc.Bacc("TRN2", target_bir_lowering=False, num_devices=1)
    A, feed = {}, {}
    for name, a in arrays.items():
        a = np.ascontiguousarray(a)
        feed[f"in_{name}"] = a
        A[name] = nc.dram_tensor(f"in_{name}", a.shape, mybir.dt.from_np(a.dtype), kind="ExternalInput").ap()
    out = nc.dram_tensor("out", (NTOK, D), F32, kind="ExternalOutput").ap()
    build(nc, A, out)
    r = run_bass_kernel_spmd(nc, [feed], core_ids=[0])
    return r.results[0]["out"].reshape(_OUT[0])
```

```python
from contextlib import ExitStack

import concourse.bass as bass
from concourse import mybir

ALU = mybir.AluOpType
ACT = mybir.ActivationFunctionType
F32 = mybir.dt.float32
F16 = mybir.dt.float16
U32 = mybir.dt.uint32
I32 = mybir.dt.int32
U8 = mybir.dt.uint8
AX = mybir.AxisListType.X
ds = bass.ds

P = 128
D = 128
SEQ = 64
NB = 64
NTOK = NB * SEQ
NT = NTOK // P
CT_TILES = 4
CHUNK = CT_TILES * P
NC = NTOK // CHUNK
NP = NC // 2
CB = CHUNK // SEQ
H, DH = 16, 8
HP = H // 2
HG = 4
E, FF, TOPK = 8, 512, 2
FC = FF // P
SLOTS = NTOK * TOPK
TILE = 256
CAP = NTOK + TILE
ROW16 = 2 * D + 2
TILES = (SLOTS // TILE + E, SLOTS // TILE)
FIX0 = E * CAP
XS_ROWS = E * CAP + E * TILE
DUMMY = SLOTS
Y_ROWS = SLOTS + 2 * E * TILE
WSCALE = 256.0
EPS = 1e-5
BIG = 3.0e38
QK_PARTS = ((0, 1, 0), (0, 0, 1))
QK_ROWS = 3 * HG * DH
QK_SCALE = (float(DH) ** -0.5, 1.0)
MASKED = -60000.0
STORED = 32
XS_LEAD = 8


def bc(ap, axis, n):
    shape = list(ap.shape)
    shape.insert(axis, n)
    return ap.unsqueeze(axis).broadcast_to(shape)


def build(nc, A, out):
    ctx = ExitStack()
    with ctx:
        def sb(name, shape, dt=F32):
            return ctx.enter_context(nc.sbuf_tensor(name, shape, dt))

        def sem(name):
            return ctx.enter_context(nc.semaphore(name))

        xs = [nc.dram_tensor(f"xs{l}", [XS_ROWS, ROW16], F16).ap() for l in range(2)]
        ys = [nc.dram_tensor(f"ys{l}", [Y_ROWS, D], F32).ap() for l in range(2)]
        qk_dram = [nc.dram_tensor(n, [NC, QK_ROWS, HG, CHUNK], F16).ap() for n in ("q_parts", "k_parts")]
        nmax_dram = nc.dram_tensor("max_rows", [2, HG, HG, HG * CHUNK], F16).ap()
        mask_dram = nc.dram_tensor("mask_row", [NT, P], F16).ap()

        X = sb("X", [P, NT, D])
        XN = sb("XN", [P, NT, D])
        W = sb("W", [P, 11, D])
        wq, wqT, wk, wkT, wv, wtT, wp, wq1T, wk1T, wv1T, wo1T = (W[:, i, :] for i in range(11))
        wa = sb("wa", [P, 2, H])
        wr = sb("wr", [P, 2, E])
        bcol = sb("bcol", [P, 4])
        bacol = sb("bacol", [P, 2])
        bprow = sb("bprow", [1, D])
        brb = sb("brb", [P, E])
        b1 = sb("b1", [P, E * FC])
        g4 = sb("g4", [P, 4])
        gt = sb("gt", [P, 4])
        ident = sb("ident", [P, P])
        ident16 = sb("ident16", [P, P], F16)
        tri16 = sb("tri16", [P, P], F16)
        ones16 = sb("ones16", [P, P], F16)
        onesrow = sb("onesrow", [1, P])
        hmask = sb("hmask", [P, H])
        expert_i = sb("expert_i", [P, E], I32)
        expert_row = sb("expert_row", [P, E])
        rev_i = sb("rev_i", [P, E], I32)
        rev = sb("rev", [P, E])
        id_tok = sb("id_tok", [P, NT, TOPK], U32)
        id_pad = sb("id_pad", [P, 2 * E, 2], U32)
        pos_i = sb("pos_i", [P, 80], I32)
        pos128 = sb("pos128", [P, 80])
        lane_i = sb("lane_i", [P, 1], I32)
        lane = sb("lane", [P, 1])
        eidx_i = sb("eidx_i", [P, 2, TILES[0]], I32)
        stats = sb("stats", [P, NT, 6])
        mv = sb("mv", [P, NT, 2])
        rstd = sb("rstd", [P, NT])
        nwt = sb("nwt", [P, 2, 2 * CT_TILES])
        lg = sb("lg", [P, NT, E])
        rtmp = sb("rtmp", [P, 3, 2 * CT_TILES, E])
        rmax = sb("rmax", [P, 4, NT])
        oh = sb("oh", [P, TOPK, NT, E])
        sel16 = sb("sel16", [P, NT, E], F16)
        cum16 = sb("cum16", [P, E], F16)
        csum = sb("csum", [P, E])
        wdif = sb("wdif", [P, NT])
        wexp = sb("wexp", [P, NT])
        wden = sb("wden", [P, NT])
        wgt = sb("wgt", [P, NT, TOPK])
        adr = sb("adr", [P, TOPK, NT])
        adr_i = sb("adr_i", [P, TOPK, NT], U32)
        pack = sb("pack", [P, 2, CT_TILES, TOPK, ROW16], F16)
        turn = sb("turn", [1, XS_LEAD])
        zrow = sb("zrow", [P, ROW16], F16)
        rxt = sb("rxt", [P, CHUNK])
        cnt = sb("cnt", [P, E])
        cnt_i = sb("cnt_i", [P, E], I32)
        cnt_s = sb("cnt_s", [P, E])
        incl = sb("incl", [P, E])
        jump = sb("jump", [P, E])
        onesE = sb("onesE", [P, E])
        big1 = sb("big1", [P, 80, E])
        row_f = sb("row_f", [P, 80])
        er_f = sb("er_f", [P, 80])
        fx_f = sb("fx_f", [P, 3, 80])
        rows_i = sb("rows_i", [P, 80], I32)
        tail_f = sb("tail_f", [P, E])
        tail_i = sb("tail_i", [P, E], I32)
        fixp = sb("fixp", [P, 4, E])
        fixp_i = sb("fixp_i", [P, E], I32)
        fixadr_i = sb("fixadr_i", [P, E], U32)

        mask_u8 = sb("mask_u8", [NT, P], U8)
        mask_f = sb("mask_f", [NT, P])
        mask16 = sb("mask16", [NT, P], F16)
        mask_bias = sb("mask_bias", [P, NT])

        w1h = sb("w1h", [P, E * FF], F16)
        w1l = sb("w1l", [P, E * FF], F16)
        w2 = sb("w2", [P, E * FF])

        WORK = int(109.5 * 1024)
        work = sb("work", [P, WORK // 4])

        def at(kb, shape, dt=F32):
            size = {F32: 4, U32: 4, F16: 2}[dt]
            n = 1
            for s in shape:
                n *= s
            a = int(kb * 256)
            assert a + n * size // 4 <= WORK // 4, (kb, shape)
            v = work[:, a:a + n * size // 4]
            if dt is not F32:
                v = v.bitcast(dt)
            names = "abcdef"[:len(shape)]
            if len(shape) > 1:
                v = v.rearrange(f"p ({' '.join(names)}) -> p {' '.join(names)}",
                                **{k: s for k, s in zip(names[1:], shape[1:])})
            return v

        ctT = at(52, [NTOK])
        xnT = at(36, [NTOK])
        ctx_tok = at(0, [NT, D])
        sl = at(16, [1024])
        se = at(20, [1024])
        w2blk = at(24, [NT, 2, H])
        xp = at(28, [1024])
        prod = at(32, [1024])
        g32 = at(68, [NB, 32])
        gp = at(76, [NB, H])
        wa32 = at(80, [2, 4, 32])
        wka_bk = at(81, [32])
        wqqa = at(81.25, [32])
        wtp = at(82, [D])
        wqp = at(82.5, [D])
        crow = at(83, [D])
        btq = at(83.5, [2])
        qb = at(83.75, [2])
        kb16 = at(84, [H])
        pq = at(84.25, [NB])
        pkv = at(84.5, [NB])
        smx = at(84.75, [H])
        ssum = at(84.85, [16])
        srec = at(84.95, [16])
        uT = at(85.5, [2, CHUNK])
        w1raw = at(90, [2, FF])
        padt = at(94, [E, 2, ROW16], F16)
        b2b = at(104, [E * D])
        xin = at(0, [XS_LEAD, 2, ROW16], F16)
        xgT = at(8.25, [2, 2, TILE], F16)
        hid = at(10.25, [2, FC, TILE])
        yrow = at(18.5, [XS_LEAD, 2, D])
        yc = at(44, [2, CT_TILES, TOPK, D])
        fixs = at(104, [7, ROW16], F16)
        qmask = at(0, [2, HG, HG, CHUNK], F16)
        kmask = at(77.5, [2, HG, HG, CHUNK], F16)
        p16 = at(40, [2, 2, 1024], F16)
        q3 = at(32, [2, HG, CHUNK], F16)
        k3 = w2[:, 0:3 * HG * CHUNK // 2].bitcast(F16).rearrange("p (u r n) -> p u r n", u=3, r=HG)
        rmaxq = at(48, [2, CT_TILES, H])
        nmax = at(48.5, [CT_TILES * H])
        nmax16 = at(48.75, [2, CT_TILES * H], F16)
        nmaxT = at(49, [P], F16)
        orec = at(49.25, [32])
        onorm = at(49.5, [2, HP * 2 * DH])
        oT = at(50.5, [2, P])
        v9h = at(68, [2, CT_TILES, H, 2, DH + 1], F16)
        v9l = at(72.5, [2, CT_TILES, H, 2, DH + 1], F16)
        xnT1 = at(40, [2, CHUNK])
        qk16 = w1l[:, 0:8 * CHUNK].rearrange("p (u w h n) -> p u w h n", u=2, w=2, h=2)
        w1raw1 = w2[:, 3 * HG * CHUNK // 2:3 * HG * CHUNK // 2 + 2 * FF].rearrange("p (u n) -> p u n", u=2)
        pexp = XN[:, NT // 2:NT, :].rearrange("p (u t) d -> p u (t d)", u=2)

        PS = ctx.enter_context(nc.psum_tensor("PS", [P, 8, 512], F32))
        PF = PS[:, :, :].rearrange("p b n -> p (b n)")

        def banks(b, n):
            return PF[:, b * 512:b * 512 + n]

        w_in = sem("w_in")
        x_in = [sem(f"x_in{c}") for c in range(NC)]
        pool_step = sem("pool_step")
        consts = sem("consts")
        dve_step = sem("dve_step")
        fold_ps, fold_sb = sem("fold_ps"), sem("fold_sb")
        xn_done = sem("xn_done")
        xt_ps, xt_done = sem("xt_ps"), sem("xt_done")
        c_ps, c_done = sem("c_ps"), sem("c_done")
        soft = {k: sem(f"soft_{k}") for k in ("logits", "shifted", "exp", "weights", "wT", "blocks", "pooled",
                                              "pooled_sb", "projected", "head_prod")}
        gsem = {k: sem(f"g_{k}") for k in ("moving", "ps", "sb")}
        v_ps, u_done = sem("v_ps"), sem("u_done")
        att_ps, x1_done = sem("att_ps"), sem("x1_done")
        gates = sem("gates")
        fold_in = sem("fold_in")
        rt = [{k: sem(f"r{l}_{k}") for k in ("xn", "xT", "xT_sb", "logits", "lg", "mask", "rank",
                                             "rank_read", "ranked", "count", "packed")} for l in range(2)]
        total, table, gap, gap_exp = (sem(f"r_{k}") for k in ("total", "table", "gap", "exp"))
        scat = [[sem(f"scat{l}_{u}") for u in range(2)] for l in range(2)]
        tails = sem("tails")
        zero, filled = sem("zero"), sem("filled")
        spare = sem("spare")
        fix_read, fix_kept = sem("fix_read"), sem("fix_kept")
        w1_in = [[sem(f"w1_in{l}_{u}") for u in range(2)] for l in range(2)]
        w2_in = [sem(f"w2_in{l}") for l in range(2)]
        w1_lo = [sem(f"w1_lo{l}") for l in range(2)]
        ff = {k: [sem(f"f_{k}{u}") for u in range(n)] for k, n in
              (("xin", XS_LEAD), ("xT", 2), ("xT_sb", 2), ("up", 2), ("hid", 2), ("y", 2), ("yrow", 2), ("turn", 1),
               ("stored", XS_LEAD))}
        rounds = [TILES[l] // XS_LEAD for l in range(2)]
        before = [0, rounds[0]]
        y_in = [sem(f"y_in{u}") for u in range(2)]
        x_ff = [sem(f"x_ff{l}") for l in range(2)]
        xn3, x3t_ps, x3t_sb = sem("xn3"), sem("x3t_ps"), sem("x3t_sb")
        qk_ps, qk_hi, qk_lo = sem("qk_ps"), sem("qk_hi"), sem("qk_lo")
        qk_out = [sem(f"qk_out{u}") for u in range(2)]
        mask_rows, mask_T, mask_sb, mask_out = (sem(f"mask_{k}") for k in ("rows", "T", "sb", "out"))
        blank = sem("blank")
        qk_in = [sem(f"qk_in{u}") for u in range(2)]
        qm_in = [sem(f"qm_in{u}") for u in range(2)]
        q_blank, k_blank = sem("q_blank"), sem("k_blank")
        n_out = sem("n_out")
        n_in = sem("n_in")
        v9_ps, v9_sb, v9_lo = sem("v9_ps"), sem("v9_sb"), sem("v9_lo")
        s_ps, s_max = sem("s_ps"), sem("s_max")
        n_ready, nT_ps, nT_sb = sem("n_ready"), sem("nT_ps"), sem("nT_sb")
        st_ps, p_done, p_hi, p_lo = sem("st_ps"), sem("p_done"), sem("p_hi"), sem("p_lo")
        av_ps, o_norm = sem("av_ps"), sem("o_norm")
        oT_ps, oT_sb, o_ps, x3_done = sem("oT_ps"), sem("oT_sb"), sem("o_ps"), sem("x3_done")
        stored = sem("stored")

        block = ctx.enter_context(nc.Block())

        def wait(engine, s, value):
            if not (isinstance(value, int) and value == 0):
                engine.wait_ge(s, value)

        def expert_tiles(engine, l, step):
            for q in range(XS_LEAD):
                step(0, q)
            with engine.Fori(1, TILES[l] // XS_LEAD) as i:
                for q in range(XS_LEAD):
                    step(i, q)

        def tiles(c):
            return slice(c * CT_TILES, (c + 1) * CT_TILES)

        def cols(c):
            return slice(c * CHUNK, (c + 1) * CHUNK)

        def pair(p):
            return slice(2 * p * CT_TILES, (2 * p + 2) * CT_TILES)

        def slots(l, c):
            return tiles(c if l == 0 else c % 4)

        NW = 12
        QK_STORES = 6 * 16
        QK_LOADS = 3 + HG
        LEAD = 6
        G0, G1 = -LEAD - 2, NT + 12
        BANK_XT, BANK_LG, BANK_RANK = (2, 7), (3, 7), (6, 7)
        BANK_Q, BANK_K = (2, 5), (3, 6)
        LG0, RANK0, TOTAL0 = 256, 320, 384

        def chunk_at(g, lead):
            k, rest = divmod(g - lead, CT_TILES)
            return k if rest == 0 and 0 <= k < NC else None

        def pair_at(g, lead):
            k, rest = divmod(g - lead, 2 * CT_TILES)
            return k if rest == 0 and 0 <= k < NP else None

        @block.gpsimd
        def _(pool):
            n = [0]

            def then(ins):
                n[0] += 1
                ins.then_inc(pool_step, 1)
                pool.wait_ge(pool_step, n[0])

            g = nc.gpsimd
            g.memset(ident[:], 0.0)
            g.memset(ident16[:], 0.0)
            g.memset(tri16[:], 1.0)
            g.memset(ones16[:], 1.0)
            g.memset(onesrow[:], 1.0)
            g.memset(onesE[:], 1.0)
            g.memset(cum16[:], 0.0)
            g.memset(w2blk, 0.0)
            g.memset(g32, 0.0)
            g.memset(wa32, 0.0)
            g.memset(wqqa, 0.0)
            g.memset(padt, 0.0)
            g.memset(zrow[:], 0.0).then_inc(zero, 1)
            then(g.memset(hmask[:], 1.0))
            for t in (ident, ident16):
                g.affine_select(out=t[:], in_=t[:], compare_op=ALU.not_equal, fill=1.0, base=0,
                                pattern=[[-1, P]], channel_multiplier=1)
            g.affine_select(out=tri16[:], in_=tri16[:], compare_op=ALU.is_gt, fill=0.0, base=0,
                            pattern=[[1, P]], channel_multiplier=-1)
            then(g.affine_select(out=hmask[:], in_=hmask[:], compare_op=ALU.is_ge, fill=0.0, base=0,
                                 pattern=[[-DH, H]], channel_multiplier=1))
            g.affine_select(out=hmask[:], in_=hmask[:], compare_op=ALU.is_ge, fill=0.0, base=DH - 1,
                            pattern=[[DH, H]], channel_multiplier=-1)
            g.iota(expert_i[:], [[CAP, E]], base=0, channel_multiplier=0)
            g.iota(rev_i[:], [[-1, E]], base=E, channel_multiplier=0)
            g.iota(id_tok[:], [[TOPK * P, NT], [1, TOPK]], base=0, channel_multiplier=TOPK)
            g.iota(id_pad[:], [[TILE, 2 * E], [P, 2]], base=DUMMY, channel_multiplier=1)
            g.iota(pos_i[:], [[P, 80]], base=0, channel_multiplier=0)
            g.iota(lane_i[:], [[1, 1]], base=0, channel_multiplier=1)
            then(g.iota(eidx_i[:, 1, 0:TILES[1]], [[1, E], [0, TILES[1] // E]], base=0, channel_multiplier=0))
            g.tensor_copy(expert_row[:], expert_i[:])
            g.tensor_copy(rev[:], rev_i[:])
            g.tensor_copy(pos128[:], pos_i[:])
            g.tensor_copy(lane[:], lane_i[:]).then_inc(consts, 1)
            pid = padt.bitcast(U32)
            g.tensor_copy(pid[:, :, :, D:D + 1], id_pad[:, E:2 * E, :].unsqueeze(3)).then_inc(consts, 1)
            pool.wait_ge(consts, 2)
            g.dma_start(xs[0][FIX0:FIX0 + E * TILE, :].rearrange("(s u p) n -> p s u n", u=2, p=P),
                        padt).then_inc(spare, 16)
            pool.wait_ge(spare, 16)
            g.tensor_copy(pid[:, :, :, D:D + 1], id_pad[:, 0:E, :].unsqueeze(3)).then_inc(consts, 1)

            def scatter(l, c, parts=range(CT_TILES)):
                pool.wait_ge(rt[l]["packed"], c + 1)
                pool.wait_ge(rt[l]["ranked"], c // 2 + 1)
                for s in parts:
                    for k in range(TOPK):
                        T = c * CT_TILES + s
                        g.indirect_dma_start(xs[l], bass.IndirectOffsetOnAxis(adr_i[:, k, T:T + 1], 0),
                                             pack[:, c % 2, s, k, :], None).then_inc(scat[l][c % 2], 16)

            def experts(l):
                def step(i, q):
                    pool.wait_ge(ff["yrow"][q % 2], (i + before[l]) * (XS_LEAD // 2) + q // 2 + 1)
                    g.tensor_tensor(turn[:, q:q + 1], lane[0:1, :], lane[0:1, :], ALU.mult).then_inc(ff["turn"][0], 1)
                    for u in range(2):
                        g.indirect_dma_start(
                            ys[l], bass.IndirectOffsetOnAxis(xin[:, q, u, :].bitcast(U32)[:, D:D + 1], 0),
                            yrow[:, q, u, :], None).then_inc(ff["stored"][q], 16)

                expert_tiles(pool, l, step)

            for c in range(NC):
                scatter(0, c)
            experts(0)
            g.memset(kmask[:, 0, :, :, :], 0.0).then_inc(k_blank, 1)
            pool.wait_ge(x_ff[0], 1)
            g.memset(qmask[:, 0, :, :, :], 0.0).then_inc(q_blank, 1)
            g.memset(kmask[:, 1, :, :, :], 0.0).then_inc(k_blank, 1)
            g.memset(qmask[:, 1, :, :, :], 0.0).then_inc(q_blank, 1)
            pool.wait_ge(filled, 16 * (E + 1))
            for step in range(NT + 19):
                if step < NT:
                    pool.wait_ge(p_hi, step + 1)
                    if step >= 2:
                        pool.wait_ge(av_ps, step - 1)
                    g.tensor_tensor(p16[:, step % 2, 1, :], pexp[:, step % 2, :], p16[:, step % 2, 0, :],
                                    ALU.subtract).then_inc(p_lo, 1)
                p_, rest = divmod(step - 19, 2 * CT_TILES)
                if 0 <= p_ < NP:
                    scatter(1, 2 * p_ + rest // CT_TILES, (rest % CT_TILES,))
            pool.wait_ge(table, 2)
            for u in range(2):
                pool.wait_ge(scat[1][u], 16 * CT_TILES * TOPK * (NC // 2))
            for q in range(E - 1):
                g.indirect_dma_start(fixs[:, q, :], None, xs[1][0:FIX0, :],
                                     bass.IndirectOffsetOnAxis(fixadr_i[:, q:q + 1], 0)).then_inc(fix_read, 16)
            experts(1)

        def load_rows(sp, l, i_tile, q):
            for u in range(2):
                r = sp.value_load(rows_i[0:1, ds(i_tile * 2 + u, 1)], min_val=0, max_val=XS_ROWS - P)
                sp.dma_start(xin[:, q, u, :], xs[l][ds(r, P), :]).then_inc(ff["xin"][q], 16)

        def y_rows(l, c):
            return ys[l][c * CHUNK * TOPK:(c + 1) * CHUNK * TOPK, :].rearrange("(s p k) d -> p s (k d)", p=P, k=TOPK)

        x_rows = A["x"].rearrange("(t p) d -> p t d", p=P)
        c_rows = A["ctx"].rearrange("(t p) d -> p t d", p=P)
        out_rows = out.rearrange("(t p) d -> p t d", p=P)

        @block.sync
        def _(sp):
            for c in range(NC):
                t = slice(c * CT_TILES, (c + 1) * CT_TILES)
                sp.dma_start(X[:, t, :], x_rows[:, t, :]).then_inc(x_in[c], 16)
                if c == 0:
                    sp.dma_start(W[:], A["W"].rearrange("w i o -> i w o")).then_inc(w_in, 16)
                    sp.dma_start(wa[:], A["wa"].rearrange("w i o -> i w o")).then_inc(w_in, 16)
                    sp.dma_start(wr[:], A["wr"].rearrange("w i o -> i w o")).then_inc(w_in, 16)
                    sp.dma_start(bcol[:], A["bcol"]).then_inc(w_in, 16)
                    sp.dma_start(bacol[:], A["bacol"]).then_inc(w_in, 16)
                    sp.dma_start(bprow[:], A["bp"]).then_inc(w_in, 16)
                    sp.dma_start(brb[:], A["br"].partition_broadcast(P)).then_inc(w_in, 16)
                    sp.dma_start(b1[:], A["b1"]).then_inc(w_in, 16)
                    sp.dma_start(b2b, A["b2"].partition_broadcast(P)).then_inc(w_in, 16)
                    sp.dma_start(g4[:], A["g"].partition_broadcast(P)).then_inc(w_in, 16)
                    sp.dma_start(mask_u8[:], A["mask"]).then_inc(w_in, 16)
                    sp.dma_start(w2[:].rearrange("p (e c d) -> p e c d", e=E, c=FC),
                                 A["w2_0"].rearrange("e (c p) d -> p e c d", p=P)).then_inc(w_in, 16)
                sp.dma_start(ctx_tok[:, t, :], c_rows[:, t, :]).then_inc(x_in[c], 16)

            def w1_loads(l, raw):
                for e in range(E):
                    if e >= 2:
                        sp.wait_ge(w1_lo[l], e - 1)
                    sp.dma_start(raw[:, e % 2, :], A[f"w1_{l}"][e]).then_inc(w1_in[l][e % 2], 16)

            sp.wait_ge(zero, 1)
            for e in range(E):
                sp.dma_start(xs[1][e * CAP:(e + 1) * CAP, :].rearrange("(p m) n -> p m n", p=P),
                             bc(zrow[:], 1, CAP // P)).then_inc(filled, 16)
            sp.dma_start(nmax_dram.rearrange("t j b n -> (t j b n)").rearrange("(p m n) -> p m n", p=P, m=2),
                         bc(zrow[:, 0:D * 2], 1, 2)).then_inc(filled, 16)
            w1_loads(0, w1raw)

            sp.wait_ge(table, 1)
            sp.wait_ge(consts, 3)
            for e in range(E):
                r = sp.value_load(tail_i[0:1, e:e + 1], min_val=0, max_val=XS_ROWS - TILE)
                sp.dma_start(xs[0][ds(r, TILE), :].rearrange("(u p) n -> p u n", p=P), padt[:, e, :, :]).then_inc(tails, 16)
            sp.wait_ge(tails, 16 * E)
            sp.wait_ge(spare, 16)
            for u in range(2):
                sp.wait_ge(scat[0][u], 16 * CT_TILES * TOPK * (NC // 2))

            def experts(l):
                def step(i, q):
                    wait(sp, ff["stored"][q], (i + before[l]) * STORED)
                    load_rows(sp, l, i * XS_LEAD + q, q)

                expert_tiles(sp, l, step)
                for q in range(XS_LEAD):
                    sp.wait_ge(ff["stored"][q], STORED * (before[l] + rounds[l]))

            def y_load(l, c):
                if c >= 2:
                    sp.wait_ge(x_ff[l], c - 1)
                sp.dma_start(yc[:, c % 2, :, :, :].rearrange("p s k d -> p s (k d)"), y_rows(l, c)).then_inc(y_in[c % 2], 16)

            def store(c):
                sp.wait_ge(x_ff[1], c + 1)
                t = slice(c * CT_TILES, (c + 1) * CT_TILES)
                sp.dma_start(out_rows[:, t, :], X[:, t, :]).then_inc(stored, 16)

            experts(0)
            y_load(0, 0)
            y_load(0, 1)

            sp.wait_ge(mask_rows, 1)
            sp.dma_start(mask_dram, mask16[:]).then_inc(mask_out, 16)
            def blocks(dst, which, c, s_):
                for j in range(HG):
                    sp.dma_start(dst[j:QK_ROWS:HG, c % 2, j, :, :], qk_dram[which][c, j:QK_ROWS:HG]).then_inc(s_, 16)

            def load(c):
                u = c % 2
                sp.wait_ge(k_blank, u + 1)
                if c >= 2:
                    sp.wait_ge(s_ps, CT_TILES * (c - 1))
                if c >= 3:
                    sp.wait_ge(st_ps, CT_TILES * (c - 2))
                sp.dma_start(k3[0:QK_ROWS, c % 3, :, :], qk_dram[1][c]).then_inc(qk_in[u], 16)
                sp.dma_start(q3[0:QK_ROWS, u, :, :], qk_dram[0][c]).then_inc(qk_in[u], 16)
                blocks(kmask, 1, c, qk_in[u])
                row = mask_dram[tiles(c), :].rearrange("s p -> (s p)").unsqueeze(0).unsqueeze(1)
                sp.dma_start(kmask[96:97, u, :, :, :].rearrange("o j r n -> o (j r) n"),
                             row.broadcast_to([1, H, CHUNK])).then_inc(qk_in[u], 16)

            def load_blocks(c):
                sp.wait_ge(q_blank, c % 2 + 1)
                if c >= 2:
                    sp.wait_ge(st_ps, CT_TILES * (c - 1))
                blocks(qmask, 0, c, qm_in[c % 2])

            def load_max(c):
                sp.wait_ge(nT_sb, c + 1)
                if c >= 1:
                    sp.wait_ge(n_in, 16 * c)
                for term in range(2):
                    diag = nmax_dram[term].rearrange("j b n -> (j b) n")[0:HG * HG:HG + 1, :]
                    sp.dma_start(diag, nmaxT[64 * term:64 * term + 64, :]).then_inc(n_out, 16)
                if c >= 2:
                    sp.wait_ge(st_ps, CT_TILES * (c - 1))
                sp.wait_ge(n_out, 32 * (c + 1))
                sp.dma_start(qmask[96:104, c % 2, :, :, :].rearrange("p j r n -> p j (r n)"),
                             nmax_dram.rearrange("t j b n -> (t j) b n")).then_inc(n_in, 16)

            def w1_load(e):
                if e >= 2:
                    sp.wait_ge(w1_lo[1], e - 1)
                sp.dma_start(w1raw1[:, e % 2, :], A["w1_1"][e]).then_inc(w1_in[1][e % 2], 16)

            for c in range(NC):
                if c == 0:
                    for ahead in (2, 3, 4, 5):
                        y_load(0, ahead)
                elif c % 2 == 0 and c + 5 < NC:
                    y_load(0, c + 4)
                    y_load(0, c + 5)
                for n, which in enumerate((1, 0)):
                    sp.wait_ge(qk_lo, 2 * c + n + 1)
                    for third, part in enumerate(QK_PARTS[which]):
                        rows = qk_dram[which][c, third * 32:(third + 1) * 32]
                        sp.dma_start(rows.rearrange("i r n -> r i n"), qk16[:, c % 2, which, part, :])\
                            .then_inc(qk_out[c % 2], 16)
                if c in (4, 5):
                    sp.wait_ge(qk_out[c % 2], QK_STORES * 3)
                    if c == 4:
                        sp.wait_ge(blank, 1)
                        sp.wait_ge(mask_out, 16)
                    load(c - 4)
            for u in range(2):
                sp.wait_ge(qk_out[u], QK_STORES * NC // 2)
            for c in range(NC):
                load_blocks(c)
                load_max(c)
                if c + 2 < NC:
                    load(c + 2)
                w1_load(c)
            sp.wait_ge(st_ps, NT)
            sp.wait_ge(w1_lo[1], E)
            sp.dma_start(w2[:].rearrange("p (e c d) -> p e c d", e=E, c=FC),
                         A["w2_1"].rearrange("e (c p) d -> p e c d", p=P)).then_inc(w2_in[1], 16)
            sp.wait_ge(table, 2)
            sp.wait_ge(fix_read, 16 * (E - 1))
            sp.dma_start(xs[1][FIX0:FIX0 + (E - 1) * P, :].rearrange("(q p) n -> p q n", p=P), fixs).then_inc(fix_kept, 16)
            sp.wait_ge(fix_kept, 16)
            for u in range(2):
                sp.wait_ge(scat[1][u], 16 * CT_TILES * TOPK * (NC // 2))
            experts(1)
            for c in range(NC):
                y_load(1, c)
                if c >= 1:
                    store(c - 1)
            store(NC - 1)
            sp.wait_ge(stored, 16 * NC)

        @block.tensor
        def _(pe):
            t = nc.tensor

            def mm(o, lhsT, rhs, start=True, stop=True):
                return t.matmul(o, lhsT, rhs, start=start, stop=stop, skip_group_check=True)

            pe.wait_ge(w_in, 16 * NW)
            pe.wait_ge(consts, 1)
            pe.wait_ge(fold_in, 2)
            mm(PS[:, 4, 0:H], wqT, wa[:, 0, :])
            mm(PS[:, 4, D:2 * D], wtT, wp)
            mm(PS[:, 4, 2 * D:3 * D], wqT, wp)
            mm(PS[0:1, 5, 0:D], btq[:, 0:1], wp)
            mm(PS[:, 5, D:D + 1], wa32[:, 0, :, :].rearrange("p j h -> p (j h)"), bcol[:, 0:1]).then_inc(fold_ps, 1)

            def q_logits(c):
                pe.wait_ge(xt_done, c + 1)
                pe.wait_ge(fold_sb, 1)
                j = 32 * (c % 4)
                mm(PS[j:j + 32, 6 + c // 4, :], wqqa, xnT[:, cols(c)]).then_inc(soft["logits"], 1)

            for c in range(NC):
                pe.wait_ge(xn_done, c + 1)
                if c >= 2:
                    pe.wait_ge(xt_done, c - 1)
                for s in range(CT_TILES):
                    ins = t.transpose(PS[:, c % 2, s * P:(s + 1) * P], XN[:, c * CT_TILES + s, :], ident[:])
                ins.then_inc(xt_ps, 1)
                pe.wait_ge(x_in[c], 32)
                if c >= 2:
                    pe.wait_ge(c_done, c - 1)
                for s in range(CT_TILES):
                    ins = t.transpose(PS[:, 2 + c % 2, s * P:(s + 1) * P], ctx_tok[:, c * CT_TILES + s, :], ident[:])
                ins.then_inc(c_ps, 1)
                if c >= 1:
                    q_logits(c - 1)
            q_logits(NC - 1)

            def pooled(r, src, w):
                pe.wait_ge(soft["weights"], r + 1)
                for i in range(8):
                    ins = t.transpose(PS[:, i // 4, (i % 4) * P:(i % 4 + 1) * P], se[:, i * P:(i + 1) * P], ident[:])
                ins.then_inc(soft["wT"], 1)
                pe.wait_ge(soft["blocks"], r + 1)
                for T in range(NT):
                    ins = mm(PF[:, 1024 + T * 32:1024 + (T + 1) * 32], src[:, T, :],
                             w2blk[:, T, :, :].rearrange("p b h -> p (b h)"))
                ins.then_inc(soft["pooled"], 1)
                pe.wait_ge(soft["pooled_sb"], r + 1)
                for i in range(2):
                    ins = mm(PS[:, 4 + i, :], w, xp[:, i * 512:(i + 1) * 512])
                ins.then_inc(soft["projected"], 1)

            pe.wait_ge(c_done, NC)
            pooled(0, XN, wq)
            pe.wait_ge(gsem["moving"], 1)
            for i in range(2):
                mm(PS[:, 2 + i, :], wkT, gp.rearrange("p b h -> p (b h)")[:, i * 512:(i + 1) * 512])
            pqv = pq.rearrange("p (a j b) -> p a j b", a=2, j=4)
            for j in range(4):
                ins = mm(PS[32 * j:32 * j + 32, 0, 0:16], wka_bk, pqv[:, :, j, :])
            ins.then_inc(gsem["ps"], 1)
            pe.wait_ge(gsem["sb"], 1)
            for b in range(NB):
                c, bb = b // CB, b % CB
                j = 32 * (c % 4)
                ins = mm(PS[j:j + 32, 6 + c // 4, bb * SEQ:(bb + 1) * SEQ], g32[:, b, :], ctT[:, b * SEQ:(b + 1) * SEQ])
            ins.then_inc(soft["logits"], 1)
            pooled(1, ctx_tok, wk)

            def values(c):
                pe.wait_ge(*((u_done, c - 1) if c >= 2 else (soft["head_prod"], 2)))
                mm(PS[:, 4 + c % 2, :], wv, ctT[:, cols(c)]).then_inc(v_ps, 1)

            def attended(c):
                pe.wait_ge(u_done, c + 1)
                if c >= 2:
                    pe.wait_ge(x1_done, c - 1)
                for s in range(CT_TILES):
                    o = PS[:, c % 2, s * D:(s + 1) * D]
                    T = c * CT_TILES + s
                    mm(o, uT[:, c % 2, s * P:(s + 1) * P], wtp, stop=False)
                    mm(o, xnT[:, T * P:(T + 1) * P], wqp, start=False, stop=False)
                    ins = mm(o, onesrow[:], crow[0:1, :], start=False)
                ins.then_inc(att_ps, 1)

            def route_transposed(l, c):
                pe.wait_ge(rt[l]["xn"], c + 1)
                if c >= 1:
                    pe.wait_ge(rt[l]["xT_sb"], c)
                for s in range(CT_TILES):
                    ins = t.transpose(PS[:, BANK_XT[l], s * P:(s + 1) * P], XN[:, slots(l, c).start + s, :], ident[:])
                ins.then_inc(rt[l]["xT"], 1)

            def route_logits(l, c):
                pe.wait_ge(rt[l]["xT_sb"], c + 1)
                if c >= 1:
                    pe.wait_ge(rt[l]["lg"], c)
                for s in range(CT_TILES):
                    ins = mm(PS[:, BANK_LG[l], LG0 + s * E:LG0 + (s + 1) * E], rxt[:, s * P:(s + 1) * P], wr[:, l, :])
                ins.then_inc(rt[l]["logits"], 1)

            def route_rank(l, p):
                pe.wait_ge(rt[l]["mask"], p + 1)
                if p >= 1:
                    pe.wait_ge(rt[l]["rank_read"], p)
                    pe.wait_ge(rt[l]["count"], p)
                t0 = pair(p).start
                for s in range(2 * CT_TILES):
                    o = PS[:, BANK_RANK[l], RANK0 + s * E:RANK0 + (s + 1) * E]
                    mm(o, ones16[:], cum16[:], stop=False)
                    for b in range(s):
                        mm(o, ones16[:], sel16[:, t0 + b, :], start=False, stop=False)
                    ins = mm(o, tri16[:], sel16[:, t0 + s, :], start=False)
                ins.then_inc(rt[l]["rank"], 1)

            def route_total(l):
                pe.wait_ge(rt[l]["count"], NP)
                mm(PS[:, BANK_RANK[l], TOTAL0:TOTAL0 + E], ones16[:], cum16[:]).then_inc(total, 1)

            for p in range(NP + 1):
                for c in (2 * p, 2 * p + 1):
                    if p < NP:
                        values(c)
                for c in (2 * p, 2 * p + 1):
                    if p < NP:
                        attended(c)
                if p >= 1:
                    route_rank(0, p - 1)
                for c in (2 * p, 2 * p + 1):
                    if p < NP:
                        route_transposed(0, c)
                        route_logits(0, c)
            route_total(0)

            def experts(l):
                f, i0 = ff, before[l]
                pe.wait_ge(w1_lo[l], E)
                if l == 1:
                    pe.wait_ge(w2_in[1], 16)
                pe.wait_ge(table, l + 1)

                def gather(i, q):
                    v, m = q % 2, (i + i0) * (XS_LEAD // 2) + q // 2
                    pe.wait_ge(f["xin"][q], (i + i0) * 32 + 32)
                    wait(pe, f["xT_sb"][v], m)
                    o = PS[:, v, 0:TILE].bitcast(F16).rearrange("p (h u n) -> p h u n", h=2, u=2)
                    for u in range(2):
                        for h in range(2):
                            ins = t.transpose(o[:, h, u, :], xin[:, q, u, h * D:(h + 1) * D], ident16[:])
                    ins.then_inc(f["xT"][v], 1)

                def up(i, q, e):
                    v, m = q % 2, (i + i0) * (XS_LEAD // 2) + q // 2
                    pe.wait_ge(f["xT_sb"][v], m + 1)
                    wait(pe, f["hid"][v], m)
                    for c in range(FC):
                        o = PF[:, (2 + 2 * v) * 512 + c * TILE:(2 + 2 * v) * 512 + (c + 1) * TILE]
                        for k, (w, h) in enumerate(((w1h, 0), (w1h, 1), (w1l, 0))):
                            ins = mm(o, w[:, ds(e * FF + c * P, P)], xgT[:, v, h, :], start=k == 0, stop=k == 2)
                    ins.then_inc(f["up"][v], 1)

                def down(i, q, e):
                    v, m = q % 2, (i + i0) * (XS_LEAD // 2) + q // 2
                    pe.wait_ge(f["hid"][v], m + 1)
                    wait(pe, f["yrow"][v], m)
                    for u in range(2):
                        for c in range(FC):
                            ins = mm(PS[:, 6 + v, u * D:(u + 1) * D], hid[:, v, c, u * P:(u + 1) * P],
                                     w2[:, ds(e * FF + c * D, D)], start=c == 0, stop=c == FC - 1)
                    ins.then_inc(f["y"][v], 1)

                def expert(tile):
                    return pe.value_load(eidx_i[0:1, l, ds(tile, 1)], min_val=0, max_val=E - 1)

                def round_(i, first, last):
                    for q in range(XS_LEAD):
                        if q < XS_LEAD - 1:
                            gather(i, q + 1)
                        elif not last:
                            gather(i + 1, 0)
                        up(i, q, expert(i * XS_LEAD + q))
                        if q >= 1:
                            down(i, q - 1, expert(i * XS_LEAD + q - 1))
                        elif not first:
                            down(i - 1, XS_LEAD - 1, expert(i * XS_LEAD - 1))

                n = TILES[l] // XS_LEAD
                gather(0, 0)
                round_(0, True, False)
                with pe.Fori(1, n - 1) as i:
                    round_(i, False, False)
                round_(n - 1, False, True)
                down(n - 1, XS_LEAD - 1, expert(TILES[l] - 1))

            experts(0)

            pe.wait_ge(mask_rows, 1)
            t.transpose(PS[:, 4, 0:NT], mask_f[:], ident[0:NT, 0:NT]).then_inc(mask_T, 1)
            for c in range(NC):
                pe.wait_ge(xn3, c + 1)
                if c >= 2:
                    pe.wait_ge(x3t_sb, c - 1)
                for s in range(CT_TILES):
                    ins = t.transpose(PS[:, c % 2, s * P:(s + 1) * P], XN[:, c * CT_TILES + s, :], ident[:])
                ins.then_inc(x3t_ps, 1)
                if c >= 2:
                    pe.wait_ge(qk_lo, 2 * (c - 1))
                mm(PS[:, BANK_K[c % 2], :], wk1T, ctT[:, cols(c)]).then_inc(qk_ps, 1)
                pe.wait_ge(x3t_sb, c + 1)
                mm(PS[:, BANK_Q[c % 2], :], wq1T, xnT1[:, c % 2, :]).then_inc(qk_ps, 1)

            def scores(T):
                c, s = T // CT_TILES, T % CT_TILES
                if s == 0:
                    pe.wait_ge(qk_in[c % 2], 16 * QK_LOADS * (c // 2 + 1))
                if T >= 1:
                    pe.wait_ge(s_max, T)
                for b in range(2):
                    q_ = slice(s * P + b * SEQ, s * P + (b + 1) * SEQ)
                    for r in range(HG):
                        ins = mm(PF[b * SEQ:(b + 1) * SEQ, r * 256:(r + 1) * 256], q3[0:97, c % 2, r, q_],
                                 kmask[0:97, c % 2, :, r, q_])
                ins.then_inc(s_ps, 1)

            def scores_by_key(T):
                c, s = T // CT_TILES, T % CT_TILES
                if s == 0:
                    pe.wait_ge(qm_in[c % 2], 16 * HG * (c // 2 + 1))
                    pe.wait_ge(n_in, 16 * (c + 1))
                if T >= 1:
                    pe.wait_ge(p_done, T)
                for b in range(2):
                    q_ = slice(s * P + b * SEQ, s * P + (b + 1) * SEQ)
                    for r in range(HG):
                        ins = mm(PF[b * SEQ:(b + 1) * SEQ, 1024 + r * 256:1024 + (r + 1) * 256],
                                 k3[0:104, c % 3, r, q_], qmask[0:104, c % 2, :, r, q_])
                ins.then_inc(st_ps, 1)

            def weigh(T):
                c, s = T // CT_TILES, T % CT_TILES
                pe.wait_ge(p_lo, T + 1)
                if s == 0:
                    pe.wait_ge(v9_lo, c + 1)
                if T >= 1:
                    pe.wait_ge(o_norm, T)
                for hp in range(HP):
                    for k, (h, v) in enumerate(((0, v9h), (0, v9l), (1, v9h))):
                        ins = mm(PS[:, 4, hp * 36:(hp + 1) * 36], p16[:, T % 2, h, hp * P:(hp + 1) * P],
                                 v[:, c % 2, s, 2 * hp:2 * hp + 2, :, :].rearrange("p h b n -> p (h b n)"),
                                 start=k == 0, stop=k == 2)
                ins.then_inc(av_ps, 1)

            def heads_transposed(T):
                pe.wait_ge(o_norm, T + 1)
                if T >= 1:
                    pe.wait_ge(oT_sb, T)
                for b in range(2):
                    ins = t.transpose(PS[:, 5, b * P:(b + 1) * P], onorm[:, b, :], ident[:])
                ins.then_inc(oT_ps, 1)

            def project_heads(T):
                pe.wait_ge(oT_sb, T + 1)
                if T >= 1:
                    pe.wait_ge(x3_done, T)
                mm(PS[:, 6, 0:D], oT[:, T % 2, :], wo1T).then_inc(o_ps, 1)

            pe.wait_ge(mask_sb, 1)
            for g in range(G0, G1):
                if 0 <= g < NT:
                    scores_by_key(g)
                if 0 <= g + LEAD < NT:
                    scores(g + LEAD)
                if 0 <= g - 2 < NT:
                    weigh(g - 2)
                if 0 <= g - 3 < NT:
                    heads_transposed(g - 3)
                if 0 <= g - 4 < NT:
                    project_heads(g - 4)
                k = pair_at(g, 17)
                if k is not None:
                    route_logits(1, 2 * k + 1)
                k = chunk_at(g, 3 - LEAD)
                if k is not None:
                    pe.wait_ge(n_ready, k + 1)
                    before_lg, before_rank = (g - 17) // 8 + 1, (g - 18) // 8 + 1
                    if before_lg >= 1:
                        pe.wait_ge(rt[1]["lg"], 2 * before_lg)
                    if before_rank >= 1:
                        pe.wait_ge(rt[1]["rank_read"], before_rank)
                    t.transpose(PS[:, 7, 0:P // 2].bitcast(F16), nmax16.rearrange("p k n -> p (k n)"), ident16[:])\
                        .then_inc(nT_ps, 1)
                k = chunk_at(g, -2)
                if k is not None:
                    pe.wait_ge(nT_sb, k + 1)
                    for s in range(CT_TILES):
                        T = k * CT_TILES + s
                        ins = mm(PS[:, 7, s * D:(s + 1) * D], ctT[:, T * P:(T + 1) * P], wv1T)
                    ins.then_inc(v9_ps, 1)
                k = pair_at(g, 18)
                if k is not None:
                    pe.wait_ge(v9_lo, min(2 * k + 6, NC))
                    route_rank(1, k)
                k = pair_at(g, 15)
                if k is not None:
                    pe.wait_ge(v9_lo, min(2 * k + 5, NC))
                    if k >= 1:
                        pe.wait_ge(rt[1]["rank_read"], k)
                    route_transposed(1, 2 * k)
                k = pair_at(g, 16)
                if k is not None:
                    route_logits(1, 2 * k)
                    pe.wait_ge(rt[1]["lg"], 2 * k + 1)
                    route_transposed(1, 2 * k + 1)
            route_total(1)
            experts(1)

        @block.scalar
        def _(act):
            a = nc.scalar
            act.wait_ge(w_in, 16 * NW)
            a.activation(gt[:], g4[:], ACT.Tanh).then_inc(gates, 1)
            for c in range(NC):
                act.wait_ge(xt_ps, c + 1)
                a.activation(xnT[:, cols(c)], PS[:, c % 2, :], ACT.Copy).then_inc(xt_done, 1)
                act.wait_ge(c_ps, c + 1)
                a.activation(ctT[:, cols(c)], PS[:, 2 + c % 2, :], ACT.Copy).then_inc(c_done, 1)

            def soft_steps(r):
                act.wait_ge(soft["shifted"], r + 1)
                a.activation(se, sl, ACT.Exp, scale=float(DH) ** -0.5).then_inc(soft["exp"], 1)
                act.wait_ge(soft["pooled"], r + 1)
                a.activation(xp, banks(2, 1024), ACT.Copy).then_inc(soft["pooled_sb"], 1)

            soft_steps(0)
            act.wait_ge(gsem["ps"], 1)
            act.wait_ge(consts, 1)
            a.activation(g32[:, :, 0:H], banks(2, 1024).rearrange("p (b h) -> p b h", h=H), ACT.Copy).then_inc(gsem["sb"], 1)
            soft_steps(1)

            def route_xT(l, c):
                act.wait_ge(rt[l]["xT"], c + 1)
                if c >= 1:
                    act.wait_ge(rt[l]["logits"], c)
                a.activation(rxt[:], PS[:, BANK_XT[l], :], ACT.Copy).then_inc(rt[l]["xT_sb"], 1)

            def route_exp(l, p):
                act.wait_ge(gap, l * NP + p + 1)
                a.activation(wexp[:, pair(p)], wdif[:, pair(p)], ACT.Exp).then_inc(gap_exp, 1)

            for p in range(NP):
                route_xT(0, 2 * p)
                route_xT(0, 2 * p + 1)
                route_exp(0, p)

            def experts(l):
                f, i0 = ff, before[l]
                act.wait_ge(table, l + 1)
                def step(i, q):
                    v, m = q % 2, (i + i0) * (XS_LEAD // 2) + q // 2
                    act.wait_ge(f["up"][v], m + 1)
                    wait(act, f["y"][v], m)
                    b = 2 + 2 * v
                    if l == 0:
                        e = act.value_load(eidx_i[0:1, l, ds(i * XS_LEAD + q, 1)], min_val=0, max_val=E - 1)
                        for c in range(FC):
                            ins = a.activation(hid[:, v, c, :], PF[:, b * 512 + c * TILE:b * 512 + (c + 1) * TILE],
                                               ACT.Relu, bias=b1[:, ds(e * FC + c, 1)], scale=1 / WSCALE)
                    else:
                        ins = a.activation(hid[:, v, :, :].rearrange("p c n -> p (c n)"), banks(b, 1024),
                                           ACT.Gelu, scale=1 / WSCALE)
                    ins.then_inc(f["hid"][v], 1)

                expert_tiles(act, l, step)

            experts(0)

            act.wait_ge(mask_T, 1)
            a.activation(mask_bias[:], PS[:, 4, 0:NT], ACT.Copy).then_inc(mask_sb, 1)
            for c in range(NC):
                act.wait_ge(x3t_ps, c + 1)
                a.activation(xnT1[:, c % 2, :], PS[:, c % 2, :], ACT.Copy).then_inc(x3t_sb, 1)
                for n, (which, bank) in enumerate(((1, BANK_K), (0, BANK_Q))):
                    act.wait_ge(qk_ps, 2 * c + n + 1)
                    if c >= 2:
                        act.wait_ge(qk_out[c % 2], QK_STORES * (c // 2))
                    a.activation(qk16[:, c % 2, which, 0, :], PS[:, bank[c % 2], :], ACT.Copy, scale=QK_SCALE[which])\
                        .then_inc(qk_hi, 1)

            act.wait_ge(mask_sb, 1)
            for g in range(G0, G1):
                T = g
                if 0 <= T < NT:
                    act.wait_ge(st_ps, T + 1)
                    if T >= 2:
                        act.wait_ge(p_lo, T - 1)
                    a.activation(pexp[:, T % 2, :], banks(2, 1024), ACT.Exp, bias=mask_bias[:, T:T + 1]).then_inc(p_done, 1)
                T = g - 3
                if 0 <= T < NT:
                    act.wait_ge(oT_ps, T + 1)
                    if T >= 2:
                        act.wait_ge(o_ps, T - 1)
                    for h2 in range(2):
                        ph = slice(h2 * 64, h2 * 64 + 64)
                        ins = a.activation(oT[ph, T % 2, :].rearrange("p (b q) -> p b q", b=2),
                                           PS[ph, 5, 0:2 * P].rearrange("p (b h q) -> p b h q", b=2, h=2)[:, :, h2, :],
                                           ACT.Copy)
                    ins.then_inc(oT_sb, 1)
                k = chunk_at(g, 3 - LEAD)
                if k is not None:
                    act.wait_ge(nT_ps, k + 1)
                    if k >= 1:
                        act.wait_ge(n_out, 32 * k)
                    a.activation(nmaxT, PS[:, 7, 0:P // 2].bitcast(F16), ACT.Copy).then_inc(nT_sb, 1)
                k = chunk_at(g, -2)
                if k is not None:
                    act.wait_ge(v9_ps, k + 1)
                    act.wait_ge(blank, 1)
                    if k >= 2:
                        act.wait_ge(av_ps, CT_TILES * (k - 1))
                    for hb in range(2):
                        ph = slice(hb * 64, hb * 64 + 64)
                        ins = a.activation(v9h[ph, k % 2, :, :, hb, 0:DH].rearrange("p s h d -> p (s h) d"),
                                           PS[ph, 7, :].rearrange("p (n d) -> p n d", d=DH), ACT.Copy)
                    ins.then_inc(v9_sb, 1)
                for half in range(2):
                    k = pair_at(g, 15 + half)
                    if k is not None:
                        route_xT(1, 2 * k + half)
                k = pair_at(g, 17)
                if k is not None:
                    route_exp(1, k)
            experts(1)

        @block.vector
        def _(dve):
            n = [0]
            v_ = nc.vector

            def link(ins):
                n[0] += 1
                ins.then_inc(dve_step, 1)
                dve.wait_ge(dve_step, n[0])

            def tt(o, x, y, op):
                return v_.tensor_tensor(o, x, y, op)

            def norm(t, slot, done):
                w = t.stop - t.start
                for T in range(t.start, t.stop):
                    ins = v_.bn_stats(stats[:, T, :], X[:, T, :])
                link(ins)
                for T in range(t.start, t.stop):
                    ins = v_.bn_aggr(mv[:, T, :], stats[:, T, :])
                link(ins)
                x, y, z = nwt[:, 0, 0:w], rstd[:, t], nwt[:, 1, 0:w]
                link(v_.tensor_scalar(x, mv[:, t, 1], EPS, None, ALU.add))
                link(v_.tensor_scalar(z.bitcast(I32), x.bitcast(I32), 1, None, ALU.arith_shift_right))
                link(v_.tensor_scalar(y.bitcast(I32), z.bitcast(I32), -1.0, float(0x5F3759DF), ALU.mult, ALU.add))
                for _ in range(3):
                    link(v_.scalar_tensor_tensor(out=z, in0=y, scalar=-0.5, in1=y, op0=ALU.mult, op1=ALU.mult))
                    link(tt(z, z, x, ALU.mult))
                    link(v_.scalar_tensor_tensor(out=y, in0=z, scalar=1.5, in1=y, op0=ALU.add, op1=ALU.mult))
                for s in range(w):
                    T = t.start + s
                    ins = v_.tensor_scalar(XN[:, slot + s, :], X[:, T, :], mv[:, T, 0:1], rstd[:, T:T + 1],
                                           ALU.subtract, ALU.mult)
                    if s % CT_TILES == CT_TILES - 1:
                        ins.then_inc(done, 1)

            def split_w1(l, raw, e):
                dve.wait_ge(w1_in[l][e % 2], 16 * (e // 2 + 1))
                o = slice(e * FF, (e + 1) * FF)
                link(v_.tensor_scalar(w1h[:, o], raw[:, e % 2, :], WSCALE, None, ALU.mult))
                v_.scalar_tensor_tensor(out=w1l[:, o], in0=raw[:, e % 2, :], scalar=WSCALE, in1=w1h[:, o],
                                        op0=ALU.mult, op1=ALU.subtract).then_inc(w1_lo[l], 1)

            dve.wait_ge(w_in, 16 * NW)
            dve.wait_ge(consts, 1)
            v_.tensor_copy(wa32[:, :, :, 0:H], bc(wa[:], 2, 4)).then_inc(fold_in, 1)
            tt(btq[:, 0:1], bcol[:, 0:1], bcol[:, 3:4], ALU.add).then_inc(fold_in, 1)
            for c in range(NC):
                dve.wait_ge(x_in[c], 32)
                norm(tiles(c), tiles(c).start, xn_done)
                if c == 0:
                    dve.wait_ge(fold_ps, 1)
                    dve.wait_ge(gates, 1)
                    v_.tensor_copy(wqqa[:, 0:H], PS[:, 4, 0:H])
                    v_.tensor_scalar(wtp, PS[:, 4, D:2 * D], gt[:, 0:1], None, ALU.mult)
                    v_.tensor_scalar(wqp, PS[:, 4, 2 * D:3 * D], gt[:, 0:1], None, ALU.mult)
                    link(tt(crow[0:1, :], PS[0:1, 5, 0:D], bprow[:], ALU.add))
                    v_.tensor_scalar(crow[0:1, :], crow[0:1, :], gt[0:1, 0:1], None, ALU.mult)
                    tt(qb[:, 0:1], PS[:, 5, D:D + 1], bacol[:, 0:1], ALU.add).then_inc(fold_sb, 1)

            def softmax(r, groups=16):
                lp = banks(6, 1024)
                g3 = sl.rearrange("p (g l) -> p g l", l=SEQ)
                e3 = se.rearrange("p (g l) -> p g l", l=SEQ)
                dve.wait_ge(soft["logits"], NC + r)
                if r == 0:
                    dve.wait_ge(fold_sb, 1)
                    link(v_.tensor_scalar(sl, lp, qb[:, 0:1], None, ALU.add))
                else:
                    link(tt(g3, lp.rearrange("p (g l) -> p g l", l=SEQ), bc(kb16, 2, SEQ), ALU.add))
                link(v_.tensor_reduce(smx, g3, AX, ALU.max))
                tt(g3, g3, bc(smx, 2, SEQ), ALU.subtract).then_inc(soft["shifted"], 1)
                dve.wait_ge(soft["exp"], r + 1)
                link(v_.tensor_reduce(ssum, e3, AX, ALU.add))
                link(v_.reciprocal(srec, ssum))
                tt(e3, e3, bc(srec, 2, SEQ), ALU.mult).then_inc(soft["weights"], 1)
                dve.wait_ge(soft["wT"], r + 1)
                for hb in range(2):
                    ph = slice(hb * 64, hb * 64 + 64)
                    for a in range(2):
                        o = w2blk.rearrange("p (a j s) b h -> p a s j b h", a=2, j=4)[ph, a, :, :, hb, :]
                        i_ = PS[ph, a, :].rearrange("p (s j h) -> p s j h", s=4, j=4)[:, :, :, 0:H]
                        ins = v_.tensor_copy(o, i_)
                ins.then_inc(soft["blocks"], 1)

            def head_sum(r, dst, bias):
                dve.wait_ge(soft["projected"], r + 1)
                p3 = prod.rearrange("p (b h) -> p b h", h=H)
                link(tt(p3, banks(4, 1024).rearrange("p (b h) -> p b h", h=H), bc(hmask[:], 1, NB), ALU.mult))
                link(v_.tensor_reduce(dst, p3, AX, ALU.add))
                v_.tensor_scalar(dst, dst, bias, None, ALU.add).then_inc(soft["head_prod"], 1)
                dve.wait_ge(soft["head_prod"], r + 1)

            softmax(0)
            head_sum(0, pq, bcol[:, 0:1])
            v_.tensor_scalar(wka_bk, wa32[:, 1, 0, :], bcol[:, 1:2], None, ALU.mult)
            tt(gp, bc(wa[:, 1, :], 1, NB), bc(pq, 2, H), ALU.mult).then_inc(gsem["moving"], 1)
            dve.wait_ge(gsem["ps"], 1)
            link(v_.tensor_scalar(kb16, PS[:, 0, 0:16], bacol[:, 1:2], None, ALU.add))
            softmax(1)
            head_sum(1, pkv, bcol[:, 1:2])

            def scaled_values(c):
                dve.wait_ge(v_ps, c + 1)
                if c >= 2:
                    dve.wait_ge(att_ps, c - 1)
                v_.scalar_tensor_tensor(out=uT[:, c % 2, :].rearrange("p (b l) -> p b l", l=SEQ),
                                        in0=PS[:, 4 + c % 2, :].rearrange("p (b l) -> p b l", l=SEQ),
                                        scalar=bcol[:, 2:3], in1=bc(pkv[:, c * CB:(c + 1) * CB], 2, SEQ),
                                        op0=ALU.add, op1=ALU.mult).then_inc(u_done, 1)

            def residual(c):
                dve.wait_ge(att_ps, c + 1)
                x = X[:, tiles(c), :].rearrange("p s d -> p (s d)")
                tt(x, x, PS[:, c % 2, :], ALU.add).then_inc(x1_done, 1)
                dve.wait_ge(x1_done, c + 1)

            def route_norm(l, p):
                if l == 1 and p >= 2:
                    dve.wait_ge(rt[l]["xT"], 2 * (p - 1))
                norm(pair(p), slots(l, 2 * p).start, rt[l]["xn"])

            def route_lg(l, c):
                t = tiles(c)
                lp = PS[:, BANK_LG[l], LG0:LG0 + CT_TILES * E].rearrange("p (s e) -> p s e", e=E)
                dve.wait_ge(rt[l]["logits"], c + 1)
                if l == 0:
                    tt(lg[:, t, :], lp, bc(brb[:], 1, CT_TILES), ALU.add).then_inc(rt[l]["lg"], 1)
                else:
                    v_.tensor_copy(lg[:, t, :], lp).then_inc(rt[l]["lg"], 1)

            def route_choose(l, p):
                t = pair(p)
                L = lg[:, t, :]
                a_, b_ = rtmp[:, 0, :, :], rtmp[:, 1, :, :]
                rv = bc(rev[:], 1, 2 * CT_TILES)
                dve.wait_ge(rt[l]["lg"], 2 * p + 2)
                link(v_.tensor_reduce(rmax[:, 0, t], L, AX, ALU.max))
                link(tt(a_, L, bc(rmax[:, 0, t], 2, E), ALU.is_equal))
                link(tt(a_, a_, rv, ALU.mult))
                link(v_.tensor_reduce(rmax[:, 1, t], a_, AX, ALU.max))
                link(tt(oh[:, 0, t, :], a_, bc(rmax[:, 1, t], 2, E), ALU.is_equal))
                link(v_.scalar_tensor_tensor(out=b_, in0=oh[:, 0, t, :], scalar=-BIG, in1=L, op0=ALU.mult, op1=ALU.add))
                link(v_.tensor_reduce(rmax[:, 2, t], b_, AX, ALU.max))
                tt(wdif[:, t], rmax[:, 2, t], rmax[:, 0, t], ALU.subtract).then_inc(gap, 1)
                link(tt(a_, b_, bc(rmax[:, 2, t], 2, E), ALU.is_equal))
                link(tt(a_, a_, rv, ALU.mult))
                link(v_.tensor_reduce(rmax[:, 3, t], a_, AX, ALU.max))
                link(tt(oh[:, 1, t, :], a_, bc(rmax[:, 3, t], 2, E), ALU.is_equal))
                tt(sel16[:, t, :], oh[:, 0, t, :], oh[:, 1, t, :], ALU.add).then_inc(rt[l]["mask"], 1)

            def route_rows(l, p):
                t = pair(p)
                a_, b2 = rtmp[:, 0, :, :], rtmp[:, 1:3, :, :]
                dve.wait_ge(rt[l]["rank"], p + 1)
                tt(a_, PS[:, BANK_RANK[l], RANK0:RANK0 + 2 * CT_TILES * E].rearrange("p (s e) -> p s e", e=E),
                   bc(expert_row[:], 1, 2 * CT_TILES), ALU.add).then_inc(rt[l]["rank_read"], 1)
                v_.tensor_reduce(csum[:], sel16[:, t, :].rearrange("p s e -> p e s"), AX, ALU.add)
                dve.wait_ge(rt[l]["rank_read"], p + 1)
                link(tt(b2, oh[:, :, t, :], bc(a_, 1, TOPK), ALU.mult))
                link(v_.tensor_reduce(adr[:, :, t], b2, AX, ALU.add))
                v_.tensor_copy(adr_i[:, :, t], adr[:, :, t]).then_inc(rt[l]["ranked"], 1)
                tt(cum16[:], cum16[:], csum[:], ALU.add).then_inc(rt[l]["count"], 1)

            def route_pack(l, c):
                t, u = tiles(c), c % 2
                if c >= 2:
                    dve.wait_ge(scat[l][u], 16 * CT_TILES * TOPK * (c // 2))
                xn = XN[:, slots(l, c), :]
                v_.tensor_copy(pack.bitcast(U32)[:, u, :, :, D], id_tok[:, t, :])
                link(v_.tensor_copy(pack[:, u, :, 0, 0:D], xn))
                link(tt(pack[:, u, :, 0, D:2 * D], xn, pack[:, u, :, 0, 0:D], ALU.subtract))
                v_.tensor_copy(pack[:, u, :, 1, 0:2 * D], pack[:, u, :, 0, 0:2 * D]).then_inc(rt[l]["packed"], 1)

            def route_weights(l, p):
                t = pair(p)
                dve.wait_ge(gap_exp, l * NP + p + 1)
                link(v_.tensor_scalar(wden[:, t], wexp[:, t], 1.0, None, ALU.add))
                link(v_.reciprocal(wden[:, t], wden[:, t]))
                g_ = gt[:, 2 + l:3 + l]
                v_.tensor_scalar(wgt[:, t, 0], wden[:, t], g_, None, ALU.mult)
                v_.scalar_tensor_tensor(out=wgt[:, t, 1], in0=wden[:, t], scalar=g_, in1=wexp[:, t], op0=ALU.mult, op1=ALU.mult)

            def route_table(l):
                nl = SLOTS // P if l == 1 else 2 * TILES[0]
                dve.wait_ge(total, l + 1)
                link(v_.tensor_copy(cnt[:], PS[:, BANK_RANK[l], TOTAL0:TOTAL0 + E]))
                if l == 0:
                    link(v_.tensor_scalar(cnt_s[:], cnt[:], float(TILE - 1), None, ALU.add))
                    link(v_.tensor_copy(cnt_i[:], cnt_s[:]))
                    link(v_.tensor_scalar(cnt_i[:], cnt_i[:], 8, 8, ALU.arith_shift_right, ALU.logical_shift_left))
                    link(v_.tensor_copy(cnt_s[:], cnt_i[:]))
                    link(tt(tail_f[:], cnt[:], expert_row[:], ALU.add))
                    v_.tensor_copy(tail_i[:], tail_f[:])
                else:
                    link(v_.tensor_copy(cnt_s[:], cnt[:]))
                link(v_.tensor_tensor_scan(incl[:], onesE[:], cnt_s[:], 0.0, ALU.mult, ALU.add))
                link(v_.tensor_scalar(jump[:], cnt_s[:], -1.0, float(CAP), ALU.mult, ALU.add))
                pos, row, er, B = pos128[:, 0:nl], row_f[:, 0:nl], er_f[:, 0:nl], big1[:, 0:nl, :]

                def count(B, at_, o_er, o_row, m):
                    link(tt(B, bc(incl[:], 1, m), bc(at_, 2, E), ALU.is_le))
                    if o_er is not None:
                        link(v_.tensor_reduce(o_er, B, AX, ALU.add))
                    if o_row is not None:
                        link(tt(B, B, bc(jump[:], 1, m), ALU.mult))
                        link(v_.tensor_reduce(o_row, B, AX, ALU.add))
                        link(tt(o_row, o_row, at_, ALU.add))

                count(B, pos, er, row, nl)
                if l == 0:
                    link(v_.tensor_scalar(fx_f[:, 0, 0:nl], er, float(E - 1), None, ALU.min))
                    v_.tensor_copy(eidx_i[:, 0, :], fx_f[:, 0, 0:nl].rearrange("p (j u) -> p j u", u=2)[:, :, 0])
                else:
                    last, er2, alt = fx_f[:, 0, 0:nl], fx_f[:, 1, 0:nl], fx_f[:, 2, 0:nl]
                    link(v_.tensor_scalar(last, pos, float(P - 1), None, ALU.add))
                    count(B, last, er2, None, nl)
                    link(tt(er2, er2, er, ALU.is_gt))
                    link(v_.tensor_scalar(alt, er, float(P), float(FIX0), ALU.mult, ALU.add))
                    link(tt(alt, alt, row, ALU.subtract))
                    link(tt(alt, alt, er2, ALU.mult))
                    link(tt(row, row, alt, ALU.add))
                    link(v_.tensor_copy(fixp_i[:], incl[:]))
                    link(v_.tensor_scalar(fixp_i[:], fixp_i[:], 7, 7, ALU.arith_shift_right, ALU.logical_shift_left))
                    link(v_.tensor_copy(fixp[:, 0, :], fixp_i[:]))
                    link(v_.tensor_scalar(fixp[:, 1, :], fixp[:, 0, :], float(SLOTS - P), lane[:, 0:1], ALU.min, ALU.add))
                    count(B[:, 0:E, :], fixp[:, 1, :], None, fixp[:, 2, :], E)
                    v_.tensor_copy(fixadr_i[:], fixp[:, 2, :])
                v_.tensor_copy(rows_i[:, 0:nl], row).then_inc(table, 1)

            for p in range(NP + 1):
                both = (2 * p, 2 * p + 1)
                for c in both:
                    if p < NP:
                        scaled_values(c)
                if p >= 1:
                    route_choose(0, p - 1)
                for c in both:
                    if p < NP:
                        residual(c)
                        split_w1(0, w1raw, c)
                if p >= 1:
                    route_rows(0, p - 1)
                    for c in (2 * p - 2, 2 * p - 1):
                        route_pack(0, c)
                    route_weights(0, p - 1)
                if p < NP:
                    route_norm(0, p)
                    for c in both:
                        route_lg(0, c)
            route_table(0)

            def parts_of_projection(c):
                for n, (which, bank) in enumerate(((1, BANK_K), (0, BANK_Q))):
                    dve.wait_ge(qk_hi, 2 * c + n + 1)
                    v_.scalar_tensor_tensor(out=qk16[:, c % 2, which, 1, :], in0=PS[:, bank[c % 2], :],
                                            scalar=QK_SCALE[which], in1=qk16[:, c % 2, which, 0, :],
                                            op0=ALU.mult, op1=ALU.subtract).then_inc(qk_lo, 1)

            def experts(l):
                f, i0 = ff, before[l]

                def parts(i, q):
                    v, m = q % 2, (i + i0) * (XS_LEAD // 2) + q // 2
                    dve.wait_ge(f["xT"][v], m + 1)
                    wait(dve, f["up"][v], m)
                    v_.tensor_copy(xgT[:, v, :, :].rearrange("p h n -> p (h n)"), PS[:, v, 0:TILE].bitcast(F16))\
                        .then_inc(f["xT_sb"][v], 1)

                def result(i, q):
                    v, m = q % 2, (i + i0) * (XS_LEAD // 2) + q // 2
                    dve.wait_ge(f["y"][v], m + 1)
                    if not (isinstance(i, int) and i + i0 == 0):
                        dve.wait_ge(f["turn"][0], (i + i0 - 1) * XS_LEAD + q + 1)
                        dve.wait_ge(f["stored"][q], (i + i0) * STORED)
                    y = PS[:, 6 + v, 0:2 * D].rearrange("p (u d) -> p u d", u=2)
                    if l == 0:
                        e = dve.value_load(eidx_i[0:1, l, ds(i * XS_LEAD + q, 1)], min_val=0, max_val=E - 1)
                        ins = tt(yrow[:, q, :, :], y, bc(b2b[:, ds(e * D, D)], 1, 2), ALU.add)
                    else:
                        ins = v_.tensor_copy(yrow[:, q, :, :], y)
                    ins.then_inc(f["yrow"][v], 1)

                def round_(i, first, last):
                    for q in range(XS_LEAD):
                        if q < XS_LEAD - 1:
                            parts(i, q + 1)
                        elif not last:
                            parts(i + 1, 0)
                        if q >= 1:
                            result(i, q - 1)
                        elif not first:
                            result(i - 1, XS_LEAD - 1)

                rounds_ = TILES[l] // XS_LEAD
                parts(0, 0)
                round_(0, True, False)
                with dve.Fori(1, rounds_ - 1) as i:
                    round_(i, False, False)
                round_(rounds_ - 1, False, True)
                result(rounds_ - 1, XS_LEAD - 1)

            def combine(l, c):
                dve.wait_ge(y_in[c % 2], 16 * (l * NC // 2 + c // 2 + 1))
                for k in range(TOPK):
                    for s in range(CT_TILES):
                        T = c * CT_TILES + s
                        ins = v_.scalar_tensor_tensor(out=X[:, T, :], in0=yc[:, c % 2, s, k, :],
                                                      scalar=wgt[:, T, k:k + 1], in1=X[:, T, :],
                                                      op0=ALU.mult, op1=ALU.add)
                    if k == 0:
                        link(ins)
                ins.then_inc(x_ff[l], 1)

            experts(0)

            dve.wait_ge(w_in, 16 * NW)
            link(v_.tensor_copy(mask_f[:], mask_u8[:]))
            v_.tensor_scalar(mask16[:], mask_f[:], -1.0, -MASKED, ALU.add, ALU.mult)
            link(v_.tensor_scalar(mask_f[:], mask_f[:], -1.0, None, ALU.add))
            v_.tensor_scalar(mask_f[:], mask_f[:], BIG, None, ALU.mult).then_inc(mask_rows, 1)
            v_.tensor_scalar(wo1T, wo1T, gt[:, 1:2], None, ALU.mult)
            link(v_.memset(cum16[:], 0.0))
            v_.memset(v9l, 0.0)
            link(v_.memset(v9h, 0.0))
            for hb in range(2):
                v_.memset(v9h[hb * 64:hb * 64 + 64, :, :, :, hb, DH:DH + 1].rearrange("p u s h n -> p (u s h) n"), 1.0)
            for p in range(NP):
                for c in (2 * p, 2 * p + 1):
                    combine(0, c)
                dve.wait_ge(x_ff[0], 2 * p + 2)
                norm(pair(p), pair(p).start, xn3)
                if p == 0:
                    v_.memset(q3[96:97, :, :, :], 1.0)
                    v_.memset(k3[96:104, :, :, :], 1.0).then_inc(blank, 1)
                else:
                    parts_of_projection(2 * p - 2)
                    parts_of_projection(2 * p - 1)
            parts_of_projection(NC - 2)
            parts_of_projection(NC - 1)
            for g in range(G0, G1):
                T = g - 5
                if 0 <= T < NT:
                    dve.wait_ge(o_ps, T + 1)
                    tt(X[:, T, :], X[:, T, :], PS[:, 6, 0:D], ALU.add).then_inc(x3_done, 1)
                T = g - 3
                if 0 <= T < NT:
                    o = PS[:, 4, 0:HP * 36].rearrange("p (m h b n) -> p m h b n", m=HP, h=2, b=2)
                    rec = orec.rearrange("p (m h b) -> p b m h", b=2, m=HP)
                    dve.wait_ge(av_ps, T + 1)
                    link(v_.reciprocal(orec, PS[:, 4, 0:HP * 36].rearrange("p (k n) -> p k n", n=DH + 1)[:, :, DH]))
                    if T >= 1:
                        dve.wait_ge(oT_ps, T)
                    for b in range(2):
                        ins = tt(onorm[:, b, :].rearrange("p (h m d) -> p m h d", h=2, m=HP), o[:, :, :, b, 0:DH],
                                 bc(rec[:, b, :, :], 3, DH), ALU.mult)
                    ins.then_inc(o_norm, 1)
                T = g + LEAD
                if 0 <= T < NT:
                    c, s = T // CT_TILES, T % CT_TILES
                    dve.wait_ge(s_ps, T + 1)
                    v_.tensor_reduce(rmaxq[:, c % 2, s, :], banks(0, 1024).rearrange("p (h k) -> p h k", h=H),
                                     AX, ALU.max).then_inc(s_max, 1)
                    if s == CT_TILES - 1:
                        dve.wait_ge(s_max, T + 1)
                        if c >= 1:
                            dve.wait_ge(nT_ps, c)
                        link(v_.tensor_scalar(nmax.rearrange("p (j r s) -> p s r j", j=HG, r=HG),
                                              rmaxq[:, c % 2, :, :].rearrange("p s (r j) -> p s r j", r=HG),
                                              -1.0, None, ALU.mult))
                        link(v_.tensor_copy(nmax16[:, 0, :], nmax))
                        tt(nmax16[:, 1, :], nmax, nmax16[:, 0, :], ALU.subtract).then_inc(n_ready, 1)
                T = g
                if 0 <= T < NT:
                    dve.wait_ge(p_done, T + 1)
                    if T >= 2:
                        dve.wait_ge(av_ps, T - 1)
                    v_.tensor_copy(p16[:, T % 2, 0, :], pexp[:, T % 2, :]).then_inc(p_hi, 1)
                k = chunk_at(g, -2)
                if k is not None:
                    dve.wait_ge(v9_sb, k + 1)
                    for hb in range(2):
                        ph = slice(hb * 64, hb * 64 + 64)
                        v9 = [v[ph, k % 2, :, :, hb, 0:DH].rearrange("p s h d -> p (s h) d") for v in (v9h, v9l)]
                        ins = tt(v9[1], PS[ph, 7, :].rearrange("p (n d) -> p n d", d=DH), v9[0], ALU.subtract)
                    ins.then_inc(v9_lo, 1)
                k = pair_at(g, 12)
                if k is not None:
                    dve.wait_ge(x3_done, 2 * CT_TILES * (k + 1))
                    route_norm(1, k)
                for half in range(2):
                    k = pair_at(g, 16 + half)
                    if k is not None:
                        route_lg(1, 2 * k + half)
                k = pair_at(g, 17)
                if k is not None:
                    route_choose(1, k)
                k = pair_at(g, 18)
                if k is not None:
                    route_rows(1, k)
                    route_pack(1, 2 * k)
                k = pair_at(g, 19)
                if k is not None:
                    route_pack(1, 2 * k + 1)
                    route_weights(1, k)
                k = chunk_at(g, 3)
                if k == 0:
                    for u in range(2):
                        dve.wait_ge(qk_out[u], QK_STORES * NC // 2)
                if k is not None:
                    split_w1(1, w1raw1, k)
            route_table(1)
            experts(1)
            for c in range(NC):
                combine(1, c)


_OUT = ((NB, SEQ, D), "float32")


def kernel(**inputs):
    import numpy as np
    import concourse.bacc as bacc
    from concourse.bass_utils import run_bass_kernel_spmd

    v = {k: np.ascontiguousarray(a) for k, a in inputs.items()}
    col = lambda a: a.reshape(D, 1)

    def by_group(a):
        z = np.zeros((4, 32), a.dtype)
        z[:, :H] = a
        return z.reshape(P, 1)

    def by_lane(w):
        return w.reshape(D, HG, HG, DH).transpose(0, 1, 3, 2).reshape(D, D)

    wo = v["L1_xattn_Wo"].T.reshape(HP, 2, DH, D).transpose(1, 0, 2, 3).reshape(D, D)
    arrays = {
        "x": v["x"].reshape(NTOK, D), "ctx": v["ctx_1024"].reshape(NTOK, D),
        "mask": v["mask_Bx1x1xS2_bf1"].reshape(NT, P).view(np.uint8),
        "g": np.concatenate([v["g_xattn"], v["g_ffn"]]).reshape(1, 4),
        "W": np.stack([v["L0_xattn_Wq"], v["L0_xattn_Wq"].T, v["L0_xattn_Wk"], v["L0_xattn_Wk"].T, v["L0_xattn_Wv"],
                       v["L0_xattn_Wt"].T, v["L0_xattn_Wp"], by_lane(v["L1_xattn_Wq"].T), by_lane(v["L1_xattn_Wk"].T),
                       v["L1_xattn_Wv"].T, wo]),
        "wa": np.stack([v["L0_xattn_Wqa"], v["L0_xattn_Wka"]]),
        "wr": np.stack([v["L0_ffn_W_router"], v["L1_ffn_router_w"].T]),
        "bcol": np.concatenate([col(v["L0_xattn_" + b]) for b in ("bq", "bk", "bv", "bt")], axis=1),
        "bacol": np.concatenate([by_group(v["L0_xattn_bqa"]), by_group(v["L0_xattn_bka"])], axis=1),
        "bp": v["L0_xattn_bp"].reshape(1, D), "br": v["L0_ffn_b_router"].reshape(1, E),
        "b1": v["L0_ffn_b1"].reshape(E, FC, P).transpose(2, 0, 1).reshape(P, E * FC),
        "b2": v["L0_ffn_b2"].reshape(1, E * D),
        "w1_0": v["L0_ffn_W1"], "w2_0": v["L0_ffn_W2"], "w1_1": v["L1_ffn_w1"], "w2_1": v["L1_ffn_w2"],
    }
    nc = bacc.Bacc("TRN2", target_bir_lowering=False, num_devices=1)
    A, feed = {}, {}
    for name, a in arrays.items():
        a = np.ascontiguousarray(a)
        feed[f"in_{name}"] = a
        A[name] = nc.dram_tensor(f"in_{name}", a.shape, mybir.dt.from_np(a.dtype), kind="ExternalInput").ap()
    out = nc.dram_tensor("out", (NTOK, D), F32, kind="ExternalOutput").ap()
    build(nc, A, out)
    r = run_bass_kernel_spmd(nc, [feed], core_ids=[0])
    return r.results[0]["out"].reshape(_OUT[0])
```

```python
from contextlib import ExitStack

import concourse.bass as bass
from concourse import mybir

ALU = mybir.AluOpType
ACT = mybir.ActivationFunctionType
F32 = mybir.dt.float32
F16 = mybir.dt.float16
U32 = mybir.dt.uint32
I32 = mybir.dt.int32
U8 = mybir.dt.uint8
AX = mybir.AxisListType.X
ds = bass.ds

P = 128
D = 128
SEQ = 64
NB = 64
NTOK = NB * SEQ
NT = NTOK // P
CT_TILES = 4
CHUNK = CT_TILES * P
NC = NTOK // CHUNK
NP = NC // 2
CB = CHUNK // SEQ
H, DH = 16, 8
HP = H // 2
HG = 4
E, FF, TOPK = 8, 512, 2
FC = FF // P
SLOTS = NTOK * TOPK
TILE = 256
CAP = NTOK + TILE
ROW16 = 2 * D + 2
TILES = (SLOTS // TILE + E, SLOTS // TILE)
FIX0 = E * CAP
XS_ROWS = E * CAP + E * TILE
DUMMY = SLOTS
Y_ROWS = SLOTS + 2 * E * TILE
WSCALE = 256.0
EPS = 1e-5
BIG = 3.0e38
QK_PARTS = ((0, 1, 0), (0, 0, 1))
QK_ROWS = 3 * HG * DH
QK_SCALE = (float(DH) ** -0.5, 1.0)
MASKED = -60000.0
STORED = 32
XS_LEAD = 8


def bc(ap, axis, n):
    shape = list(ap.shape)
    shape.insert(axis, n)
    return ap.unsqueeze(axis).broadcast_to(shape)


def build(nc, A, out):
    ctx = ExitStack()
    with ctx:
        def sb(name, shape, dt=F32):
            return ctx.enter_context(nc.sbuf_tensor(name, shape, dt))

        def sem(name):
            return ctx.enter_context(nc.semaphore(name))

        xs = [nc.dram_tensor(f"xs{l}", [XS_ROWS, ROW16], F16).ap() for l in range(2)]
        ys = [nc.dram_tensor(f"ys{l}", [Y_ROWS, D], F32).ap() for l in range(2)]
        qk_dram = [nc.dram_tensor(n, [NC, QK_ROWS, HG, CHUNK], F16).ap() for n in ("q_parts", "k_parts")]
        nmax_dram = nc.dram_tensor("max_rows", [2, HG, HG, HG * CHUNK], F16).ap()
        mask_dram = nc.dram_tensor("mask_row", [NT, P], F16).ap()

        X = sb("X", [P, NT, D])
        XN = sb("XN", [P, NT, D])
        W = sb("W", [P, 11, D])
        wq, wqT, wk, wkT, wv, wtT, wp, wq1T, wk1T, wv1T, wo1T = (W[:, i, :] for i in range(11))
        wa = sb("wa", [P, 2, H])
        wr = sb("wr", [P, 2, E])
        bcol = sb("bcol", [P, 4])
        bacol = sb("bacol", [P, 2])
        bprow = sb("bprow", [1, D])
        brb = sb("brb", [P, E])
        b1 = sb("b1", [P, E * FC])
        g4 = sb("g4", [P, 4])
        gt = sb("gt", [P, 4])
        ident = sb("ident", [P, P])
        ident16 = sb("ident16", [P, P], F16)
        tri16 = sb("tri16", [P, P], F16)
        ones16 = sb("ones16", [P, P], F16)
        onesrow = sb("onesrow", [1, P])
        hmask = sb("hmask", [P, H])
        expert_i = sb("expert_i", [P, E], I32)
        expert_row = sb("expert_row", [P, E])
        rev_i = sb("rev_i", [P, E], I32)
        rev = sb("rev", [P, E])
        id_tok = sb("id_tok", [P, NT, TOPK], U32)
        id_pad = sb("id_pad", [P, 2 * E, 2], U32)
        pos_i = sb("pos_i", [P, 80], I32)
        pos128 = sb("pos128", [P, 80])
        lane_i = sb("lane_i", [P, 1], I32)
        lane = sb("lane", [P, 1])
        eidx_i = sb("eidx_i", [P, 2, TILES[0]], I32)
        stats = sb("stats", [P, NT, 6])
        mv = sb("mv", [P, NT, 2])
        rstd = sb("rstd", [P, NT])
        nwt = sb("nwt", [P, 2, 2 * CT_TILES])
        lg = sb("lg", [P, NT, E])
        rtmp = sb("rtmp", [P, 3, 2 * CT_TILES, E])
        rmax = sb("rmax", [P, 4, NT])
        oh = sb("oh", [P, TOPK, NT, E])
        sel16 = sb("sel16", [P, NT, E], F16)
        cum16 = sb("cum16", [P, E], F16)
        csum = sb("csum", [P, E])
        wdif = sb("wdif", [P, NT])
        wexp = sb("wexp", [P, NT])
        wden = sb("wden", [P, NT])
        wgt = sb("wgt", [P, NT, TOPK])
        adr = sb("adr", [P, TOPK, NT])
        adr_i = sb("adr_i", [P, TOPK, NT], U32)
        pack = sb("pack", [P, 2, CT_TILES, TOPK, ROW16], F16)
        turn = sb("turn", [1, XS_LEAD])
        zrow = sb("zrow", [P, ROW16], F16)
        rxt = sb("rxt", [P, 2, CHUNK])
        cnt = sb("cnt", [P, E])
        cnt_i = sb("cnt_i", [P, E], I32)
        cnt_s = sb("cnt_s", [P, E])
        incl = sb("incl", [P, E])
        jump = sb("jump", [P, E])
        onesE = sb("onesE", [P, E])
        big1 = rxt[:, :, :].rearrange("p u n -> p (u n)")[:, 0:80 * E].rearrange("p (n e) -> p n e", e=E)
        row_f = sb("row_f", [P, 80])
        er_f = sb("er_f", [P, 80])
        fx_f = sb("fx_f", [P, 3, 80])
        rows_i = sb("rows_i", [P, 80], I32)
        tail_f = sb("tail_f", [P, E])
        tail_i = sb("tail_i", [P, E], I32)
        fixp = sb("fixp", [P, 4, E])
        fixp_i = sb("fixp_i", [P, E], I32)
        fixadr_i = sb("fixadr_i", [P, E], U32)

        mask_u8 = sb("mask_u8", [NT, P], U8)
        mask_f = sb("mask_f", [NT, P])
        mask16 = sb("mask16", [NT, P], F16)
        mask_bias = sb("mask_bias", [P, NT])

        w1h = sb("w1h", [P, E * FF], F16)
        w1l = sb("w1l", [P, E * FF], F16)
        w2 = sb("w2", [P, E * FF])

        WORK = int(109.5 * 1024)
        work = sb("work", [P, WORK // 4])

        def at(kb, shape, dt=F32):
            size = {F32: 4, U32: 4, F16: 2}[dt]
            n = 1
            for s in shape:
                n *= s
            a = int(kb * 256)
            assert a + n * size // 4 <= WORK // 4, (kb, shape)
            v = work[:, a:a + n * size // 4]
            if dt is not F32:
                v = v.bitcast(dt)
            names = "abcdef"[:len(shape)]
            if len(shape) > 1:
                v = v.rearrange(f"p ({' '.join(names)}) -> p {' '.join(names)}",
                                **{k: s for k, s in zip(names[1:], shape[1:])})
            return v

        ctT = at(52, [NTOK])
        xnT = at(36, [NTOK])
        ctx_tok = at(0, [NT, D])
        sl = at(16, [1024])
        se = at(20, [1024])
        w2blk = at(24, [NT, 2, H])
        xp = at(28, [1024])
        prod = at(32, [1024])
        g32 = at(68, [NB, 32])
        gp = at(76, [NB, H])
        wa32 = at(80, [2, 4, 32])
        wka_bk = at(81, [32])
        wqqa = at(81.25, [32])
        wtp = at(82, [D])
        wqp = at(82.5, [D])
        crow = at(83, [D])
        btq = at(83.5, [2])
        qb = at(83.75, [2])
        kb16 = at(84, [H])
        pq = at(84.25, [NB])
        pkv = at(84.5, [NB])
        smx = at(84.75, [H])
        ssum = at(84.85, [16])
        srec = at(84.95, [16])
        uT = at(85.5, [2, CHUNK])
        w1raw = at(90, [2, FF])
        padt = at(94, [E, 2, ROW16], F16)
        b2b = at(104, [E * D])
        xin = at(0, [XS_LEAD, 2, ROW16], F16)
        xgT = at(8.25, [2, 2, TILE], F16)
        hid = at(10.25, [2, FC, TILE])
        yrow = at(18.5, [XS_LEAD, 2, D])
        yc = at(44, [4, CT_TILES, TOPK, D])
        fixs = at(104, [7, ROW16], F16)
        qmask = at(0, [2, HG, HG, CHUNK], F16)
        kmask = at(77.5, [2, HG, HG, CHUNK], F16)
        p16 = at(40, [2, 2, 1024], F16)
        q3 = at(32, [2, HG, CHUNK], F16)
        k3 = w2[:, 0:3 * HG * CHUNK // 2].bitcast(F16).rearrange("p (u r n) -> p u r n", u=3, r=HG)
        rmaxq = at(48, [2, CT_TILES, H])
        nmax = at(48.5, [CT_TILES * H])
        nmax16 = at(48.75, [2, CT_TILES * H], F16)
        nmaxT = at(49, [P], F16)
        orec = at(49.25, [32])
        onorm = at(49.5, [2, HP * 2 * DH])
        oT = at(50.5, [2, P])
        v9h = at(68, [2, CT_TILES, H, 2, DH + 1], F16)
        v9l = at(72.5, [2, CT_TILES, H, 2, DH + 1], F16)
        xnT1 = at(40, [2, CHUNK])
        qk16 = w1l[:, 0:8 * CHUNK].rearrange("p (u w h n) -> p u w h n", u=2, w=2, h=2)
        w1raw1 = w2[:, 3 * HG * CHUNK // 2:3 * HG * CHUNK // 2 + 2 * FF].rearrange("p (u n) -> p u n", u=2)
        pexp = XN[:, NT // 2:NT, :].rearrange("p (u t) d -> p u (t d)", u=2)

        PS = ctx.enter_context(nc.psum_tensor("PS", [P, 8, 512], F32))
        PF = PS[:, :, :].rearrange("p b n -> p (b n)")

        def banks(b, n):
            return PF[:, b * 512:b * 512 + n]

        w_late = sem("w_late")
        w_in = sem("w_in")
        x_in = [sem(f"x_in{c}") for c in range(NC)]
        pool_step = sem("pool_step")
        consts = sem("consts")
        dve_step = sem("dve_step")
        fold_ps, fold_sb = sem("fold_ps"), sem("fold_sb")
        xn_done = sem("xn_done")
        xt_ps, xt_done = sem("xt_ps"), sem("xt_done")
        c_ps, c_done = sem("c_ps"), sem("c_done")
        soft = {k: sem(f"soft_{k}") for k in ("logits", "shifted", "exp", "weights", "wT", "blocks", "pooled",
                                              "pooled_sb", "projected", "head_prod")}
        gsem = {k: sem(f"g_{k}") for k in ("moving", "ps", "sb")}
        v_ps, u_done = sem("v_ps"), sem("u_done")
        att_ps, x1_done = sem("att_ps"), sem("x1_done")
        gates = sem("gates")
        fold_in = sem("fold_in")
        rt = [{k: sem(f"r{l}_{k}") for k in ("xn", "xT", "xT_sb", "logits", "lg", "mask", "rank",
                                             "rank_read", "ranked", "count", "packed")} for l in range(2)]
        total, table, gap, gap_exp = (sem(f"r_{k}") for k in ("total", "table", "gap", "exp"))
        scat = [[sem(f"scat{l}_{u}") for u in range(2)] for l in range(2)]
        tails = sem("tails")
        zero, filled = sem("zero"), sem("filled")
        spare = sem("spare")
        fix_read, fix_kept = sem("fix_read"), sem("fix_kept")
        w1_in = [[sem(f"w1_in{l}_{u}") for u in range(2)] for l in range(2)]
        w2_in = sem("w2_in")
        pack_hi, pack_lo = sem("pack_hi"), sem("pack_lo")
        w1_lo = [sem(f"w1_lo{l}") for l in range(2)]
        ff = {k: [sem(f"f_{k}{u}") for u in range(n)] for k, n in
              (("xin", XS_LEAD), ("xT", 2), ("xT_sb", 2), ("up", 2), ("hid", 2), ("y", 2), ("yrow", 2), ("turn", 1),
               ("stored", XS_LEAD))}
        rounds = [TILES[l] // XS_LEAD for l in range(2)]
        before = [0, rounds[0]]
        y_in = [sem(f"y_in{u}") for u in range(2)]
        x_ff = [sem(f"x_ff{l}") for l in range(2)]
        xn3, x3t_ps, x3t_sb = sem("xn3"), sem("x3t_ps"), sem("x3t_sb")
        qk_ps, qk_hi, qk_lo = sem("qk_ps"), sem("qk_hi"), sem("qk_lo")
        qk_out = [sem(f"qk_out{u}") for u in range(2)]
        mask_rows, mask_T, mask_sb, mask_out = (sem(f"mask_{k}") for k in ("rows", "T", "sb", "out"))
        blank = sem("blank")
        qk_in = [sem(f"qk_in{u}") for u in range(2)]
        qm_in = [sem(f"qm_in{u}") for u in range(2)]
        q_blank, k_blank = sem("q_blank"), sem("k_blank")
        n_out = sem("n_out")
        n_in = sem("n_in")
        v9_ps, v9_sb, v9_lo = sem("v9_ps"), sem("v9_sb"), sem("v9_lo")
        s_ps, s_max = sem("s_ps"), sem("s_max")
        n_ready, nT_ps, nT_sb = sem("n_ready"), sem("nT_ps"), sem("nT_sb")
        st_ps, p_done, p_hi, p_lo = sem("st_ps"), sem("p_done"), sem("p_hi"), sem("p_lo")
        av_ps, o_norm = sem("av_ps"), sem("o_norm")
        oT_ps, oT_sb, o_ps, x3_done = sem("oT_ps"), sem("oT_sb"), sem("o_ps"), sem("x3_done")
        stored = sem("stored")

        YC = (2, 4)

        def y_slot(l, c):
            if l == 0:
                return c % 2, y_in[c % 2], 16 * (c // 2 + 1)
            return c % 4, ff["xin"][c % 4], 32 * (before[1] + rounds[1]) + 16 * (c // 4 + 1)

        block = ctx.enter_context(nc.Block())

        def wait(engine, s, value):
            if not (isinstance(value, int) and value == 0):
                engine.wait_ge(s, value)

        def expert_tiles(engine, l, step):
            for q in range(XS_LEAD):
                step(0, q)
            with engine.Fori(1, TILES[l] // XS_LEAD) as i:
                for q in range(XS_LEAD):
                    step(i, q)

        def tiles(c):
            return slice(c * CT_TILES, (c + 1) * CT_TILES)

        def cols(c):
            return slice(c * CHUNK, (c + 1) * CHUNK)

        def pair(p):
            return slice(2 * p * CT_TILES, (2 * p + 2) * CT_TILES)

        def slots(l, c):
            return tiles(c if l == 0 else c % 4)

        NL = 6
        NW = 6
        ORDER = [s_.split() for s_ in (
            "load 0/load 1/load 2/load 3/logits 0 0/load 4/weights 0 0/load 5/pool 0 0/split 0/load 6/load 7/heads 0 0/"
            "logits 0 1/split 1/keys 0/weights 0 1/split 2/pool 0 1/logits 1 0/split 3/weights 1 0/split 4/pool 1 0/"
            "heads 0 1/split 5/keys 1/split 6/heads 1 0/logits 1 1/values 0/scale 0/attend 0/add 0/values 1/split 7/"
            "weights 1 1/scale 1/pool 1 1/route 0/attend 1/choose 0/heads 1 1/add 1/rows 0/values 2/scale 2/attend 2/"
            "values 3/route 1/add 2/choose 1/scale 3/attend 3/rows 1/route 2/add 3/choose 2/rows 2/route 3/choose 3/"
            "rows 3").split("/")]
        ORDER = [(s_[0], int(s_[1]), int(s_[-1])) for s_ in ORDER]
        XT_BANK, XT_PREV = (0, 1, 0, 1, 1, 5, 1, 5), (None, None, 0, 1, 3, None, 4, 5)
        CT_BANK, CT_PREV = (2, 3, 2, 3, 3, 3, 3, 3), (None, None, 0, 1, 3, 4, 5, 6)
        V_BANK, A_BANK, V_PREV = (4, 4, 4, 4, 4, 5, 4, 5), (0, 0, 0, 0, 0, 1, 0, 1), (None, 0, 1, 2, 3, None, 4, 5)
        QK_STORES = 6 * 16
        QK_LOADS = 3 + HG
        LEAD = 6
        G0, G1 = -LEAD - 2, NT + 13
        BANK_XT, BANK_LG, BANK_RANK = ((2, 3), (7, 7)), (6, 7), (6, 7)
        BANK_Q, BANK_K = (2, 5), (3, 6)
        LG0, RANK0, TOTAL0 = 256, 320, 384

        def chunk_at(g, lead):
            k, rest = divmod(g - lead, CT_TILES)
            return k if rest == 0 and 0 <= k < NC else None

        def pair_at(g, lead):
            k, rest = divmod(g - lead, 2 * CT_TILES)
            return k if rest == 0 and 0 <= k < NP else None

        @block.gpsimd
        def _(pool):
            n = [0]

            def then(ins):
                n[0] += 1
                ins.then_inc(pool_step, 1)
                pool.wait_ge(pool_step, n[0])

            g = nc.gpsimd
            g.memset(ident[:], 0.0)
            g.memset(ident16[:], 0.0)
            g.memset(tri16[:], 1.0)
            g.memset(ones16[:], 1.0)
            g.memset(onesrow[:], 1.0)
            g.memset(onesE[:], 1.0)
            g.memset(cum16[:], 0.0)
            g.memset(wa32, 0.0)
            g.memset(wqqa, 0.0)
            then(g.memset(hmask[:], 1.0))
            for t in (ident, ident16):
                g.affine_select(out=t[:], in_=t[:], compare_op=ALU.not_equal, fill=1.0, base=0,
                                pattern=[[-1, P]], channel_multiplier=1)
            g.affine_select(out=tri16[:], in_=tri16[:], compare_op=ALU.is_gt, fill=0.0, base=0,
                            pattern=[[1, P]], channel_multiplier=-1)
            then(g.affine_select(out=hmask[:], in_=hmask[:], compare_op=ALU.is_ge, fill=0.0, base=0,
                                 pattern=[[-DH, H]], channel_multiplier=1))
            g.affine_select(out=hmask[:], in_=hmask[:], compare_op=ALU.is_ge, fill=0.0, base=DH - 1,
                            pattern=[[DH, H]], channel_multiplier=-1)
            g.iota(expert_i[:], [[CAP, E]], base=0, channel_multiplier=0)
            g.iota(rev_i[:], [[-1, E]], base=E, channel_multiplier=0)
            g.iota(id_tok[:], [[TOPK * P, NT], [1, TOPK]], base=0, channel_multiplier=TOPK)
            g.iota(id_pad[:], [[TILE, 2 * E], [P, 2]], base=DUMMY, channel_multiplier=1)
            g.iota(pos_i[:], [[P, 80]], base=0, channel_multiplier=0)
            g.iota(lane_i[:], [[1, 1]], base=0, channel_multiplier=1)
            then(g.iota(eidx_i[:, 1, 0:TILES[1]], [[1, E], [0, TILES[1] // E]], base=0, channel_multiplier=0))
            g.tensor_copy(expert_row[:], expert_i[:])
            g.tensor_copy(rev[:], rev_i[:])
            g.tensor_copy(pos128[:], pos_i[:])
            g.tensor_copy(lane[:], lane_i[:]).then_inc(consts, 1)
            g.memset(zrow[:], 0.0).then_inc(zero, 1)
            g.memset(w2blk, 0.0)
            g.memset(g32, 0.0)
            then(g.memset(padt, 0.0))
            pid = padt.bitcast(U32)
            g.tensor_copy(pid[:, :, :, D:D + 1], id_pad[:, E:2 * E, :].unsqueeze(3)).then_inc(consts, 1)
            pool.wait_ge(consts, 2)
            g.dma_start(xs[0][FIX0:FIX0 + E * TILE, :].rearrange("(s u p) n -> p s u n", u=2, p=P),
                        padt).then_inc(spare, 16)
            pool.wait_ge(spare, 16)
            g.tensor_copy(pid[:, :, :, D:D + 1], id_pad[:, 0:E, :].unsqueeze(3)).then_inc(consts, 1)

            def scatter(l, c, parts=range(CT_TILES)):
                pool.wait_ge(rt[l]["packed"], c + 1)
                pool.wait_ge(rt[l]["ranked"], c // 2 + 1)
                for s in parts:
                    for k in range(TOPK):
                        T = c * CT_TILES + s
                        g.indirect_dma_start(xs[l], bass.IndirectOffsetOnAxis(adr_i[:, k, T:T + 1], 0),
                                             pack[:, c % 2, s, k, :], None).then_inc(scat[l][c % 2], 16)

            def experts(l):
                def step(i, q):
                    pool.wait_ge(ff["yrow"][q % 2], (i + before[l]) * (XS_LEAD // 2) + q // 2 + 1)
                    g.tensor_tensor(turn[:, q:q + 1], lane[0:1, :], lane[0:1, :], ALU.mult).then_inc(ff["turn"][0], 1)
                    for u in range(2):
                        g.indirect_dma_start(
                            ys[l], bass.IndirectOffsetOnAxis(xin[:, q, u, :].bitcast(U32)[:, D:D + 1], 0),
                            yrow[:, q, u, :], None).then_inc(ff["stored"][q], 16)

                expert_tiles(pool, l, step)

            for c in range(NC):
                scatter(0, c)
            experts(0)
            g.memset(kmask[:, 0, :, :, :], 0.0).then_inc(k_blank, 1)
            pool.wait_ge(x_ff[0], 1)
            pool.wait_ge(k_blank, 1)
            then(g.memset(q3[96:97, :, :, :], 1.0))
            g.memset(k3[96:104, :, :, :], 1.0).then_inc(k_blank, 1)
            pool.wait_ge(k_blank, 2)
            g.memset(qmask[:, 0, :, :, :], 0.0).then_inc(q_blank, 1)
            g.memset(kmask[:, 1, :, :, :], 0.0).then_inc(k_blank, 1)
            g.memset(qmask[:, 1, :, :, :], 0.0).then_inc(q_blank, 1)
            pool.wait_ge(filled, 16 * (E + 1))
            for step in range(NT + 19):
                if step < NT:
                    pool.wait_ge(p_hi, step + 1)
                    if step >= 2:
                        pool.wait_ge(av_ps, step - 1)
                    g.tensor_tensor(p16[:, step % 2, 1, :], pexp[:, step % 2, :], p16[:, step % 2, 0, :],
                                    ALU.subtract).then_inc(p_lo, 1)
                p_, rest = divmod(step - 19, 2 * CT_TILES)
                if 0 <= p_ < NP:
                    scatter(1, 2 * p_ + rest // CT_TILES, (rest % CT_TILES,))
            pool.wait_ge(table, 2)
            for u in range(2):
                pool.wait_ge(scat[1][u], 16 * CT_TILES * TOPK * (NC // 2))
            for q in range(E - 1):
                g.indirect_dma_start(fixs[:, q, :], None, xs[1][0:FIX0, :],
                                     bass.IndirectOffsetOnAxis(fixadr_i[:, q:q + 1], 0)).then_inc(fix_read, 16)
            experts(1)

        def load_rows(sp, l, i_tile, q):
            for u in range(2):
                r = sp.value_load(rows_i[0:1, ds(i_tile * 2 + u, 1)], min_val=0, max_val=XS_ROWS - P)
                sp.dma_start(xin[:, q, u, :], xs[l][ds(r, P), :]).then_inc(ff["xin"][q], 16)

        def y_rows(l, c):
            return ys[l][c * CHUNK * TOPK:(c + 1) * CHUNK * TOPK, :].rearrange("(s p k) d -> p s (k d)", p=P, k=TOPK)

        x_rows = A["x"].rearrange("(t p) d -> p t d", p=P)
        c_rows = A["ctx"].rearrange("(t p) d -> p t d", p=P)
        out_rows = out.rearrange("(t p) d -> p t d", p=P)

        @block.sync
        def _(sp):
            for c in range(NC):
                sp.dma_start(X[:, tiles(c), :], x_rows[:, tiles(c), :]).then_inc(x_in[c], 16)
                sp.dma_start(ctx_tok[:, tiles(c), :], c_rows[:, tiles(c), :]).then_inc(x_in[c], 16)
                if c == 1:
                    sp.dma_start(W[:], A["W"].rearrange("w i o -> i w o")).then_inc(w_in, 16)
                    sp.dma_start(wa[:], A["wa"].rearrange("w i o -> i w o")).then_inc(w_in, 16)
                    sp.dma_start(bcol[:], A["bcol"]).then_inc(w_in, 16)
                    sp.dma_start(bacol[:], A["bacol"]).then_inc(w_in, 16)
                    sp.dma_start(bprow[:], A["bp"]).then_inc(w_in, 16)
                    sp.dma_start(g4[:], A["g"].partition_broadcast(P)).then_inc(w_in, 16)
            sp.dma_start(wr[:], A["wr"].rearrange("w i o -> i w o")).then_inc(w_late, 16)
            sp.dma_start(brb[:], A["br"].partition_broadcast(P)).then_inc(w_late, 16)
            sp.dma_start(b1[:], A["b1"]).then_inc(w_late, 16)
            sp.dma_start(b2b, A["b2"].partition_broadcast(P)).then_inc(w_late, 16)
            sp.dma_start(mask_u8[:], A["mask"]).then_inc(w_late, 16)
            sp.dma_start(w2[:].rearrange("p (e c d) -> p e c d", e=E, c=FC),
                         A["w2_0"].rearrange("e (c p) d -> p e c d", p=P)).then_inc(w_late, 16)

            sp.wait_ge(zero, 1)
            for e in range(E + 2):
                if e >= 2:
                    sp.dma_start(xs[1][(e - 2) * CAP:(e - 1) * CAP, :].rearrange("(p m) n -> p m n", p=P),
                                 bc(zrow[:], 1, CAP // P)).then_inc(filled, 16)
                if e < E:
                    if e >= 2:
                        sp.wait_ge(w1_lo[0], e - 1)
                    sp.dma_start(w1raw[:, e % 2, :], A["w1_0"][e]).then_inc(w1_in[0][e % 2], 16)
            sp.dma_start(nmax_dram.rearrange("t j b n -> (t j b n)").rearrange("(p m n) -> p m n", p=P, m=2),
                         bc(zrow[:, 0:D * 2], 1, 2)).then_inc(filled, 16)

            sp.wait_ge(table, 1)
            sp.wait_ge(consts, 3)
            for e in range(E):
                r = sp.value_load(tail_i[0:1, e:e + 1], min_val=0, max_val=XS_ROWS - TILE)
                sp.dma_start(xs[0][ds(r, TILE), :].rearrange("(u p) n -> p u n", p=P), padt[:, e, :, :]).then_inc(tails, 16)
            sp.wait_ge(tails, 16 * E)
            sp.wait_ge(spare, 16)
            for u in range(2):
                sp.wait_ge(scat[0][u], 16 * CT_TILES * TOPK * (NC // 2))

            def experts(l):
                def step(i, q):
                    wait(sp, ff["stored"][q], (i + before[l]) * STORED)
                    load_rows(sp, l, i * XS_LEAD + q, q)

                expert_tiles(sp, l, step)
                for q in range(XS_LEAD):
                    sp.wait_ge(ff["stored"][q], STORED * (before[l] + rounds[l]))

            def y_load(l, c):
                slot, s_, _ = y_slot(l, c)
                if c >= YC[l]:
                    sp.wait_ge(x_ff[l], c - YC[l] + 1)
                sp.dma_start(yc[:, slot, :, :, :].rearrange("p s k d -> p s (k d)"), y_rows(l, c)).then_inc(s_, 16)

            experts(0)
            y_load(0, 0)
            y_load(0, 1)

            sp.wait_ge(mask_rows, 1)
            sp.dma_start(mask_dram, mask16[:]).then_inc(mask_out, 16)
            def blocks(dst, which, c, s_):
                for j in range(HG):
                    sp.dma_start(dst[j:QK_ROWS:HG, c % 2, j, :, :], qk_dram[which][c, j:QK_ROWS:HG]).then_inc(s_, 16)

            def load(c):
                u = c % 2
                sp.wait_ge(k_blank, u + 2)
                if c >= 2:
                    sp.wait_ge(s_ps, CT_TILES * (c - 1))
                if c >= 3:
                    sp.wait_ge(st_ps, CT_TILES * (c - 2))
                sp.dma_start(k3[0:QK_ROWS, c % 3, :, :], qk_dram[1][c]).then_inc(qk_in[u], 16)
                sp.dma_start(q3[0:QK_ROWS, u, :, :], qk_dram[0][c]).then_inc(qk_in[u], 16)
                blocks(kmask, 1, c, qk_in[u])
                row = mask_dram[tiles(c), :].rearrange("s p -> (s p)").unsqueeze(0).unsqueeze(1)
                sp.dma_start(kmask[96:97, u, :, :, :].rearrange("o j r n -> o (j r) n"),
                             row.broadcast_to([1, H, CHUNK])).then_inc(qk_in[u], 16)

            def load_blocks(c):
                sp.wait_ge(q_blank, c % 2 + 1)
                if c >= 2:
                    sp.wait_ge(st_ps, CT_TILES * (c - 1))
                blocks(qmask, 0, c, qm_in[c % 2])

            def load_max(c):
                sp.wait_ge(nT_sb, c + 1)
                if c >= 1:
                    sp.wait_ge(n_in, 16 * c)
                for term in range(2):
                    diag = nmax_dram[term].rearrange("j b n -> (j b) n")[0:HG * HG:HG + 1, :]
                    sp.dma_start(diag, nmaxT[64 * term:64 * term + 64, :]).then_inc(n_out, 16)
                if c >= 2:
                    sp.wait_ge(st_ps, CT_TILES * (c - 1))
                sp.wait_ge(n_out, 32 * (c + 1))
                sp.dma_start(qmask[96:104, c % 2, :, :, :].rearrange("p j r n -> p j (r n)"),
                             nmax_dram.rearrange("t j b n -> (t j) b n")).then_inc(n_in, 16)

            def w1_load(e):
                if e >= 2:
                    sp.wait_ge(w1_lo[1], e - 1)
                sp.dma_start(w1raw1[:, e % 2, :], A["w1_1"][e]).then_inc(w1_in[1][e % 2], 16)

            for c in range(NC):
                if c == 0:
                    for ahead in (2, 3, 4, 5):
                        y_load(0, ahead)
                elif c % 2 == 0 and c + 5 < NC:
                    y_load(0, c + 4)
                    y_load(0, c + 5)
                for n, which in enumerate((1, 0)):
                    sp.wait_ge(qk_lo, 2 * c + n + 1)
                    for third, part in enumerate(QK_PARTS[which]):
                        rows = qk_dram[which][c, third * 32:(third + 1) * 32]
                        sp.dma_start(rows.rearrange("i r n -> r i n"), qk16[:, c % 2, which, part, :])\
                            .then_inc(qk_out[c % 2], 16)
                if c in (5, 6):
                    sp.wait_ge(qk_out[(c - 5) % 2], QK_STORES * 3)
                    if c == 5:
                        sp.wait_ge(mask_out, 16)
                    load(c - 5)
            for u in range(2):
                sp.wait_ge(qk_out[u], QK_STORES * NC // 2)
            for c in range(NC):
                load_blocks(c)
                load_max(c)
                if c + 2 < NC:
                    load(c + 2)
                w1_load(c)
            sp.wait_ge(st_ps, NT)
            sp.wait_ge(w1_lo[1], E)
            sp.dma_start(w2[:].rearrange("p (e c d) -> p e c d", e=E, c=FC),
                         A["w2_1"].rearrange("e (c p) d -> p e c d", p=P)).then_inc(w2_in, 16)
            sp.wait_ge(table, 2)
            sp.wait_ge(fix_read, 16 * (E - 1))
            sp.dma_start(xs[1][FIX0:FIX0 + (E - 1) * P, :].rearrange("(q p) n -> p q n", p=P), fixs).then_inc(fix_kept, 16)
            sp.wait_ge(fix_kept, 16)
            for u in range(2):
                sp.wait_ge(scat[1][u], 16 * CT_TILES * TOPK * (NC // 2))
            experts(1)
            for c in range(NC):
                y_load(1, c)
            sp.wait_ge(stored, 16 * NC)

        @block.tensor
        def _(pe):
            t = nc.tensor

            def mm(o, lhsT, rhs, start=True, stop=True):
                return t.matmul(o, lhsT, rhs, start=start, stop=stop, skip_group_check=True)

            pe.wait_ge(w_in, 16 * NW)
            pe.wait_ge(consts, 1)
            pe.wait_ge(fold_in, 2)
            mm(PS[:, 4, 0:H], wqT, wa[:, 0, :])
            mm(PS[:, 4, D:2 * D], wtT, wp)
            mm(PS[:, 4, 2 * D:3 * D], wqT, wp)
            mm(PS[0:1, 5, 0:D], btq[:, 0:1], wp)
            mm(PS[:, 5, D:D + 1], wa32[:, 0, :, :].rearrange("p j h -> p (j h)"), bcol[:, 0:1]).then_inc(fold_ps, 1)

            def q_logits(c):
                pe.wait_ge(xt_done, c + 1)
                pe.wait_ge(fold_sb, 1)
                j = 32 * (c % 4)
                mm(PS[j:j + 32, 6 + c // 4, :], wqqa, xnT[:, cols(c)]).then_inc(soft["logits"], 1)

            def load(c):
                pe.wait_ge(xn_done, c + 1)
                if XT_PREV[c] is not None:
                    pe.wait_ge(xt_done, XT_PREV[c] + 1)
                for s in range(CT_TILES):
                    ins = t.transpose(PS[:, XT_BANK[c], s * P:(s + 1) * P], XN[:, c * CT_TILES + s, :], ident[:])
                ins.then_inc(xt_ps, 1)
                pe.wait_ge(x_in[c], 32)
                if CT_PREV[c] is not None:
                    pe.wait_ge(c_done, CT_PREV[c] + 1)
                for s in range(CT_TILES):
                    ins = t.transpose(PS[:, CT_BANK[c], s * P:(s + 1) * P], ctx_tok[:, c * CT_TILES + s, :], ident[:])
                ins.then_inc(c_ps, 1)
                q_logits(c)

            def weights_transposed(r, a):
                pe.wait_ge(soft["weights"], 2 * r + a + 1)
                pe.wait_ge(xt_done, 4 * (a + 1))
                for i in range(4):
                    col = a * 512 + i * P
                    ins = t.transpose(PS[:, a, i * P:(i + 1) * P], se[:, col:col + P], ident[:])
                ins.then_inc(soft["wT"], 1)

            def pool_(r, a):
                src, w = ((XN, wq), (ctx_tok, wk))[r]
                pe.wait_ge(soft["blocks"], 2 * r + a + 1)
                pe.wait_ge(c_done, 4 * (a + 1))
                for T in range(a * NT // 2, (a + 1) * NT // 2):
                    ins = mm(PF[:, 1024 + T * 32:1024 + (T + 1) * 32], src[:, T, :],
                             w2blk[:, T, :, :].rearrange("p b h -> p (b h)"))
                ins.then_inc(soft["pooled"], 1)
                pe.wait_ge(soft["pooled_sb"], 2 * r + a + 1)
                mm(PS[:, 4 + a, :], w, xp[:, a * 512:(a + 1) * 512]).then_inc(soft["projected"], 1)

            def keys(a):
                pe.wait_ge(gsem["moving"], a + 1)
                mm(PS[:, 2 + a, :], wkT, gp.rearrange("p b h -> p (b h)")[:, a * 512:(a + 1) * 512])
                pqv = pq.rearrange("p (a j b) -> p a j b", a=2, j=4)
                for j in range(4):
                    ins = mm(PS[32 * j:32 * j + 32, a, 0:CB], wka_bk, pqv[:, a, j, :])
                ins.then_inc(gsem["ps"], 1)
                pe.wait_ge(gsem["sb"], a + 1)
                for b in range(a * NB // 2, (a + 1) * NB // 2):
                    c, bb = b // CB, b % CB
                    j = 32 * (c % 4)
                    ins = mm(PS[j:j + 32, 6 + a, bb * SEQ:(bb + 1) * SEQ], g32[:, b, :], ctT[:, b * SEQ:(b + 1) * SEQ])
                ins.then_inc(soft["logits"], 1)

            def values(c):
                if V_PREV[c] is not None:
                    pe.wait_ge(u_done, V_PREV[c] + 1)
                pe.wait_ge(soft["head_prod"], 3 + c // 4)
                mm(PS[:, V_BANK[c], :], wv, ctT[:, cols(c)]).then_inc(v_ps, 1)

            def attended(c):
                pe.wait_ge(u_done, c + 1)
                if V_PREV[c] is not None:
                    pe.wait_ge(x1_done, V_PREV[c] + 1)
                for s in range(CT_TILES):
                    o = PS[:, A_BANK[c], s * D:(s + 1) * D]
                    T = c * CT_TILES + s
                    mm(o, uT[:, c % 2, s * P:(s + 1) * P], wtp, stop=False)
                    mm(o, xnT[:, T * P:(T + 1) * P], wqp, start=False, stop=False)
                    ins = mm(o, onesrow[:], crow[0:1, :], start=False)
                ins.then_inc(att_ps, 1)

            def route_transposed(l, c):
                pe.wait_ge(rt[l]["xn"], c + 1)
                if c >= 1 and (l == 1 or c % 2 == 0):
                    pe.wait_ge(rt[l]["xT_sb"], c)
                for s in range(CT_TILES):
                    ins = t.transpose(PS[:, BANK_XT[l][c % 2], s * P:(s + 1) * P], XN[:, slots(l, c).start + s, :], ident[:])
                ins.then_inc(rt[l]["xT"], 1)

            def route_logits(l, c):
                pe.wait_ge(rt[l]["xT_sb"], c + 1)
                if l == 0 and c >= 2:
                    pe.wait_ge(rt[l]["lg"], c // 2 * 2)
                    pe.wait_ge(rt[l]["rank_read"], c // 2)
                if l == 1 and c >= 1:
                    pe.wait_ge(rt[l]["lg"], c)
                if l == 0:
                    pe.wait_ge(w_late, 16 * NL)
                for s in range(CT_TILES):
                    o = LG0 + (c % 2 * CT_TILES + s) * E
                    ins = mm(PS[:, BANK_LG[l], o:o + E], rxt[:, c % 2, s * P:(s + 1) * P], wr[:, l, :])
                ins.then_inc(rt[l]["logits"], 1)

            def route_rank(l, p):
                pe.wait_ge(rt[l]["mask"], p + 1)
                if p >= 1:
                    pe.wait_ge(rt[l]["rank_read"], p)
                    pe.wait_ge(rt[l]["count"], p)
                t0 = pair(p).start
                for s in range(2 * CT_TILES):
                    o = PS[:, BANK_RANK[l], RANK0 + s * E:RANK0 + (s + 1) * E]
                    mm(o, ones16[:], cum16[:], stop=False)
                    for b in range(s):
                        mm(o, ones16[:], sel16[:, t0 + b, :], start=False, stop=False)
                    ins = mm(o, tri16[:], sel16[:, t0 + s, :], start=False)
                ins.then_inc(rt[l]["rank"], 1)

            def route_total(l):
                pe.wait_ge(rt[l]["count"], NP)
                mm(PS[:, BANK_RANK[l], TOTAL0:TOTAL0 + E], ones16[:], cum16[:]).then_inc(total, 1)

            for step, m, n in ORDER:
                if step == "load":
                    load(m)
                elif step == "weights":
                    weights_transposed(m, n)
                elif step == "pool":
                    pool_(m, n)
                elif step == "keys":
                    keys(m)
                elif step == "choose":
                    route_rank(0, m)
                for c in (2 * m, 2 * m + 1):
                    if step == "values":
                        values(c)
                    elif step == "attend":
                        attended(c)
                    elif step == "route":
                        route_transposed(0, c)
                if step == "route":
                    route_logits(0, 2 * m)
                    route_logits(0, 2 * m + 1)
            route_total(0)

            def experts(l):
                f, i0 = ff, before[l]
                pe.wait_ge(w1_lo[l], E)
                if l == 1:
                    pe.wait_ge(w2_in, 16)
                pe.wait_ge(table, l + 1)

                def gather(i, q):
                    v, m = q % 2, (i + i0) * (XS_LEAD // 2) + q // 2
                    pe.wait_ge(f["xin"][q], (i + i0) * 32 + 32)
                    wait(pe, f["xT_sb"][v], m)
                    o = PS[:, v, 0:TILE].bitcast(F16).rearrange("p (h u n) -> p h u n", h=2, u=2)
                    for u in range(2):
                        for h in range(2):
                            ins = t.transpose(o[:, h, u, :], xin[:, q, u, h * D:(h + 1) * D], ident16[:])
                    ins.then_inc(f["xT"][v], 1)

                def up(i, q, e):
                    v, m = q % 2, (i + i0) * (XS_LEAD // 2) + q // 2
                    pe.wait_ge(f["xT_sb"][v], m + 1)
                    wait(pe, f["hid"][v], m)
                    for c in range(FC):
                        o = PF[:, (2 + 2 * v) * 512 + c * TILE:(2 + 2 * v) * 512 + (c + 1) * TILE]
                        for k, (w, h) in enumerate(((w1h, 0), (w1h, 1), (w1l, 0))):
                            ins = mm(o, w[:, ds(e * FF + c * P, P)], xgT[:, v, h, :], start=k == 0, stop=k == 2)
                    ins.then_inc(f["up"][v], 1)

                def down(i, q, e):
                    v, m = q % 2, (i + i0) * (XS_LEAD // 2) + q // 2
                    pe.wait_ge(f["hid"][v], m + 1)
                    wait(pe, f["yrow"][v], m)
                    for u in range(2):
                        for c in range(FC):
                            ins = mm(PS[:, 6 + v, u * D:(u + 1) * D], hid[:, v, c, u * P:(u + 1) * P],
                                     w2[:, ds(e * FF + c * D, D)], start=c == 0, stop=c == FC - 1)
                    ins.then_inc(f["y"][v], 1)

                def expert(tile):
                    return pe.value_load(eidx_i[0:1, l, ds(tile, 1)], min_val=0, max_val=E - 1)

                def round_(i, first, last):
                    for q in range(XS_LEAD):
                        if q < XS_LEAD - 1:
                            gather(i, q + 1)
                        elif not last:
                            gather(i + 1, 0)
                        up(i, q, expert(i * XS_LEAD + q))
                        if q >= 1:
                            down(i, q - 1, expert(i * XS_LEAD + q - 1))
                        elif not first:
                            down(i - 1, XS_LEAD - 1, expert(i * XS_LEAD - 1))

                n = TILES[l] // XS_LEAD
                gather(0, 0)
                round_(0, True, False)
                with pe.Fori(1, n - 1) as i:
                    round_(i, False, False)
                round_(n - 1, False, True)
                down(n - 1, XS_LEAD - 1, expert(TILES[l] - 1))

            experts(0)

            pe.wait_ge(mask_rows, 1)
            t.transpose(PS[:, 4, 0:NT], mask_f[:], ident[0:NT, 0:NT]).then_inc(mask_T, 1)
            for c in range(NC):
                pe.wait_ge(xn3, c + 1)
                if c >= 2:
                    pe.wait_ge(x3t_sb, c - 1)
                for s in range(CT_TILES):
                    ins = t.transpose(PS[:, c % 2, s * P:(s + 1) * P], XN[:, c * CT_TILES + s, :], ident[:])
                ins.then_inc(x3t_ps, 1)
                if c >= 2:
                    pe.wait_ge(qk_lo, 2 * (c - 1))
                mm(PS[:, BANK_K[c % 2], :], wk1T, ctT[:, cols(c)]).then_inc(qk_ps, 1)
                pe.wait_ge(x3t_sb, c + 1)
                mm(PS[:, BANK_Q[c % 2], :], wq1T, xnT1[:, c % 2, :]).then_inc(qk_ps, 1)

            def scores(T):
                c, s = T // CT_TILES, T % CT_TILES
                if s == 0:
                    pe.wait_ge(qk_in[c % 2], 16 * QK_LOADS * (c // 2 + 1))
                if T >= 1:
                    pe.wait_ge(s_max, T)
                for b in range(2):
                    q_ = slice(s * P + b * SEQ, s * P + (b + 1) * SEQ)
                    for r in range(HG):
                        ins = mm(PF[b * SEQ:(b + 1) * SEQ, r * 256:(r + 1) * 256], q3[0:97, c % 2, r, q_],
                                 kmask[0:97, c % 2, :, r, q_])
                ins.then_inc(s_ps, 1)

            def scores_by_key(T):
                c, s = T // CT_TILES, T % CT_TILES
                if s == 0:
                    pe.wait_ge(qm_in[c % 2], 16 * HG * (c // 2 + 1))
                    pe.wait_ge(n_in, 16 * (c + 1))
                if T >= 1:
                    pe.wait_ge(p_done, T)
                for b in range(2):
                    q_ = slice(s * P + b * SEQ, s * P + (b + 1) * SEQ)
                    for r in range(HG):
                        ins = mm(PF[b * SEQ:(b + 1) * SEQ, 1024 + r * 256:1024 + (r + 1) * 256],
                                 k3[0:104, c % 3, r, q_], qmask[0:104, c % 2, :, r, q_])
                ins.then_inc(st_ps, 1)

            def weigh(T):
                c, s = T // CT_TILES, T % CT_TILES
                pe.wait_ge(p_lo, T + 1)
                if s == 0:
                    pe.wait_ge(v9_lo, c + 1)
                if T >= 1:
                    pe.wait_ge(o_norm, T)
                for hp in range(HP):
                    for k, (h, v) in enumerate(((0, v9h), (0, v9l), (1, v9h))):
                        ins = mm(PS[:, 4, hp * 36:(hp + 1) * 36], p16[:, T % 2, h, hp * P:(hp + 1) * P],
                                 v[:, c % 2, s, 2 * hp:2 * hp + 2, :, :].rearrange("p h b n -> p (h b n)"),
                                 start=k == 0, stop=k == 2)
                ins.then_inc(av_ps, 1)

            def heads_transposed(T):
                pe.wait_ge(o_norm, T + 1)
                if T >= 1:
                    pe.wait_ge(oT_sb, T)
                for b in range(2):
                    ins = t.transpose(PS[:, 5, b * P:(b + 1) * P], onorm[:, b, :], ident[:])
                ins.then_inc(oT_ps, 1)

            def project_heads(T):
                pe.wait_ge(oT_sb, T + 1)
                if T >= 1:
                    pe.wait_ge(x3_done, T)
                mm(PS[:, 6, 0:D], oT[:, T % 2, :], wo1T).then_inc(o_ps, 1)

            pe.wait_ge(mask_sb, 1)
            for g in range(G0, G1):
                if 0 <= g < NT:
                    scores_by_key(g)
                if 0 <= g + LEAD < NT:
                    scores(g + LEAD)
                if 0 <= g - 2 < NT:
                    weigh(g - 2)
                if 0 <= g - 3 < NT:
                    heads_transposed(g - 3)
                if 0 <= g - 4 < NT:
                    project_heads(g - 4)
                k = pair_at(g, 17)
                if k is not None:
                    route_logits(1, 2 * k + 1)
                k = chunk_at(g, 3 - LEAD)
                if k is not None:
                    pe.wait_ge(n_ready, k + 1)
                    before_lg, before_rank = (g - 17) // 8 + 1, (g - 18) // 8 + 1
                    if before_lg >= 1:
                        pe.wait_ge(rt[1]["lg"], 2 * before_lg)
                    if before_rank >= 1:
                        pe.wait_ge(rt[1]["rank_read"], before_rank)
                    t.transpose(PS[:, 7, 0:P // 2].bitcast(F16), nmax16.rearrange("p k n -> p (k n)"), ident16[:])\
                        .then_inc(nT_ps, 1)
                k = chunk_at(g, -2)
                if k is not None:
                    pe.wait_ge(nT_sb, k + 1)
                    for s in range(CT_TILES):
                        T = k * CT_TILES + s
                        ins = mm(PS[:, 7, s * D:(s + 1) * D], ctT[:, T * P:(T + 1) * P], wv1T)
                    ins.then_inc(v9_ps, 1)
                k = pair_at(g, 18)
                if k is not None:
                    pe.wait_ge(v9_lo, min(2 * k + 6, NC))
                    route_rank(1, k)
                k = pair_at(g, 15)
                if k is not None:
                    pe.wait_ge(v9_lo, min(2 * k + 5, NC))
                    if k >= 1:
                        pe.wait_ge(rt[1]["rank_read"], k)
                    route_transposed(1, 2 * k)
                k = pair_at(g, 16)
                if k is not None:
                    route_logits(1, 2 * k)
                    pe.wait_ge(rt[1]["lg"], 2 * k + 1)
                    route_transposed(1, 2 * k + 1)
            route_total(1)
            experts(1)

        @block.scalar
        def _(act):
            a = nc.scalar
            act.wait_ge(w_in, 16 * NW)
            a.activation(gt[:], g4[:], ACT.Tanh).then_inc(gates, 1)

            def load(c):
                act.wait_ge(xt_ps, c + 1)
                a.activation(xnT[:, cols(c)], PS[:, XT_BANK[c], :], ACT.Copy).then_inc(xt_done, 1)
                act.wait_ge(c_ps, c + 1)
                a.activation(ctT[:, cols(c)], PS[:, CT_BANK[c], :], ACT.Copy).then_inc(c_done, 1)

            def route_xT(l, c):
                act.wait_ge(rt[l]["xT"], c + 1)
                if c >= 2:
                    act.wait_ge(rt[l]["logits"], c - 1)
                a.activation(rxt[:, c % 2, :], PS[:, BANK_XT[l][c % 2], :], ACT.Copy).then_inc(rt[l]["xT_sb"], 1)

            def route_high(l, c):
                act.wait_ge(rt[l]["xn"], c + 1)
                if c >= 2:
                    act.wait_ge(scat[l][c % 2], 16 * CT_TILES * TOPK * (c // 2))
                a.activation(pack[:, c % 2, :, 0, 0:D], XN[:, slots(l, c), :], ACT.Copy).then_inc(pack_hi, 1)

            def route_copy(l, c):
                act.wait_ge(pack_lo, l * NC + c + 1)
                a.activation(pack[:, c % 2, :, 1, 0:2 * D], pack[:, c % 2, :, 0, 0:2 * D], ACT.Copy).then_inc(rt[l]["packed"], 1)

            def route_exp(l, p):
                act.wait_ge(gap, l * NP + p + 1)
                a.activation(wexp[:, pair(p)], wdif[:, pair(p)], ACT.Exp).then_inc(gap_exp, 1)

            for step, m, n in ORDER:
                half = slice(n * 512, (n + 1) * 512)
                if step == "load":
                    load(m)
                elif step == "logits":
                    act.wait_ge(soft["shifted"], 2 * m + n + 1)
                    a.activation(se[:, half], sl[:, half], ACT.Exp, scale=float(DH) ** -0.5).then_inc(soft["exp"], 1)
                elif step == "pool":
                    act.wait_ge(soft["pooled"], 2 * m + n + 1)
                    a.activation(xp[:, half], PS[:, 2 + n, :], ACT.Copy).then_inc(soft["pooled_sb"], 1)
                elif step == "keys":
                    act.wait_ge(gsem["ps"], m + 1)
                    act.wait_ge(consts, 2)
                    a.activation(g32[:, m * NB // 2:(m + 1) * NB // 2, 0:H], PS[:, 2 + m, :].rearrange("p (b h) -> p b h", h=H),
                                 ACT.Copy).then_inc(gsem["sb"], 1)
                elif step == "route":
                    route_xT(0, 2 * m)
                    route_xT(0, 2 * m + 1)
                elif step == "choose":
                    for c in (2 * m, 2 * m + 1):
                        route_high(0, c)
                    route_exp(0, m)
                elif step == "rows":
                    for c in (2 * m, 2 * m + 1):
                        route_copy(0, c)

            def experts(l):
                f, i0 = ff, before[l]
                act.wait_ge(table, l + 1)
                act.wait_ge(w_late, 16 * NL)
                def step(i, q):
                    v, m = q % 2, (i + i0) * (XS_LEAD // 2) + q // 2
                    act.wait_ge(f["up"][v], m + 1)
                    wait(act, f["y"][v], m)
                    b = 2 + 2 * v
                    if l == 0:
                        e = act.value_load(eidx_i[0:1, l, ds(i * XS_LEAD + q, 1)], min_val=0, max_val=E - 1)
                        for c in range(FC):
                            ins = a.activation(hid[:, v, c, :], PF[:, b * 512 + c * TILE:b * 512 + (c + 1) * TILE],
                                               ACT.Relu, bias=b1[:, ds(e * FC + c, 1)], scale=1 / WSCALE)
                    else:
                        ins = a.activation(hid[:, v, :, :].rearrange("p c n -> p (c n)"), banks(b, 1024),
                                           ACT.Gelu, scale=1 / WSCALE)
                    ins.then_inc(f["hid"][v], 1)

                expert_tiles(act, l, step)

            experts(0)

            act.wait_ge(mask_T, 1)
            a.activation(mask_bias[:], PS[:, 4, 0:NT], ACT.Copy).then_inc(mask_sb, 1)
            for c in range(NC):
                act.wait_ge(x3t_ps, c + 1)
                a.activation(xnT1[:, c % 2, :], PS[:, c % 2, :], ACT.Copy).then_inc(x3t_sb, 1)
                for n, (which, bank) in enumerate(((1, BANK_K), (0, BANK_Q))):
                    act.wait_ge(qk_ps, 2 * c + n + 1)
                    if c >= 2:
                        act.wait_ge(qk_out[c % 2], QK_STORES * (c // 2))
                    a.activation(qk16[:, c % 2, which, 0, :], PS[:, bank[c % 2], :], ACT.Copy, scale=QK_SCALE[which])\
                        .then_inc(qk_hi, 1)

            act.wait_ge(mask_sb, 1)
            for g in range(G0, G1):
                T = g
                if 0 <= T < NT:
                    act.wait_ge(st_ps, T + 1)
                    if T >= 2:
                        act.wait_ge(p_lo, T - 1)
                    a.activation(pexp[:, T % 2, :], banks(2, 1024), ACT.Exp, bias=mask_bias[:, T:T + 1]).then_inc(p_done, 1)
                    act.wait_ge(p_done, T + 1)
                    if T >= 2:
                        act.wait_ge(av_ps, T - 1)
                    a.activation(p16[:, T % 2, 0, :], pexp[:, T % 2, :], ACT.Copy).then_inc(p_hi, 1)
                T = g - 3
                if 0 <= T < NT:
                    act.wait_ge(oT_ps, T + 1)
                    if T >= 2:
                        act.wait_ge(o_ps, T - 1)
                    for h2 in range(2):
                        ph = slice(h2 * 64, h2 * 64 + 64)
                        ins = a.activation(oT[ph, T % 2, :].rearrange("p (b q) -> p b q", b=2),
                                           PS[ph, 5, 0:2 * P].rearrange("p (b h q) -> p b h q", b=2, h=2)[:, :, h2, :],
                                           ACT.Copy)
                    ins.then_inc(oT_sb, 1)
                k = chunk_at(g, 3 - LEAD)
                if k is not None:
                    act.wait_ge(nT_ps, k + 1)
                    if k >= 1:
                        act.wait_ge(n_out, 32 * k)
                    a.activation(nmaxT, PS[:, 7, 0:P // 2].bitcast(F16), ACT.Copy).then_inc(nT_sb, 1)
                k = chunk_at(g, -2)
                if k is not None:
                    act.wait_ge(v9_ps, k + 1)
                    act.wait_ge(blank, 1)
                    if k >= 2:
                        act.wait_ge(av_ps, CT_TILES * (k - 1))
                    for hb in range(2):
                        ph = slice(hb * 64, hb * 64 + 64)
                        ins = a.activation(v9h[ph, k % 2, :, :, hb, 0:DH].rearrange("p s h d -> p (s h) d"),
                                           PS[ph, 7, :].rearrange("p (n d) -> p n d", d=DH), ACT.Copy)
                    ins.then_inc(v9_sb, 1)
                for half in range(2):
                    k = pair_at(g, 15 + half)
                    if k is not None:
                        route_xT(1, 2 * k + half)
                k = pair_at(g, 17)
                if k is not None:
                    route_exp(1, k)
                for half in range(2):
                    k = pair_at(g, 17 + half)
                    if k is not None:
                        route_high(1, 2 * k + half)
                    k = pair_at(g, 19 + half)
                    if k is not None:
                        route_copy(1, 2 * k + half)
            experts(1)
            for c in range(NC):
                act.wait_ge(x_ff[1], c + 1)
                act.dma_start(out_rows[:, tiles(c), :], X[:, tiles(c), :]).then_inc(stored, 16)

        @block.vector
        def _(dve):
            n = [0]
            v_ = nc.vector

            def link(ins):
                n[0] += 1
                ins.then_inc(dve_step, 1)
                dve.wait_ge(dve_step, n[0])

            def tt(o, x, y, op):
                return v_.tensor_tensor(o, x, y, op)

            def norm(t, slot, done):
                w = t.stop - t.start
                for T in range(t.start, t.stop):
                    ins = v_.bn_stats(stats[:, T, :], X[:, T, :])
                link(ins)
                for T in range(t.start, t.stop):
                    ins = v_.bn_aggr(mv[:, T, :], stats[:, T, :])
                link(ins)
                x, y, z = nwt[:, 0, 0:w], rstd[:, t], nwt[:, 1, 0:w]
                link(v_.tensor_scalar(x, mv[:, t, 1], EPS, None, ALU.add))
                link(v_.tensor_scalar(z.bitcast(I32), x.bitcast(I32), 1, None, ALU.arith_shift_right))
                link(v_.tensor_scalar(y.bitcast(I32), z.bitcast(I32), -1.0, float(0x5F3759DF), ALU.mult, ALU.add))
                for _ in range(3):
                    link(v_.scalar_tensor_tensor(out=z, in0=y, scalar=-0.5, in1=y, op0=ALU.mult, op1=ALU.mult))
                    link(tt(z, z, x, ALU.mult))
                    link(v_.scalar_tensor_tensor(out=y, in0=z, scalar=1.5, in1=y, op0=ALU.add, op1=ALU.mult))
                for s in range(w):
                    T = t.start + s
                    ins = v_.tensor_scalar(XN[:, slot + s, :], X[:, T, :], mv[:, T, 0:1], rstd[:, T:T + 1],
                                           ALU.subtract, ALU.mult)
                    if s % CT_TILES == CT_TILES - 1:
                        ins.then_inc(done, 1)

            def split_w1(l, raw, e):
                dve.wait_ge(w1_in[l][e % 2], 16 * (e // 2 + 1))
                o = slice(e * FF, (e + 1) * FF)
                link(v_.tensor_scalar(w1h[:, o], raw[:, e % 2, :], WSCALE, None, ALU.mult))
                v_.scalar_tensor_tensor(out=w1l[:, o], in0=raw[:, e % 2, :], scalar=WSCALE, in1=w1h[:, o],
                                        op0=ALU.mult, op1=ALU.subtract).then_inc(w1_lo[l], 1)


            def load(c):
                if c % 2:
                    return
                dve.wait_ge(x_in[c], 32)
                dve.wait_ge(x_in[c + 1], 32)
                norm(pair(c // 2), pair(c // 2).start, xn_done)
                if c == 0:
                    dve.wait_ge(w_in, 16 * NW)
                    dve.wait_ge(consts, 1)
                    v_.tensor_copy(wa32[:, :, :, 0:H], bc(wa[:], 2, 4)).then_inc(fold_in, 1)
                    tt(btq[:, 0:1], bcol[:, 0:1], bcol[:, 3:4], ALU.add).then_inc(fold_in, 1)
                    dve.wait_ge(fold_ps, 1)
                    dve.wait_ge(gates, 1)
                    v_.tensor_copy(wqqa[:, 0:H], PS[:, 4, 0:H])
                    v_.tensor_scalar(wtp, PS[:, 4, D:2 * D], gt[:, 0:1], None, ALU.mult)
                    v_.tensor_scalar(wqp, PS[:, 4, 2 * D:3 * D], gt[:, 0:1], None, ALU.mult)
                    v_.tensor_scalar(wka_bk, wa32[:, 1, 0, :], bcol[:, 1:2], None, ALU.mult)
                    link(tt(crow[0:1, :], PS[0:1, 5, 0:D], bprow[:], ALU.add))
                    v_.tensor_scalar(crow[0:1, :], crow[0:1, :], gt[0:1, 0:1], None, ALU.mult)
                    tt(qb[:, 0:1], PS[:, 5, D:D + 1], bacol[:, 0:1], ALU.add).then_inc(fold_sb, 1)

            def shift(r, a):
                half = slice(a * 512, (a + 1) * 512)
                g3 = sl[:, half].rearrange("p (g l) -> p g l", l=SEQ)
                mx = smx[:, a * CB:(a + 1) * CB]
                if r == 0:
                    dve.wait_ge(soft["logits"], 4 * (a + 1))
                    dve.wait_ge(fold_sb, 1)
                    link(v_.tensor_scalar(sl[:, half], PS[:, 6 + a, :], qb[:, 0:1], None, ALU.add))
                else:
                    dve.wait_ge(soft["logits"], NC + a + 1)
                    link(tt(g3, PS[:, 6 + a, :].rearrange("p (g l) -> p g l", l=SEQ),
                            bc(kb16[:, a * CB:(a + 1) * CB], 2, SEQ), ALU.add))
                link(v_.tensor_reduce(mx, g3, AX, ALU.max))
                tt(g3, g3, bc(mx, 2, SEQ), ALU.subtract).then_inc(soft["shifted"], 1)

            def weights(r, a):
                e3 = se[:, a * 512:(a + 1) * 512].rearrange("p (g l) -> p g l", l=SEQ)
                g_ = slice(a * CB, (a + 1) * CB)
                dve.wait_ge(soft["exp"], 2 * r + a + 1)
                link(v_.tensor_reduce(ssum[:, g_], e3, AX, ALU.add))
                link(v_.reciprocal(srec[:, g_], ssum[:, g_]))
                tt(e3, e3, bc(srec[:, g_], 2, SEQ), ALU.mult).then_inc(soft["weights"], 1)

            def weight_blocks(r, a):
                dve.wait_ge(soft["wT"], 2 * r + a + 1)
                dve.wait_ge(consts, 2)
                for hb in range(2):
                    ph = slice(hb * 64, hb * 64 + 64)
                    o = w2blk.rearrange("p (a j s) b h -> p a s j b h", a=2, j=4)[ph, a, :, :, hb, :]
                    i_ = PS[ph, a, :].rearrange("p (s j h) -> p s j h", s=4, j=4)[:, :, :, 0:H]
                    ins = v_.tensor_copy(o, i_)
                ins.then_inc(soft["blocks"], 1)

            def heads(r, a):
                dst, bias = ((pq, bcol[:, 0:1]), (pkv, bcol[:, 1:2]))[r]
                b_ = slice(a * NB // 2, (a + 1) * NB // 2)
                dve.wait_ge(soft["projected"], 2 * r + a + 1)
                p3 = prod.rearrange("p (b h) -> p b h", h=H)[:, b_, :]
                link(tt(p3, PS[:, 4 + a, :].rearrange("p (b h) -> p b h", h=H), bc(hmask[:], 1, NB // 2), ALU.mult))
                link(v_.tensor_reduce(dst[:, b_], p3, AX, ALU.add))
                v_.tensor_scalar(dst[:, b_], dst[:, b_], bias, None, ALU.add).then_inc(soft["head_prod"], 1)
                dve.wait_ge(soft["head_prod"], 2 * r + a + 1)
                if r == 0:
                    tt(gp[:, b_, :], bc(wa[:, 1, :], 1, NB // 2), bc(pq[:, b_], 2, H), ALU.mult).then_inc(gsem["moving"], 1)

            def key_bias(a):
                dve.wait_ge(gsem["ps"], a + 1)
                link(v_.tensor_scalar(kb16[:, a * CB:(a + 1) * CB], PS[:, a, 0:CB], bacol[:, 1:2], None, ALU.add))

            def scaled_values(c):
                dve.wait_ge(v_ps, c + 1)
                if c >= 2:
                    dve.wait_ge(att_ps, c - 1)
                v_.scalar_tensor_tensor(out=uT[:, c % 2, :].rearrange("p (b l) -> p b l", l=SEQ),
                                        in0=PS[:, V_BANK[c], :].rearrange("p (b l) -> p b l", l=SEQ),
                                        scalar=bcol[:, 2:3], in1=bc(pkv[:, c * CB:(c + 1) * CB], 2, SEQ),
                                        op0=ALU.add, op1=ALU.mult).then_inc(u_done, 1)

            def residual(c):
                dve.wait_ge(att_ps, c + 1)
                x = X[:, tiles(c), :].rearrange("p s d -> p (s d)")
                tt(x, x, PS[:, A_BANK[c], :], ALU.add).then_inc(x1_done, 1)
                dve.wait_ge(x1_done, c + 1)

            def route_norm(l, p):
                if l == 1 and p >= 2:
                    dve.wait_ge(rt[l]["xT"], 2 * (p - 1))
                norm(pair(p), slots(l, 2 * p).start, rt[l]["xn"])

            def route_lg(l, c):
                t = tiles(c)
                o = LG0 + c % 2 * CT_TILES * E
                lp = PS[:, BANK_LG[l], o:o + CT_TILES * E].rearrange("p (s e) -> p s e", e=E)
                dve.wait_ge(rt[l]["logits"], c // 2 * 2 + 2 if l == 0 else c + 1)
                if l == 0:
                    dve.wait_ge(w_late, 16 * NL)
                    tt(lg[:, t, :], lp, bc(brb[:], 1, CT_TILES), ALU.add).then_inc(rt[l]["lg"], 1)
                else:
                    v_.tensor_copy(lg[:, t, :], lp).then_inc(rt[l]["lg"], 1)

            def route_choose(l, p):
                t = pair(p)
                L = lg[:, t, :]
                a_, b_ = rtmp[:, 0, :, :], rtmp[:, 1, :, :]
                rv = bc(rev[:], 1, 2 * CT_TILES)
                dve.wait_ge(rt[l]["lg"], 2 * p + 2)
                link(v_.tensor_reduce(rmax[:, 0, t], L, AX, ALU.max))
                link(tt(a_, L, bc(rmax[:, 0, t], 2, E), ALU.is_equal))
                link(tt(a_, a_, rv, ALU.mult))
                link(v_.tensor_reduce(rmax[:, 1, t], a_, AX, ALU.max))
                link(tt(oh[:, 0, t, :], a_, bc(rmax[:, 1, t], 2, E), ALU.is_equal))
                link(v_.scalar_tensor_tensor(out=b_, in0=oh[:, 0, t, :], scalar=-BIG, in1=L, op0=ALU.mult, op1=ALU.add))
                link(v_.tensor_reduce(rmax[:, 2, t], b_, AX, ALU.max))
                tt(wdif[:, t], rmax[:, 2, t], rmax[:, 0, t], ALU.subtract).then_inc(gap, 1)
                link(tt(a_, b_, bc(rmax[:, 2, t], 2, E), ALU.is_equal))
                link(tt(a_, a_, rv, ALU.mult))
                link(v_.tensor_reduce(rmax[:, 3, t], a_, AX, ALU.max))
                link(tt(oh[:, 1, t, :], a_, bc(rmax[:, 3, t], 2, E), ALU.is_equal))
                tt(sel16[:, t, :], oh[:, 0, t, :], oh[:, 1, t, :], ALU.add).then_inc(rt[l]["mask"], 1)

            def route_rows(l, p):
                t = pair(p)
                a_, b2 = rtmp[:, 0, :, :], rtmp[:, 1:3, :, :]
                dve.wait_ge(rt[l]["rank"], p + 1)
                tt(a_, PS[:, BANK_RANK[l], RANK0:RANK0 + 2 * CT_TILES * E].rearrange("p (s e) -> p s e", e=E),
                   bc(expert_row[:], 1, 2 * CT_TILES), ALU.add).then_inc(rt[l]["rank_read"], 1)
                v_.tensor_reduce(csum[:], sel16[:, t, :].rearrange("p s e -> p e s"), AX, ALU.add)
                dve.wait_ge(rt[l]["rank_read"], p + 1)
                link(tt(b2, oh[:, :, t, :], bc(a_, 1, TOPK), ALU.mult))
                link(v_.tensor_reduce(adr[:, :, t], b2, AX, ALU.add))
                v_.tensor_copy(adr_i[:, :, t], adr[:, :, t]).then_inc(rt[l]["ranked"], 1)
                tt(cum16[:], cum16[:], csum[:], ALU.add).then_inc(rt[l]["count"], 1)

            def route_pack(l, c):
                t, u = tiles(c), c % 2
                dve.wait_ge(pack_hi, l * NC + c + 1)
                v_.tensor_copy(pack.bitcast(U32)[:, u, :, :, D], id_tok[:, t, :])
                tt(pack[:, u, :, 0, D:2 * D], XN[:, slots(l, c), :], pack[:, u, :, 0, 0:D], ALU.subtract)\
                    .then_inc(pack_lo, 1)

            def route_weights(l, p):
                t = pair(p)
                dve.wait_ge(gap_exp, l * NP + p + 1)
                link(v_.tensor_scalar(wden[:, t], wexp[:, t], 1.0, None, ALU.add))
                link(v_.reciprocal(wden[:, t], wden[:, t]))
                g_ = gt[:, 2 + l:3 + l]
                v_.tensor_scalar(wgt[:, t, 0], wden[:, t], g_, None, ALU.mult)
                v_.scalar_tensor_tensor(out=wgt[:, t, 1], in0=wden[:, t], scalar=g_, in1=wexp[:, t], op0=ALU.mult, op1=ALU.mult)

            def route_table(l):
                nl = SLOTS // P if l == 1 else 2 * TILES[0]
                dve.wait_ge(total, l + 1)
                link(v_.tensor_copy(cnt[:], PS[:, BANK_RANK[l], TOTAL0:TOTAL0 + E]))
                if l == 0:
                    link(v_.tensor_scalar(cnt_s[:], cnt[:], float(TILE - 1), None, ALU.add))
                    link(v_.tensor_copy(cnt_i[:], cnt_s[:]))
                    link(v_.tensor_scalar(cnt_i[:], cnt_i[:], 8, 8, ALU.arith_shift_right, ALU.logical_shift_left))
                    link(v_.tensor_copy(cnt_s[:], cnt_i[:]))
                    link(tt(tail_f[:], cnt[:], expert_row[:], ALU.add))
                    v_.tensor_copy(tail_i[:], tail_f[:])
                else:
                    link(v_.tensor_copy(cnt_s[:], cnt[:]))
                link(v_.tensor_tensor_scan(incl[:], onesE[:], cnt_s[:], 0.0, ALU.mult, ALU.add))
                link(v_.tensor_scalar(jump[:], cnt_s[:], -1.0, float(CAP), ALU.mult, ALU.add))
                pos, row, er, B = pos128[:, 0:nl], row_f[:, 0:nl], er_f[:, 0:nl], big1[:, 0:nl, :]

                def count(B, at_, o_er, o_row, m):
                    link(tt(B, bc(incl[:], 1, m), bc(at_, 2, E), ALU.is_le))
                    if o_er is not None:
                        link(v_.tensor_reduce(o_er, B, AX, ALU.add))
                    if o_row is not None:
                        link(tt(B, B, bc(jump[:], 1, m), ALU.mult))
                        link(v_.tensor_reduce(o_row, B, AX, ALU.add))
                        link(tt(o_row, o_row, at_, ALU.add))

                count(B, pos, er, row, nl)
                if l == 0:
                    link(v_.tensor_scalar(fx_f[:, 0, 0:nl], er, float(E - 1), None, ALU.min))
                    v_.tensor_copy(eidx_i[:, 0, :], fx_f[:, 0, 0:nl].rearrange("p (j u) -> p j u", u=2)[:, :, 0])
                else:
                    last, er2, alt = fx_f[:, 0, 0:nl], fx_f[:, 1, 0:nl], fx_f[:, 2, 0:nl]
                    link(v_.tensor_scalar(last, pos, float(P - 1), None, ALU.add))
                    count(B, last, er2, None, nl)
                    link(tt(er2, er2, er, ALU.is_gt))
                    link(v_.tensor_scalar(alt, er, float(P), float(FIX0), ALU.mult, ALU.add))
                    link(tt(alt, alt, row, ALU.subtract))
                    link(tt(alt, alt, er2, ALU.mult))
                    link(tt(row, row, alt, ALU.add))
                    link(v_.tensor_copy(fixp_i[:], incl[:]))
                    link(v_.tensor_scalar(fixp_i[:], fixp_i[:], 7, 7, ALU.arith_shift_right, ALU.logical_shift_left))
                    link(v_.tensor_copy(fixp[:, 0, :], fixp_i[:]))
                    link(v_.tensor_scalar(fixp[:, 1, :], fixp[:, 0, :], float(SLOTS - P), lane[:, 0:1], ALU.min, ALU.add))
                    count(B[:, 0:E, :], fixp[:, 1, :], None, fixp[:, 2, :], E)
                    v_.tensor_copy(fixadr_i[:], fixp[:, 2, :])
                v_.tensor_copy(rows_i[:, 0:nl], row).then_inc(table, 1)

            for step, m, a in ORDER:
                if step == "load":
                    load(m)
                elif step == "logits":
                    shift(m, a)
                elif step == "weights":
                    weights(m, a)
                elif step == "pool":
                    weight_blocks(m, a)
                elif step == "heads":
                    heads(m, a)
                elif step == "keys":
                    key_bias(m)
                elif step == "split":
                    split_w1(0, w1raw, m)
                elif step == "route":
                    route_norm(0, m)
                elif step == "choose":
                    route_lg(0, 2 * m)
                    route_lg(0, 2 * m + 1)
                    route_choose(0, m)
                elif step == "rows":
                    for c in (2 * m, 2 * m + 1):
                        route_pack(0, c)
                    route_rows(0, m)
                    route_weights(0, m)
                for c in (2 * m, 2 * m + 1):
                    if step == "scale":
                        scaled_values(c)
                    elif step == "add":
                        residual(c)
            route_table(0)

            def parts_of_projection(c):
                for n, (which, bank) in enumerate(((1, BANK_K), (0, BANK_Q))):
                    dve.wait_ge(qk_hi, 2 * c + n + 1)
                    v_.scalar_tensor_tensor(out=qk16[:, c % 2, which, 1, :], in0=PS[:, bank[c % 2], :],
                                            scalar=QK_SCALE[which], in1=qk16[:, c % 2, which, 0, :],
                                            op0=ALU.mult, op1=ALU.subtract).then_inc(qk_lo, 1)

            def experts(l):
                f, i0 = ff, before[l]

                def parts(i, q):
                    v, m = q % 2, (i + i0) * (XS_LEAD // 2) + q // 2
                    dve.wait_ge(f["xT"][v], m + 1)
                    wait(dve, f["up"][v], m)
                    v_.tensor_copy(xgT[:, v, :, :].rearrange("p h n -> p (h n)"), PS[:, v, 0:TILE].bitcast(F16))\
                        .then_inc(f["xT_sb"][v], 1)

                def result(i, q):
                    v, m = q % 2, (i + i0) * (XS_LEAD // 2) + q // 2
                    dve.wait_ge(f["y"][v], m + 1)
                    if not (isinstance(i, int) and i + i0 == 0):
                        dve.wait_ge(f["turn"][0], (i + i0 - 1) * XS_LEAD + q + 1)
                        dve.wait_ge(f["stored"][q], (i + i0) * STORED)
                    y = PS[:, 6 + v, 0:2 * D].rearrange("p (u d) -> p u d", u=2)
                    if l == 0:
                        e = dve.value_load(eidx_i[0:1, l, ds(i * XS_LEAD + q, 1)], min_val=0, max_val=E - 1)
                        ins = tt(yrow[:, q, :, :], y, bc(b2b[:, ds(e * D, D)], 1, 2), ALU.add)
                    else:
                        ins = v_.tensor_copy(yrow[:, q, :, :], y)
                    ins.then_inc(f["yrow"][v], 1)

                def round_(i, first, last):
                    for q in range(XS_LEAD):
                        if q < XS_LEAD - 1:
                            parts(i, q + 1)
                        elif not last:
                            parts(i + 1, 0)
                        if q >= 1:
                            result(i, q - 1)
                        elif not first:
                            result(i - 1, XS_LEAD - 1)

                rounds_ = TILES[l] // XS_LEAD
                parts(0, 0)
                round_(0, True, False)
                with dve.Fori(1, rounds_ - 1) as i:
                    round_(i, False, False)
                round_(rounds_ - 1, False, True)
                result(rounds_ - 1, XS_LEAD - 1)

            def combine(l, c):
                slot, s_, value = y_slot(l, c)
                dve.wait_ge(s_, value)
                for k in range(TOPK):
                    for s in range(CT_TILES):
                        T = c * CT_TILES + s
                        ins = v_.scalar_tensor_tensor(out=X[:, T, :], in0=yc[:, slot, s, k, :],
                                                      scalar=wgt[:, T, k:k + 1], in1=X[:, T, :],
                                                      op0=ALU.mult, op1=ALU.add)
                    if k == 0:
                        link(ins)
                ins.then_inc(x_ff[l], 1)

            experts(0)

            dve.wait_ge(w_late, 16 * NL)
            link(v_.tensor_copy(mask_f[:], mask_u8[:]))
            v_.tensor_scalar(mask16[:], mask_f[:], -1.0, -MASKED, ALU.add, ALU.mult)
            link(v_.tensor_scalar(mask_f[:], mask_f[:], -1.0, None, ALU.add))
            v_.tensor_scalar(mask_f[:], mask_f[:], BIG, None, ALU.mult).then_inc(mask_rows, 1)
            v_.tensor_scalar(wo1T, wo1T, gt[:, 1:2], None, ALU.mult)
            link(v_.memset(cum16[:], 0.0))
            v_.memset(v9l, 0.0)
            link(v_.memset(v9h, 0.0))
            for hb in range(2):
                ins = v_.memset(v9h[hb * 64:hb * 64 + 64, :, :, :, hb, DH:DH + 1].rearrange("p u s h n -> p (u s h) n"), 1.0)
            ins.then_inc(blank, 1)
            for p in range(NP):
                for c in (2 * p, 2 * p + 1):
                    combine(0, c)
                dve.wait_ge(x_ff[0], 2 * p + 2)
                norm(pair(p), pair(p).start, xn3)
                if p >= 1:
                    parts_of_projection(2 * p - 2)
                    parts_of_projection(2 * p - 1)
            parts_of_projection(NC - 2)
            parts_of_projection(NC - 1)
            for g in range(G0, G1):
                T = g - 5
                if 0 <= T < NT:
                    dve.wait_ge(o_ps, T + 1)
                    tt(X[:, T, :], X[:, T, :], PS[:, 6, 0:D], ALU.add).then_inc(x3_done, 1)
                T = g - 3
                if 0 <= T < NT:
                    o = PS[:, 4, 0:HP * 36].rearrange("p (m h b n) -> p m h b n", m=HP, h=2, b=2)
                    rec = orec.rearrange("p (m h b) -> p b m h", b=2, m=HP)
                    dve.wait_ge(av_ps, T + 1)
                    link(v_.reciprocal(orec, PS[:, 4, 0:HP * 36].rearrange("p (k n) -> p k n", n=DH + 1)[:, :, DH]))
                    if T >= 1:
                        dve.wait_ge(oT_ps, T)
                    for b in range(2):
                        ins = tt(onorm[:, b, :].rearrange("p (h m d) -> p m h d", h=2, m=HP), o[:, :, :, b, 0:DH],
                                 bc(rec[:, b, :, :], 3, DH), ALU.mult)
                    ins.then_inc(o_norm, 1)
                T = g + LEAD
                if 0 <= T < NT:
                    c, s = T // CT_TILES, T % CT_TILES
                    dve.wait_ge(s_ps, T + 1)
                    v_.tensor_reduce(rmaxq[:, c % 2, s, :], banks(0, 1024).rearrange("p (h k) -> p h k", h=H),
                                     AX, ALU.max).then_inc(s_max, 1)
                    if s == CT_TILES - 1:
                        dve.wait_ge(s_max, T + 1)
                        if c >= 1:
                            dve.wait_ge(nT_ps, c)
                        link(v_.tensor_scalar(nmax.rearrange("p (j r s) -> p s r j", j=HG, r=HG),
                                              rmaxq[:, c % 2, :, :].rearrange("p s (r j) -> p s r j", r=HG),
                                              -1.0, None, ALU.mult))
                        link(v_.tensor_copy(nmax16[:, 0, :], nmax))
                        tt(nmax16[:, 1, :], nmax, nmax16[:, 0, :], ALU.subtract).then_inc(n_ready, 1)
                k = chunk_at(g, -2)
                if k is not None:
                    dve.wait_ge(v9_sb, k + 1)
                    for hb in range(2):
                        ph = slice(hb * 64, hb * 64 + 64)
                        v9 = [v[ph, k % 2, :, :, hb, 0:DH].rearrange("p s h d -> p (s h) d") for v in (v9h, v9l)]
                        ins = tt(v9[1], PS[ph, 7, :].rearrange("p (n d) -> p n d", d=DH), v9[0], ALU.subtract)
                    ins.then_inc(v9_lo, 1)
                k = pair_at(g, 12)
                if k is not None:
                    dve.wait_ge(x3_done, 2 * CT_TILES * (k + 1))
                    route_norm(1, k)
                for half in range(2):
                    k = pair_at(g, 16 + half)
                    if k is not None:
                        route_lg(1, 2 * k + half)
                k = pair_at(g, 17)
                if k is not None:
                    route_choose(1, k)
                k = pair_at(g, 18)
                if k is not None:
                    route_rows(1, k)
                    route_pack(1, 2 * k)
                k = pair_at(g, 19)
                if k is not None:
                    route_pack(1, 2 * k + 1)
                    route_weights(1, k)
                k = chunk_at(g, 3)
                if k == 0:
                    for u in range(2):
                        dve.wait_ge(qk_out[u], QK_STORES * NC // 2)
                if k is not None:
                    split_w1(1, w1raw1, k)
            route_table(1)
            experts(1)
            for c in range(NC):
                combine(1, c)


_OUT = ((NB, SEQ, D), "float32")


def kernel(**inputs):
    import numpy as np
    import concourse.bacc as bacc
    from concourse.bass_utils import run_bass_kernel_spmd

    v = {k: np.ascontiguousarray(a) for k, a in inputs.items()}
    col = lambda a: a.reshape(D, 1)

    def by_group(a):
        z = np.zeros((4, 32), a.dtype)
        z[:, :H] = a
        return z.reshape(P, 1)

    def by_lane(w):
        return w.reshape(D, HG, HG, DH).transpose(0, 1, 3, 2).reshape(D, D)

    wo = v["L1_xattn_Wo"].T.reshape(HP, 2, DH, D).transpose(1, 0, 2, 3).reshape(D, D)
    arrays = {
        "x": v["x"].reshape(NTOK, D), "ctx": v["ctx_1024"].reshape(NTOK, D),
        "mask": v["mask_Bx1x1xS2_bf1"].reshape(NT, P).view(np.uint8),
        "g": np.concatenate([v["g_xattn"], v["g_ffn"]]).reshape(1, 4),
        "W": np.stack([v["L0_xattn_Wq"], v["L0_xattn_Wq"].T, v["L0_xattn_Wk"], v["L0_xattn_Wk"].T, v["L0_xattn_Wv"],
                       v["L0_xattn_Wt"].T, v["L0_xattn_Wp"], by_lane(v["L1_xattn_Wq"].T), by_lane(v["L1_xattn_Wk"].T),
                       v["L1_xattn_Wv"].T, wo]),
        "wa": np.stack([v["L0_xattn_Wqa"], v["L0_xattn_Wka"]]),
        "wr": np.stack([v["L0_ffn_W_router"], v["L1_ffn_router_w"].T]),
        "bcol": np.concatenate([col(v["L0_xattn_" + b]) for b in ("bq", "bk", "bv", "bt")], axis=1),
        "bacol": np.concatenate([by_group(v["L0_xattn_bqa"]), by_group(v["L0_xattn_bka"])], axis=1),
        "bp": v["L0_xattn_bp"].reshape(1, D), "br": v["L0_ffn_b_router"].reshape(1, E),
        "b1": v["L0_ffn_b1"].reshape(E, FC, P).transpose(2, 0, 1).reshape(P, E * FC),
        "b2": v["L0_ffn_b2"].reshape(1, E * D),
        "w1_0": v["L0_ffn_W1"], "w2_0": v["L0_ffn_W2"], "w1_1": v["L1_ffn_w1"], "w2_1": v["L1_ffn_w2"],
    }
    nc = bacc.Bacc("TRN2", target_bir_lowering=False, num_devices=1)
    A, feed = {}, {}
    for name, a in arrays.items():
        a = np.ascontiguousarray(a)
        feed[f"in_{name}"] = a
        A[name] = nc.dram_tensor(f"in_{name}", a.shape, mybir.dt.from_np(a.dtype), kind="ExternalInput").ap()
    out = nc.dram_tensor("out", (NTOK, D), F32, kind="ExternalOutput").ap()
    build(nc, A, out)
    r = run_bass_kernel_spmd(nc, [feed], core_ids=[0])
    return r.results[0]["out"].reshape(_OUT[0])
```
